# Optimizing a Trainium2 kernel written in Bass

```python
import numpy as np
import jax
import jax.numpy as jnp

def _softmax(x, axis=-1):
    return jax.nn.softmax(x, axis=axis)

def _gelu(x):
    return jax.nn.gelu(x, approximate=True)

def _silu(x):
    return jax.nn.silu(x)

def _sigmoid(x):
    return jax.nn.sigmoid(x)

def _layernorm(x, axis=-1, eps=1e-05):
    m = jnp.mean(x, axis=axis, keepdims=True)
    v = jnp.var(x, axis=axis, keepdims=True)
    return (x - m) / jnp.sqrt(v + eps)

def _scatter_add(tgt, idx, src, axis=0):
    return tgt.at[idx].add(src)

def _segment_sum(src, seg, n):
    return jax.ops.segment_sum(src, seg, n)
kernel_name = 'mk_flamingo_gated_d4_seqx_r8_9f570c'

def setup_inputs(seed: int=0):
    np.random.seed(seed)
    _w = jnp.asarray

    def _rec_inputs():
        import jax
        import jax.numpy as jnp
        _rk = jax.random.key(seed)
        x = 7.22e-05 + 1 * jax.random.normal(jax.random.fold_in(_rk, 1), (4, 512, 128), jnp.float32)
        _lenS = 512 - jax.random.randint(jax.random.fold_in(_rk, 7), (4,), 0, max(1, 512 // 4) + 1, jnp.int32)
        _lenS2 = 154 - jax.random.randint(jax.random.fold_in(_rk, 8), (4,), 0, max(1, 154 // 4) + 1, jnp.int32)
        _ctx_1024P = jax.random.normal(jax.random.fold_in(_rk, 11), (4, 16, 128), jnp.float32)
        _ctx_1024c = jax.random.dirichlet(jax.random.fold_in(_rk, 511), 0.3 * jnp.ones((16,), jnp.float32), (4, 154))
        _ctx_1024t = jnp.einsum('bsk,bkd->bsd', _ctx_1024c, _ctx_1024P)
        _ctx_1024t = _ctx_1024t * jax.lax.rsqrt(jnp.mean(jnp.square(_ctx_1024t)) + 1e-12) * 0.953939
        ctx_1024 = -0.000107592 + 0.9999 * (_ctx_1024t + 0.3 * jax.random.normal(jax.random.fold_in(_rk, 611), (4, 154, 128), jnp.float32))
        _validS = jnp.arange(512)[None, :] < _lenS[:, None]
        _validS2 = jnp.arange(154)[None, :] < _lenS2[:, None]
        _causal = jnp.tril(jnp.ones((512, 512), dtype=bool))
        mask_BxS2_bf1 = jnp.ones((4, 154), dtype=bool)
        _g = jax.random.normal(jax.random.fold_in(_rk, 9001), (2, 4), jnp.float32)
        _g = jnp.sign(_g) * jnp.maximum(jnp.abs(_g), 1.0) + (_g == 0) * 1.0
        g_xattn = _g[0]
        g_ffn = _g[1]
        return (x, ctx_1024, mask_BxS2_bf1, g_xattn, g_ffn)
    x, ctx_1024, mask_BxS2_bf1, g_xattn, g_ffn = _rec_inputs()

    def _L0_xattn_setup():
        import jax, jax.numpy as jnp
        import numpy as np
        DIM = 128
        N_HEADS = 16
        HEAD_DIM = DIM // N_HEADS
        EPS = 1e-06
        Q_THETA = 32.0
        K_THETA = 1000.0

        def precompute_freqs_1d(dim, seq_len, theta):
            freqs = theta ** (-jnp.arange(0, dim, 2, dtype=jnp.float32) / dim)
            t = jnp.arange(seq_len, dtype=jnp.float32)
            ang = t[:, None] * freqs[None, :]
            return (jnp.cos(ang), jnp.sin(ang))

        def rms_norm(x, w):
            var = jnp.mean(x * x, axis=-1, keepdims=True)
            return x * jax.lax.rsqrt(var + EPS) * w

        def apply_rope(t, cos, sin):
            cos = cos[None, None, :, :]
            sin = sin[None, None, :, :]
            t1, t2 = jnp.split(t, 2, axis=-1)
            return jnp.concatenate([t1 * cos - t2 * sin, t2 * cos + t1 * sin], axis=-1)
        key = jax.random.key(seed)
        ks = jax.random.split(key, 8)
        B, T, S = (128, 64, 48)
        s = 1.0 / np.sqrt(DIM)
        return {'x': jax.random.normal(ks[0], (B, T, DIM), jnp.float32), 'context': jax.random.normal(ks[1], (B, S, DIM), jnp.float32), 'Wq': jax.random.normal(ks[2], (DIM, DIM), jnp.float32) * s, 'Wk': jax.random.normal(ks[3], (DIM, DIM), jnp.float32) * s, 'Wv': jax.random.normal(ks[4], (DIM, DIM), jnp.float32) * s, 'Wo': jax.random.normal(ks[5], (DIM, DIM), jnp.float32) * s, 'q_norm_w': jnp.ones((HEAD_DIM,), jnp.float32), 'k_norm_w': jnp.ones((HEAD_DIM,), jnp.float32)}
    _L0_xattn_all = _L0_xattn_setup()
    _L0_xattn_in = {k: v for k, v in _L0_xattn_all.items() if k in ('Wq', 'Wk', 'Wv', 'Wo', 'q_norm_w', 'k_norm_w')}
    del _L0_xattn_all

    def _L0_ffn_setup():
        import jax, jax.numpy as jnp
        import numpy as np
        D_MODEL = 128
        FF = 512
        E = 8
        TOP_K = 2
        CAP_FACTOR = 1.25
        B, T = (4, 256)

        def _moe_forward(x, gate_w, gate_b, w1, b1, w2, b2):
            Bb, Tt, d = x.shape
            S = Bb * Tt
            C = int(CAP_FACTOR * S / E)
            xf = x.reshape(S, d)
            logits = xf @ gate_w + gate_b
            probs = jax.nn.softmax(logits, axis=1)
            topk_p, topk_i = jax.lax.top_k(probs, TOP_K)
            topk_pn = topk_p / jnp.sum(topk_p, axis=1, keepdims=True)
            rows = jnp.arange(S)
            w_te = jnp.zeros((S, E), xf.dtype).at[rows[:, None], topk_i].set(topk_pn)
            mask = jnp.zeros((S, E), bool).at[rows[:, None], topk_i].set(True)
            rank = jnp.cumsum(mask.astype(jnp.int32), axis=0)
            slot = jnp.where(mask & (rank <= C), rank - 1, C)
            e_grid = jnp.broadcast_to(jnp.arange(E), (S, E))
            t_grid = jnp.broadcast_to(rows[:, None], (S, E))
            buf = jnp.full((E, C + 1), S, jnp.int32).at[e_grid, slot].set(t_grid)
            idx = buf[:, :C]
            valid = idx < S
            x_pad = jnp.concatenate([xf, jnp.zeros((1, d), xf.dtype)], axis=0)
            xin = x_pad[idx]
            h = jax.nn.relu(jnp.einsum('ecd,edh->ech', xin, w1) + b1[:, None, :])
            out = jnp.einsum('ech,ehd->ecd', h, w2) + b2[:, None, :]
            w_pad = jnp.concatenate([w_te, jnp.zeros((1, E), xf.dtype)], axis=0)
            tok_w = w_pad[idx, jnp.arange(E)[:, None]]
            out = out * jnp.where(valid, tok_w, 0.0)[:, :, None]
            final = jnp.zeros((S + 1, d), xf.dtype).at[idx.reshape(-1)].add(out.reshape(-1, d))[:S]
            return final.reshape(Bb, Tt, d)
        key = jax.random.key(seed)
        ks = jax.random.split(key, 7)
        s = 0.02
        return {'x': jax.random.normal(ks[0], (B, T, D_MODEL), jnp.float32), 'gate_w': jax.random.normal(ks[1], (D_MODEL, E), jnp.float32) * s, 'gate_b': jnp.zeros((E,), jnp.float32), 'w1': jax.random.normal(ks[2], (E, D_MODEL, FF), jnp.float32) * s, 'b1': jnp.zeros((E, FF), jnp.float32), 'w2': jax.random.normal(ks[3], (E, FF, D_MODEL), jnp.float32) * s, 'b2': jnp.zeros((E, D_MODEL), jnp.float32)}
    _L0_ffn_all = _L0_ffn_setup()
    _L0_ffn_in = {k: v for k, v in _L0_ffn_all.items() if k in ('gate_w', 'gate_b', 'w1', 'b1', 'w2', 'b2')}
    del _L0_ffn_all

    def _L1_xattn_setup():
        import jax, jax.numpy as jnp
        import numpy as np
        N_HEAD, MODEL_DIM, KEY_DIM, VALUE_DIM = (16, 128, 64, 64)
        B, S = (4, 256)
        EPS = 1e-05
        TEMP = float(np.sqrt(KEY_DIM))
        key = jax.random.key(seed)
        ks = jax.random.split(key, 12)
        d = {'query': jax.random.normal(ks[0], (B, S, MODEL_DIM), jnp.float32), 'key': jax.random.normal(ks[1], (B, S, MODEL_DIM), jnp.float32), 'value': jax.random.normal(ks[2], (B, S, MODEL_DIM), jnp.float32), 'Wq': jax.random.normal(ks[3], (MODEL_DIM, N_HEAD * KEY_DIM), jnp.float32) * np.sqrt(2.0 / (MODEL_DIM + KEY_DIM)), 'bq': jnp.zeros((N_HEAD * KEY_DIM,), jnp.float32), 'Wk': jax.random.normal(ks[4], (MODEL_DIM, N_HEAD * KEY_DIM), jnp.float32) * np.sqrt(2.0 / (MODEL_DIM + KEY_DIM)), 'bk': jnp.zeros((N_HEAD * KEY_DIM,), jnp.float32), 'Wv': jax.random.normal(ks[5], (MODEL_DIM, N_HEAD * VALUE_DIM), jnp.float32) * np.sqrt(2.0 / (MODEL_DIM + VALUE_DIM)), 'bv': jnp.zeros((N_HEAD * VALUE_DIM,), jnp.float32), 'Wo': jax.random.normal(ks[6], (N_HEAD * VALUE_DIM, MODEL_DIM), jnp.float32) * np.sqrt(2.0 / (N_HEAD * VALUE_DIM + MODEL_DIM)), 'bo': jnp.zeros((MODEL_DIM,), jnp.float32), 'ln_gamma': jnp.ones((MODEL_DIM,), jnp.float32), 'ln_beta': jnp.zeros((MODEL_DIM,), jnp.float32)}
        return d
    _L1_xattn_all = _L1_xattn_setup()
    _L1_xattn_in = {k: v for k, v in _L1_xattn_all.items() if k in ('Wq', 'bq', 'Wk', 'bk', 'Wv', 'bv', 'Wo', 'bo', 'ln_gamma', 'ln_beta')}
    del _L1_xattn_all

    def _L1_ffn_setup():
        import jax, jax.numpy as jnp
        import numpy as np
        FF_DIM = 256
        TOP_K = 2
        key = jax.random.key(seed)
        k1, k2, k3, k4 = jax.random.split(key, 4)
        B, S, D, E, F = (2, 256, 128, 8, FF_DIM)
        std = 0.006
        return {'x': jax.random.normal(k1, (B, S, D), dtype=jnp.float32), 'gate_w': jax.random.normal(k2, (D, E), dtype=jnp.float32) * 0.02, 'gate_up_w': jax.random.normal(k3, (E, D, 2 * F), dtype=jnp.float32) * std, 'down_w': jax.random.normal(k4, (E, F, D), dtype=jnp.float32) * std}
    _L1_ffn_all = _L1_ffn_setup()
    _L1_ffn_in = {k: v for k, v in _L1_ffn_all.items() if k in ('gate_w', 'gate_up_w', 'down_w')}
    del _L1_ffn_all

    def _L2_xattn_setup():
        import jax, jax.numpy as jnp
        import numpy as np
        N_HEADS = 16
        D_MODEL = 128
        HEAD_DIM = D_MODEL // N_HEADS
        MASK_FILL = -100000000.0

        def _split_heads(x):
            B, S, _ = x.shape
            return x.reshape(B, S, N_HEADS, HEAD_DIM).transpose(0, 2, 1, 3)
        key = jax.random.key(seed)
        ks = jax.random.split(key, 12)
        B, L, P = (2, 256, 256)
        s = 1.0 / np.sqrt(D_MODEL).astype(np.float32)
        inp = {'q': jax.random.normal(ks[0], (B, L, D_MODEL), dtype=jnp.float32), 'k': jax.random.normal(ks[1], (B, P, D_MODEL), dtype=jnp.float32), 'v': jax.random.normal(ks[2], (B, P, D_MODEL), dtype=jnp.float32), 'attention_mask': jnp.ones((B, P), dtype=bool), 'Wq': jax.random.normal(ks[3], (D_MODEL, D_MODEL), dtype=jnp.float32) * s, 'bq': jnp.zeros((D_MODEL,), dtype=jnp.float32), 'Wk': jax.random.normal(ks[4], (D_MODEL, D_MODEL), dtype=jnp.float32) * s, 'bk': jnp.zeros((D_MODEL,), dtype=jnp.float32), 'Wv': jax.random.normal(ks[5], (D_MODEL, D_MODEL), dtype=jnp.float32) * s, 'bv': jnp.zeros((D_MODEL,), dtype=jnp.float32), 'Wo': jax.random.normal(ks[6], (D_MODEL, D_MODEL), dtype=jnp.float32) * s, 'bo': jnp.zeros((D_MODEL,), dtype=jnp.float32)}
        return inp
    _L2_xattn_all = _L2_xattn_setup()
    _L2_xattn_in = {k: v for k, v in _L2_xattn_all.items() if k in ('Wq', 'bq', 'Wk', 'bk', 'Wv', 'bv', 'Wo', 'bo')}
    del _L2_xattn_all

    def _L2_ffn_setup():
        import jax, jax.numpy as jnp
        import numpy as np
        B, T, C = (2, 256, 128)
        H, D = (16, 64)
        CR = 8
        R = C // CR
        ROPE = D // 2
        NOPE = D - ROPE
        E, K, I, S = (8, 2, 64, 1)
        THETA = 100000.0
        EPS = 1e-05

        def _rmsnorm(x, w):
            rms = jnp.sqrt(jnp.mean(x * x, axis=-1, keepdims=True) + EPS)
            return w * (x / rms)

        def _rope(xh):
            d = xh.shape[-1]
            t = jnp.arange(xh.shape[2], dtype=jnp.float32)
            freqs = 1.0 / THETA ** (jnp.arange(0, d, 2, dtype=jnp.float32) / d)
            ang = jnp.outer(t, freqs)
            cos, sin = (jnp.cos(ang), jnp.sin(ang))
            xr = xh.reshape(xh.shape[:-1] + (d // 2, 2))
            x0, x1 = (xr[..., 0], xr[..., 1])
            rot = jnp.stack([x0 * cos - x1 * sin, x0 * sin + x1 * cos], axis=-1)
            return rot.reshape(xh.shape)

        def _attention(x, Wq, Wkva, Wkvb, Wo):
            b, t, _ = x.shape
            q = (x @ Wq).reshape(b, t, H, D).transpose(0, 2, 1, 3)
            ckv = x @ Wkva
            kv_latent, k_rope = (ckv[:, :, :R], ckv[:, :, R:])
            kv = (kv_latent @ Wkvb).reshape(b, t, H, NOPE).transpose(0, 2, 1, 3)
            k_rope = jnp.broadcast_to(k_rope[:, None, :, :], (b, H, t, ROPE))
            q_nope, q_rope = (q[..., :NOPE], q[..., NOPE:])
            q = jnp.concatenate([q_nope, _rope(q_rope)], axis=-1)
            k = jnp.concatenate([kv, _rope(k_rope)], axis=-1)
            v = jnp.concatenate([kv, jnp.zeros_like(k_rope)], axis=-1)
            att = jnp.einsum('bhqd,bhkd->bhqk', q, k) / jnp.sqrt(jnp.float32(D))
            mask = jnp.tril(jnp.ones((t, t), dtype=bool))
            att = jnp.where(mask, att, jnp.float32(-jnp.inf))
            att = jax.nn.softmax(att, axis=-1)
            y = jnp.einsum('bhqk,bhkd->bhqd', att, v)
            y = y.transpose(0, 2, 1, 3).reshape(b, t, H * D)
            return y @ Wo

        def _experts(x_flat, Wg, Wu, Wd):
            g = jax.nn.silu(jnp.einsum('nc,eci->nei', x_flat, Wg))
            u = jnp.einsum('nc,eci->nei', x_flat, Wu)
            return jnp.einsum('nei,eic->nec', g * u, Wd)

        def _moe(x, Wgate, expert_bias, Wg, Wu, Wd, sWg, sWu, sWd):
            b, t, c = x.shape
            xf = x.reshape(-1, c)
            shared = jnp.mean(_experts(xf, sWg, sWu, sWd), axis=1)
            logits = xf @ Wgate + expert_bias
            probs = jax.nn.softmax(logits, axis=-1)
            topk_p, topk_i = jax.lax.top_k(probs, K)
            topk_p = topk_p / jnp.sum(topk_p, axis=-1, keepdims=True)
            comb = jnp.sum(jax.nn.one_hot(topk_i, E, dtype=xf.dtype) * topk_p[..., None], axis=1)
            routed = jnp.einsum('ne,nec->nc', comb, _experts(xf, Wg, Wu, Wd))
            return (shared + routed).reshape(b, t, c)
        key = jax.random.key(seed)
        ks = jax.random.split(key, 16)
        w = lambda k, shp: jax.random.normal(k, shp, dtype=jnp.float32) * 0.02
        return {'x': jax.random.normal(ks[0], (B, T, C), dtype=jnp.float32), 'w_ln1': jnp.ones((C,), jnp.float32), 'Wq': w(ks[1], (C, H * D)), 'Wkva': w(ks[2], (C, R + ROPE)), 'Wkvb': w(ks[3], (R, H * NOPE)), 'Wo': w(ks[4], (H * D, C)), 'w_ln2': jnp.ones((C,), jnp.float32), 'Wgate': w(ks[5], (C, E)), 'expert_bias': jnp.zeros((E,), jnp.float32), 'Wg': w(ks[6], (E, C, I)), 'Wu': w(ks[7], (E, C, I)), 'Wd': w(ks[8], (E, I, C)), 'sWg': w(ks[9], (S, C, I)), 'sWu': w(ks[10], (S, C, I)), 'sWd': w(ks[11], (S, I, C))}
    _L2_ffn_all = _L2_ffn_setup()
    _L2_ffn_in = {k: v for k, v in _L2_ffn_all.items() if k in ('w_ln1', 'Wq', 'Wkva', 'Wkvb', 'Wo', 'w_ln2', 'Wgate', 'expert_bias', 'Wg', 'Wu', 'Wd', 'sWg', 'sWu', 'sWd')}
    del _L2_ffn_all

    def _L3_xattn_setup():
        import jax, jax.numpy as jnp
        import numpy as np
        HEADS = 16
        D_MODEL = 128
        HEAD_DIM = D_MODEL // HEADS
        key = jax.random.key(seed)
        ks = jax.random.split(key, 11)
        B, S = (4, 256)
        scale_in = 1.0 / np.sqrt(HEAD_DIM)
        scale_out = 1.0 / np.sqrt(D_MODEL)
        return {'values': jax.random.normal(ks[0], (B, S, D_MODEL), dtype=jnp.float32), 'keys': jax.random.normal(ks[1], (B, S, D_MODEL), dtype=jnp.float32), 'query': jax.random.normal(ks[2], (B, S, D_MODEL), dtype=jnp.float32), 'wq': jax.random.normal(ks[3], (HEAD_DIM, HEAD_DIM), dtype=jnp.float32) * scale_in, 'bq': jax.random.normal(ks[4], (HEAD_DIM,), dtype=jnp.float32) * 0.01, 'wk': jax.random.normal(ks[5], (HEAD_DIM, HEAD_DIM), dtype=jnp.float32) * scale_in, 'bk': jax.random.normal(ks[6], (HEAD_DIM,), dtype=jnp.float32) * 0.01, 'wv': jax.random.normal(ks[7], (HEAD_DIM, HEAD_DIM), dtype=jnp.float32) * scale_in, 'bv': jax.random.normal(ks[8], (HEAD_DIM,), dtype=jnp.float32) * 0.01, 'wo': jax.random.normal(ks[9], (D_MODEL, D_MODEL), dtype=jnp.float32) * scale_out, 'bo': jax.random.normal(ks[10], (D_MODEL,), dtype=jnp.float32) * 0.01}
    _L3_xattn_all = _L3_xattn_setup()
    _L3_xattn_in = {k: v for k, v in _L3_xattn_all.items() if k in ('wq', 'bq', 'wk', 'bk', 'wv', 'bv', 'wo', 'bo')}
    del _L3_xattn_all

    def _L3_ffn_setup():
        import jax, jax.numpy as jnp
        import numpy as np
        HIDDEN = 128
        MOE_FF = 64
        SHARED_FF = 352
        NUM_EXPERTS = 16
        TOP_K = 2
        NORM_TOPK = True
        key = jax.random.key(seed)
        ks = jax.random.split(key, 8)
        s = 0.02
        return {'layer_input': jax.random.normal(ks[0], (1, 256, HIDDEN), dtype=jnp.float32), 'gate_w': jax.random.normal(ks[1], (NUM_EXPERTS, HIDDEN), dtype=jnp.float32) * s, 'w_gate_up': jax.random.normal(ks[2], (NUM_EXPERTS, HIDDEN, 2 * MOE_FF), dtype=jnp.float32) * s, 'w_down': jax.random.normal(ks[3], (NUM_EXPERTS, MOE_FF, HIDDEN), dtype=jnp.float32) * s, 'shared_w_gate': jax.random.normal(ks[4], (SHARED_FF, HIDDEN), dtype=jnp.float32) * s, 'shared_w_up': jax.random.normal(ks[5], (SHARED_FF, HIDDEN), dtype=jnp.float32) * s, 'shared_w_down': jax.random.normal(ks[6], (HIDDEN, SHARED_FF), dtype=jnp.float32) * s, 'shared_gate_w': jax.random.normal(ks[7], (1, HIDDEN), dtype=jnp.float32) * s}
    _L3_ffn_all = _L3_ffn_setup()
    _L3_ffn_in = {k: v for k, v in _L3_ffn_all.items() if k in ('gate_w', 'w_gate_up', 'w_down', 'shared_w_gate', 'shared_w_up', 'shared_w_down', 'shared_gate_w')}
    del _L3_ffn_all
    return {'x': x, 'ctx_1024': ctx_1024, 'mask_BxS2_bf1': mask_BxS2_bf1, 'g_xattn': g_xattn, 'g_ffn': g_ffn, 'L0_xattn_Wq': _L0_xattn_in['Wq'], 'L0_xattn_Wk': _L0_xattn_in['Wk'], 'L0_xattn_Wv': _L0_xattn_in['Wv'], 'L0_xattn_Wo': _L0_xattn_in['Wo'], 'L0_xattn_q_norm_w': _L0_xattn_in['q_norm_w'], 'L0_xattn_k_norm_w': _L0_xattn_in['k_norm_w'], 'L0_ffn_gate_w': _L0_ffn_in['gate_w'], 'L0_ffn_gate_b': _L0_ffn_in['gate_b'], 'L0_ffn_w1': _L0_ffn_in['w1'], 'L0_ffn_b1': _L0_ffn_in['b1'], 'L0_ffn_w2': _L0_ffn_in['w2'], 'L0_ffn_b2': _L0_ffn_in['b2'], 'L1_xattn_Wq': _L1_xattn_in['Wq'], 'L1_xattn_bq': _L1_xattn_in['bq'], 'L1_xattn_Wk': _L1_xattn_in['Wk'], 'L1_xattn_bk': _L1_xattn_in['bk'], 'L1_xattn_Wv': _L1_xattn_in['Wv'], 'L1_xattn_bv': _L1_xattn_in['bv'], 'L1_xattn_Wo': _L1_xattn_in['Wo'], 'L1_xattn_bo': _L1_xattn_in['bo'], 'L1_xattn_ln_gamma': _L1_xattn_in['ln_gamma'], 'L1_xattn_ln_beta': _L1_xattn_in['ln_beta'], 'L1_ffn_gate_w': _L1_ffn_in['gate_w'], 'L1_ffn_gate_up_w': _L1_ffn_in['gate_up_w'], 'L1_ffn_down_w': _L1_ffn_in['down_w'], 'L2_xattn_Wq': _L2_xattn_in['Wq'], 'L2_xattn_bq': _L2_xattn_in['bq'], 'L2_xattn_Wk': _L2_xattn_in['Wk'], 'L2_xattn_bk': _L2_xattn_in['bk'], 'L2_xattn_Wv': _L2_xattn_in['Wv'], 'L2_xattn_bv': _L2_xattn_in['bv'], 'L2_xattn_Wo': _L2_xattn_in['Wo'], 'L2_xattn_bo': _L2_xattn_in['bo'], 'L2_ffn_w_ln1': _L2_ffn_in['w_ln1'], 'L2_ffn_Wq': _L2_ffn_in['Wq'], 'L2_ffn_Wkva': _L2_ffn_in['Wkva'], 'L2_ffn_Wkvb': _L2_ffn_in['Wkvb'], 'L2_ffn_Wo': _L2_ffn_in['Wo'], 'L2_ffn_w_ln2': _L2_ffn_in['w_ln2'], 'L2_ffn_Wgate': _L2_ffn_in['Wgate'], 'L2_ffn_expert_bias': _L2_ffn_in['expert_bias'], 'L2_ffn_Wg': _L2_ffn_in['Wg'], 'L2_ffn_Wu': _L2_ffn_in['Wu'], 'L2_ffn_Wd': _L2_ffn_in['Wd'], 'L2_ffn_sWg': _L2_ffn_in['sWg'], 'L2_ffn_sWu': _L2_ffn_in['sWu'], 'L2_ffn_sWd': _L2_ffn_in['sWd'], 'L3_xattn_wq': _L3_xattn_in['wq'], 'L3_xattn_bq': _L3_xattn_in['bq'], 'L3_xattn_wk': _L3_xattn_in['wk'], 'L3_xattn_bk': _L3_xattn_in['bk'], 'L3_xattn_wv': _L3_xattn_in['wv'], 'L3_xattn_bv': _L3_xattn_in['bv'], 'L3_xattn_wo': _L3_xattn_in['wo'], 'L3_xattn_bo': _L3_xattn_in['bo'], 'L3_ffn_gate_w': _L3_ffn_in['gate_w'], 'L3_ffn_w_gate_up': _L3_ffn_in['w_gate_up'], 'L3_ffn_w_down': _L3_ffn_in['w_down'], 'L3_ffn_shared_w_gate': _L3_ffn_in['shared_w_gate'], 'L3_ffn_shared_w_up': _L3_ffn_in['shared_w_up'], 'L3_ffn_shared_w_down': _L3_ffn_in['shared_w_down'], 'L3_ffn_shared_gate_w': _L3_ffn_in['shared_gate_w']}

def reference(x, ctx_1024, mask_BxS2_bf1, g_xattn, g_ffn, L0_xattn_Wq, L0_xattn_Wk, L0_xattn_Wv, L0_xattn_Wo, L0_xattn_q_norm_w, L0_xattn_k_norm_w, L0_ffn_gate_w, L0_ffn_gate_b, L0_ffn_w1, L0_ffn_b1, L0_ffn_w2, L0_ffn_b2, L1_xattn_Wq, L1_xattn_bq, L1_xattn_Wk, L1_xattn_bk, L1_xattn_Wv, L1_xattn_bv, L1_xattn_Wo, L1_xattn_bo, L1_xattn_ln_gamma, L1_xattn_ln_beta, L1_ffn_gate_w, L1_ffn_gate_up_w, L1_ffn_down_w, L2_xattn_Wq, L2_xattn_bq, L2_xattn_Wk, L2_xattn_bk, L2_xattn_Wv, L2_xattn_bv, L2_xattn_Wo, L2_xattn_bo, L2_ffn_w_ln1, L2_ffn_Wq, L2_ffn_Wkva, L2_ffn_Wkvb, L2_ffn_Wo, L2_ffn_w_ln2, L2_ffn_Wgate, L2_ffn_expert_bias, L2_ffn_Wg, L2_ffn_Wu, L2_ffn_Wd, L2_ffn_sWg, L2_ffn_sWu, L2_ffn_sWd, L3_xattn_wq, L3_xattn_bq, L3_xattn_wk, L3_xattn_bk, L3_xattn_wv, L3_xattn_bv, L3_xattn_wo, L3_xattn_bo, L3_ffn_gate_w, L3_ffn_w_gate_up, L3_ffn_w_down, L3_ffn_shared_w_gate, L3_ffn_shared_w_up, L3_ffn_shared_w_down, L3_ffn_shared_gate_w):
    import jax
    import jax.numpy as jnp

    def _L0_xattn_ref(x, context, Wq, Wk, Wv, Wo, q_norm_w, k_norm_w):
        import jax, jax.numpy as jnp
        import numpy as np
        DIM = 128
        N_HEADS = 16
        HEAD_DIM = DIM // N_HEADS
        EPS = 1e-06
        Q_THETA = 32.0
        K_THETA = 1000.0

        def precompute_freqs_1d(dim, seq_len, theta):
            freqs = theta ** (-jnp.arange(0, dim, 2, dtype=jnp.float32) / dim)
            t = jnp.arange(seq_len, dtype=jnp.float32)
            ang = t[:, None] * freqs[None, :]
            return (jnp.cos(ang), jnp.sin(ang))

        def rms_norm(x, w):
            var = jnp.mean(x * x, axis=-1, keepdims=True)
            return x * jax.lax.rsqrt(var + EPS) * w

        def apply_rope(t, cos, sin):
            cos = cos[None, None, :, :]
            sin = sin[None, None, :, :]
            t1, t2 = jnp.split(t, 2, axis=-1)
            return jnp.concatenate([t1 * cos - t2 * sin, t2 * cos + t1 * sin], axis=-1)
        B, T, C = x.shape
        S = context.shape[1]
        H, D = (N_HEADS, HEAD_DIM)
        q = (x @ Wq.T).reshape(B, T, H, D).transpose(0, 2, 1, 3)
        k = (context @ Wk.T).reshape(B, S, H, D).transpose(0, 2, 1, 3)
        v = (context @ Wv.T).reshape(B, S, H, D).transpose(0, 2, 1, 3)
        q = rms_norm(q, q_norm_w)
        k = rms_norm(k, k_norm_w)
        q_cos, q_sin = precompute_freqs_1d(D, T, Q_THETA)
        k_cos, k_sin = precompute_freqs_1d(D, S, K_THETA)
        q = apply_rope(q, q_cos, q_sin)
        k = apply_rope(k, k_cos, k_sin)
        scale = D ** (-0.5)
        attn = jnp.einsum('bhtd,bhsd->bhts', q, k) * scale
        attn = jax.nn.softmax(attn, axis=-1)
        out = jnp.einsum('bhts,bhsd->bhtd', attn, v)
        out = out.transpose(0, 2, 1, 3).reshape(B, T, C)
        return out @ Wo.T

    def _L0_ffn_ref(x, gate_w, gate_b, w1, b1, w2, b2):
        import jax, jax.numpy as jnp
        import numpy as np
        D_MODEL = 128
        FF = 512
        E = 8
        TOP_K = 2
        CAP_FACTOR = 1.25
        B, T = (4, 256)

        def _moe_forward(x, gate_w, gate_b, w1, b1, w2, b2):
            Bb, Tt, d = x.shape
            S = Bb * Tt
            C = int(CAP_FACTOR * S / E)
            xf = x.reshape(S, d)
            logits = xf @ gate_w + gate_b
            probs = jax.nn.softmax(logits, axis=1)
            topk_p, topk_i = jax.lax.top_k(probs, TOP_K)
            topk_pn = topk_p / jnp.sum(topk_p, axis=1, keepdims=True)
            rows = jnp.arange(S)
            w_te = jnp.zeros((S, E), xf.dtype).at[rows[:, None], topk_i].set(topk_pn)
            mask = jnp.zeros((S, E), bool).at[rows[:, None], topk_i].set(True)
            rank = jnp.cumsum(mask.astype(jnp.int32), axis=0)
            slot = jnp.where(mask & (rank <= C), rank - 1, C)
            e_grid = jnp.broadcast_to(jnp.arange(E), (S, E))
            t_grid = jnp.broadcast_to(rows[:, None], (S, E))
            buf = jnp.full((E, C + 1), S, jnp.int32).at[e_grid, slot].set(t_grid)
            idx = buf[:, :C]
            valid = idx < S
            x_pad = jnp.concatenate([xf, jnp.zeros((1, d), xf.dtype)], axis=0)
            xin = x_pad[idx]
            h = jax.nn.relu(jnp.einsum('ecd,edh->ech', xin, w1) + b1[:, None, :])
            out = jnp.einsum('ech,ehd->ecd', h, w2) + b2[:, None, :]
            w_pad = jnp.concatenate([w_te, jnp.zeros((1, E), xf.dtype)], axis=0)
            tok_w = w_pad[idx, jnp.arange(E)[:, None]]
            out = out * jnp.where(valid, tok_w, 0.0)[:, :, None]
            final = jnp.zeros((S + 1, d), xf.dtype).at[idx.reshape(-1)].add(out.reshape(-1, d))[:S]
            return final.reshape(Bb, Tt, d)
        return _moe_forward(x, gate_w, gate_b, w1, b1, w2, b2)

    def _L1_xattn_ref(query, key, value, Wq, bq, Wk, bk, Wv, bv, Wo, bo, ln_gamma, ln_beta):
        import jax, jax.numpy as jnp
        import numpy as np
        N_HEAD, MODEL_DIM, KEY_DIM, VALUE_DIM = (16, 128, 64, 64)
        B, S = (4, 256)
        EPS = 1e-05
        TEMP = float(np.sqrt(KEY_DIM))
        b, sq, _ = query.shape
        residual = query
        q = (query @ Wq + bq).reshape(b, sq, N_HEAD, KEY_DIM)
        k = (key @ Wk + bk).reshape(b, key.shape[1], N_HEAD, KEY_DIM)
        v = (value @ Wv + bv).reshape(b, value.shape[1], N_HEAD, VALUE_DIM)
        scores = jnp.einsum('bqhd,bkhd->bhqk', q, k) / TEMP
        attn = jax.nn.softmax(scores, axis=-1)
        out = jnp.einsum('bhqk,bkhd->bqhd', attn, v).reshape(b, sq, N_HEAD * VALUE_DIM)
        out = out @ Wo + bo + residual
        mu = jnp.mean(out, axis=-1, keepdims=True)
        var = jnp.var(out, axis=-1, keepdims=True)
        return (out - mu) * jax.lax.rsqrt(var + EPS) * ln_gamma + ln_beta

    def _L1_ffn_ref(x, gate_w, gate_up_w, down_w):
        import jax, jax.numpy as jnp
        import numpy as np
        FF_DIM = 256
        TOP_K = 2
        B, S, D = x.shape
        E = gate_up_w.shape[0]
        F = down_w.shape[1]
        x_flat = x.reshape(B * S, D)
        router_logits = x_flat @ gate_w
        router_probs = jax.nn.softmax(router_logits, axis=-1)
        top_k_probs, top_k_idx = jax.lax.top_k(router_probs, TOP_K)
        top_k_probs = top_k_probs / jnp.sum(top_k_probs, axis=-1, keepdims=True)
        gate_up = jnp.einsum('nd,edh->enh', x_flat, gate_up_w)
        gate_out = gate_up[..., :F]
        up_out = gate_up[..., F:]
        hidden = jax.nn.silu(gate_out) * up_out
        expert_out = jnp.einsum('enf,efd->end', hidden, down_w)
        out_t = jnp.transpose(expert_out, (1, 0, 2))
        sel = jnp.take_along_axis(out_t, top_k_idx[:, :, None], axis=1)
        output = jnp.sum(sel * top_k_probs[:, :, None], axis=1)
        return output.reshape(B, S, D)

    def _L2_xattn_ref(q, k, v, attention_mask, Wq, bq, Wk, bk, Wv, bv, Wo, bo):
        import jax, jax.numpy as jnp
        import numpy as np
        N_HEADS = 16
        D_MODEL = 128
        HEAD_DIM = D_MODEL // N_HEADS
        MASK_FILL = -100000000.0

        def _split_heads(x):
            B, S, _ = x.shape
            return x.reshape(B, S, N_HEADS, HEAD_DIM).transpose(0, 2, 1, 3)
        qm = _split_heads(q @ Wq.T + bq)
        km = _split_heads(k @ Wk.T + bk)
        vm = _split_heads(v @ Wv.T + bv)
        scores = jnp.einsum('bnlh,bnph->bnlp', qm, km) / np.sqrt(HEAD_DIM).astype(np.float32)
        mask = attention_mask[:, None, None, :]
        scores = jnp.where(mask, scores, MASK_FILL)
        attn = jax.nn.softmax(scores, axis=-1)
        out = jnp.einsum('bnlp,bnph->bnlh', attn, vm)
        B, _, L, _ = out.shape
        out = out.transpose(0, 2, 1, 3).reshape(B, L, D_MODEL)
        return out @ Wo.T + bo

    def _L2_ffn_ref(x, w_ln1, Wq, Wkva, Wkvb, Wo, w_ln2, Wgate, expert_bias, Wg, Wu, Wd, sWg, sWu, sWd):
        import jax, jax.numpy as jnp
        import numpy as np
        B, T, C = (2, 256, 128)
        H, D = (16, 64)
        CR = 8
        R = C // CR
        ROPE = D // 2
        NOPE = D - ROPE
        E, K, I, S = (8, 2, 64, 1)
        THETA = 100000.0
        EPS = 1e-05

        def _rmsnorm(x, w):
            rms = jnp.sqrt(jnp.mean(x * x, axis=-1, keepdims=True) + EPS)
            return w * (x / rms)

        def _rope(xh):
            d = xh.shape[-1]
            t = jnp.arange(xh.shape[2], dtype=jnp.float32)
            freqs = 1.0 / THETA ** (jnp.arange(0, d, 2, dtype=jnp.float32) / d)
            ang = jnp.outer(t, freqs)
            cos, sin = (jnp.cos(ang), jnp.sin(ang))
            xr = xh.reshape(xh.shape[:-1] + (d // 2, 2))
            x0, x1 = (xr[..., 0], xr[..., 1])
            rot = jnp.stack([x0 * cos - x1 * sin, x0 * sin + x1 * cos], axis=-1)
            return rot.reshape(xh.shape)

        def _attention(x, Wq, Wkva, Wkvb, Wo):
            b, t, _ = x.shape
            q = (x @ Wq).reshape(b, t, H, D).transpose(0, 2, 1, 3)
            ckv = x @ Wkva
            kv_latent, k_rope = (ckv[:, :, :R], ckv[:, :, R:])
            kv = (kv_latent @ Wkvb).reshape(b, t, H, NOPE).transpose(0, 2, 1, 3)
            k_rope = jnp.broadcast_to(k_rope[:, None, :, :], (b, H, t, ROPE))
            q_nope, q_rope = (q[..., :NOPE], q[..., NOPE:])
            q = jnp.concatenate([q_nope, _rope(q_rope)], axis=-1)
            k = jnp.concatenate([kv, _rope(k_rope)], axis=-1)
            v = jnp.concatenate([kv, jnp.zeros_like(k_rope)], axis=-1)
            att = jnp.einsum('bhqd,bhkd->bhqk', q, k) / jnp.sqrt(jnp.float32(D))
            mask = jnp.tril(jnp.ones((t, t), dtype=bool))
            att = jnp.where(mask, att, jnp.float32(-jnp.inf))
            att = jax.nn.softmax(att, axis=-1)
            y = jnp.einsum('bhqk,bhkd->bhqd', att, v)
            y = y.transpose(0, 2, 1, 3).reshape(b, t, H * D)
            return y @ Wo

        def _experts(x_flat, Wg, Wu, Wd):
            g = jax.nn.silu(jnp.einsum('nc,eci->nei', x_flat, Wg))
            u = jnp.einsum('nc,eci->nei', x_flat, Wu)
            return jnp.einsum('nei,eic->nec', g * u, Wd)

        def _moe(x, Wgate, expert_bias, Wg, Wu, Wd, sWg, sWu, sWd):
            b, t, c = x.shape
            xf = x.reshape(-1, c)
            shared = jnp.mean(_experts(xf, sWg, sWu, sWd), axis=1)
            logits = xf @ Wgate + expert_bias
            probs = jax.nn.softmax(logits, axis=-1)
            topk_p, topk_i = jax.lax.top_k(probs, K)
            topk_p = topk_p / jnp.sum(topk_p, axis=-1, keepdims=True)
            comb = jnp.sum(jax.nn.one_hot(topk_i, E, dtype=xf.dtype) * topk_p[..., None], axis=1)
            routed = jnp.einsum('ne,nec->nc', comb, _experts(xf, Wg, Wu, Wd))
            return (shared + routed).reshape(b, t, c)
        x = x + _attention(_rmsnorm(x, w_ln1), Wq, Wkva, Wkvb, Wo)
        residual = x
        xn = _rmsnorm(x, w_ln2)
        x_out = _moe(xn, Wgate, expert_bias, Wg, Wu, Wd, sWg, sWu, sWd)
        return residual + x_out

    def _L3_xattn_ref(values, keys, query, wq, bq, wk, bk, wv, bv, wo, bo):
        import jax, jax.numpy as jnp
        import numpy as np
        HEADS = 16
        D_MODEL = 128
        HEAD_DIM = D_MODEL // HEADS
        B, Sq = (query.shape[0], query.shape[1])
        Sk, Sv = (keys.shape[1], values.shape[1])
        v = values.reshape(B, Sv, HEADS, HEAD_DIM) @ wv.T + bv
        k = keys.reshape(B, Sk, HEADS, HEAD_DIM) @ wk.T + bk
        q = query.reshape(B, Sq, HEADS, HEAD_DIM) @ wq.T + bq
        energy = jnp.einsum('nqhd,nkhd->nhqk', q, k)
        attn = jax.nn.softmax(energy / jnp.sqrt(jnp.float32(D_MODEL)), axis=-1)
        out = jnp.einsum('nhqk,nkhd->nqhd', attn, v).reshape(B, Sq, D_MODEL)
        return out @ wo.T + bo

    def _L3_ffn_ref(layer_input, gate_w, w_gate_up, w_down, shared_w_gate, shared_w_up, shared_w_down, shared_gate_w):
        import jax, jax.numpy as jnp
        import numpy as np
        HIDDEN = 128
        MOE_FF = 64
        SHARED_FF = 352
        NUM_EXPERTS = 16
        TOP_K = 2
        NORM_TOPK = True
        B, S, D = layer_input.shape
        x = layer_input.reshape(-1, D)
        N = x.shape[0]
        shared = jax.nn.silu(x @ shared_w_gate.T) * (x @ shared_w_up.T) @ shared_w_down.T
        shared = shared * jax.nn.sigmoid(x @ shared_gate_w.T)
        logits = x @ gate_w.T
        probs = jax.nn.softmax(logits.astype(jnp.float32), axis=-1)
        rw, sel = jax.lax.top_k(probs, TOP_K)
        if NORM_TOPK:
            rw = rw / rw.sum(axis=-1, keepdims=True)
        rw = rw.astype(x.dtype)
        combine = jnp.zeros((N, NUM_EXPERTS), x.dtype).at[jnp.arange(N)[:, None], sel].set(rw)
        gu = jnp.einsum('nd,edf->nef', x, w_gate_up)
        g, h = jnp.split(gu, 2, axis=-1)
        h = jax.nn.silu(g) * h
        expert_out = jnp.einsum('nef,efd,ne->nd', h, w_down, combine)
        out = expert_out + shared
        return out.reshape(B, S, D)
    x = x + jnp.tanh(g_xattn[0]) * _L0_xattn_ref(_layernorm(x, axis=-1), ctx_1024, L0_xattn_Wq, L0_xattn_Wk, L0_xattn_Wv, L0_xattn_Wo, L0_xattn_q_norm_w, L0_xattn_k_norm_w)
    x = x + jnp.tanh(g_ffn[0]) * _L0_ffn_ref(_layernorm(x, axis=-1), L0_ffn_gate_w, L0_ffn_gate_b, L0_ffn_w1, L0_ffn_b1, L0_ffn_w2, L0_ffn_b2)
    x = x + jnp.tanh(g_xattn[1]) * _L1_xattn_ref(_layernorm(x, axis=-1), ctx_1024, ctx_1024, L1_xattn_Wq, L1_xattn_bq, L1_xattn_Wk, L1_xattn_bk, L1_xattn_Wv, L1_xattn_bv, L1_xattn_Wo, L1_xattn_bo, L1_xattn_ln_gamma, L1_xattn_ln_beta)
    x = x + jnp.tanh(g_ffn[1]) * _L1_ffn_ref(_layernorm(x, axis=-1), L1_ffn_gate_w, L1_ffn_gate_up_w, L1_ffn_down_w)
    x = x + jnp.tanh(g_xattn[2]) * _L2_xattn_ref(_layernorm(x, axis=-1), ctx_1024, ctx_1024, mask_BxS2_bf1, L2_xattn_Wq, L2_xattn_bq, L2_xattn_Wk, L2_xattn_bk, L2_xattn_Wv, L2_xattn_bv, L2_xattn_Wo, L2_xattn_bo)
    x = x + jnp.tanh(g_ffn[2]) * _L2_ffn_ref(_layernorm(x, axis=-1), L2_ffn_w_ln1, L2_ffn_Wq, L2_ffn_Wkva, L2_ffn_Wkvb, L2_ffn_Wo, L2_ffn_w_ln2, L2_ffn_Wgate, L2_ffn_expert_bias, L2_ffn_Wg, L2_ffn_Wu, L2_ffn_Wd, L2_ffn_sWg, L2_ffn_sWu, L2_ffn_sWd)
    x = x + jnp.tanh(g_xattn[3]) * _L3_xattn_ref(ctx_1024, ctx_1024, _layernorm(x, axis=-1), L3_xattn_wq, L3_xattn_bq, L3_xattn_wk, L3_xattn_bk, L3_xattn_wv, L3_xattn_bv, L3_xattn_wo, L3_xattn_bo)
    x = x + jnp.tanh(g_ffn[3]) * _L3_ffn_ref(_layernorm(x, axis=-1), L3_ffn_gate_w, L3_ffn_w_gate_up, L3_ffn_w_down, L3_ffn_shared_w_gate, L3_ffn_shared_w_up, L3_ffn_shared_w_down, L3_ffn_shared_gate_w)
    return x

_drawn_inputs = setup_inputs


def setup_inputs(seed=0):
    import zlib

    import numpy as np

    out = dict(_drawn_inputs(seed))
    spreads = {'L0_xattn_q_norm_w': (1.0, 0.6),
     'L0_xattn_k_norm_w': (1.0, 0.6),
     'L0_ffn_gate_b': (0.0, 0.435),
     'L0_ffn_b1': (0.0, 0.8),
     'L0_ffn_b2': (0.0, 0.455),
     'L1_xattn_bq': (0.0, 0.445),
     'L1_xattn_bk': (0.0, 0.8),
     'L1_xattn_bv': (0.0, 0.1),
     'L1_xattn_bo': (0.0, 0.1),
     'L1_xattn_ln_gamma': (1.0, 0.2),
     'L1_xattn_ln_beta': (0.0, 0.1),
     'L2_xattn_bq': (0.0, 0.63),
     'L2_xattn_bk': (0.0, 0.8),
     'L2_xattn_bv': (0.0, 0.1),
     'L2_xattn_bo': (0.0, 0.1),
     'L2_ffn_w_ln1': (1.0, 0.6),
     'L2_ffn_w_ln2': (1.0, 0.6),
     'L2_ffn_expert_bias': (0.0, 0.8)}
    factors = {'g_ffn': 8.0,
     'L0_ffn_gate_w': 2.994,
     'L0_ffn_w1': 5.955,
     'L0_ffn_w2': 4.46,
     'L1_ffn_gate_w': 8.0,
     'L1_ffn_gate_up_w': 8.0,
     'L1_ffn_down_w': 8.0,
     'L2_ffn_Wq': 8.0,
     'L2_ffn_Wkva': 3.683,
     'L2_ffn_Wkvb': 3.927,
     'L2_ffn_Wo': 3.334,
     'L2_ffn_Wgate': 5.798,
     'L2_ffn_Wg': 5.373,
     'L2_ffn_Wu': 5.043,
     'L2_ffn_Wd': 5.287,
     'L2_ffn_sWg': 3.535,
     'L2_ffn_sWu': 3.777,
     'L2_ffn_sWd': 4.525,
     'L3_xattn_bq': 8.0,
     'L3_xattn_bk': 8.0,
     'L3_ffn_gate_w': 8.0,
     'L3_ffn_w_gate_up': 8.0,
     'L3_ffn_w_down': 8.0,
     'L3_ffn_shared_w_gate': 5.801,
     'L3_ffn_shared_w_up': 5.907,
     'L3_ffn_shared_w_down': 5.693,
     'L3_ffn_shared_gate_w': 8.0}
    for name, (base, spread) in spreads.items():
        noise = np.random.default_rng([zlib.crc32(name.encode()), seed]).standard_normal(out[name].shape)
        drawn = base * np.exp(spread * noise) if base else spread * noise
        out[name] = jnp.asarray(drawn.astype(out[name].dtype))
    for name, factor in factors.items():
        out[name] = (out[name] * factor).astype(out[name].dtype)
    return out
```

```python
from contextlib import ExitStack

import concourse.bass as bass
from concourse import mybir
import numpy as np

F32 = mybir.dt.float32
BF16 = mybir.dt.bfloat16
U8 = mybir.dt.uint8
ALU = mybir.AluOpType
ACT = mybir.ActivationFunctionType
X_AXIS = mybir.AxisListType.X

LAYERS = 8
P = 128
D = 128
B = 4
SEQ = 512
QT = SEQ // P
NT = B * QT
CTX = 154
KC = CTX // 2
H = 16
LN_EPS = 1e-5


def at(trip, per_trip, n):
    return trip * per_trip + n


class Core:

    def __init__(self, nc, ctx):
        self.nc, self.ctx = nc, ctx
        self.resid = self.sb("resid", [P, NT, D])
        self.stat = self.sb("stat", [P, NT, 2])
        self.std = self.sb("std", [P, NT])
        self.rstd = self.sb("rstd", [P, NT])
        self.ident = self.sb("ident", [P, P])
        self.identb = self.sb("identb", [P, P], BF16)
        self.ones = self.sb("ones", [1, P])
        self.oneb = self.sb("oneb", [P, P], BF16)
        self.hmask = self.sb("hmask", [P, H])
        self.ctxT = self.sb("ctxT", [P, B * CTX])
        self.gate = self.sb("gate", [P, 8])
        self.padded = []
        self.squares = self.sem("squares")
        self.psum = ctx.enter_context(nc.psum_tensor("psum", [P, 8, 512], F32))

    def sb(self, name, shape, dt=F32):
        return self.ctx.enter_context(self.nc.sbuf_tensor(name, shape, dt))

    def sem(self, name):
        return self.ctx.enter_context(self.nc.semaphore(name))


def setup(core, io, loads):
    nc = core.nc
    with ExitStack() as scope:
        ctx_rows = scope.enter_context(nc.sbuf_tensor("ctx_rows", [KC, 2 * B, D], F32))
        parts = scope.enter_context(nc.sbuf_tensor("setup_parts", [P, NT, 6], F32))
        x_in = [core.sem(f"x_in{b}") for b in range(B)]
        ctx_in, gate_in = core.sem("ctx_in"), core.sem("gate_in")
        consts, ident_made = core.sem("consts"), core.sem("ident_made")
        ctx_ps, ctx_made = core.sem("ctx_ps"), core.sem("ctx_made")
        parts_made = core.sem("parts_made")
        zeroed = core.sem("zeroed")
        with nc.Block() as block:

            @block.sync
            def _(sp):
                sp.dma_start(ctx_rows[:], io["ctx"].rearrange("b (c p) d -> p (b c) d", p=KC)).then_inc(ctx_in, 16)
                xv = io["x"].rearrange("b (t p) d -> p (b t) d", p=P)
                for b in range(B):
                    sp.dma_start(core.resid[:, 4 * b:4 * b + 4, :], xv[:, 4 * b:4 * b + 4, :]).then_inc(x_in[b], 16)
                sp.dma_start(core.gate[:, 0:4], io["g_xattn"].partition_broadcast(P)).then_inc(gate_in, 16)
                sp.dma_start(core.gate[:, 4:8], io["g_ffn"].partition_broadcast(P)).then_inc(gate_in, 16)
                sp.wait_ge(zeroed, len(core.padded))
                for dst, src, sem, _ in loads:
                    sp.dma_start(dst, src).then_inc(sem, 16)

            @block.gpsimd
            def _(pool):
                for small in core.padded:
                    nc.gpsimd.memset(small[:], 0.0).then_inc(zeroed, 1)
                nc.gpsimd.memset(core.ident[:], 0.0).then_inc(consts, 1)
                nc.gpsimd.memset(core.ones[:], 1.0).then_inc(consts, 1)
                nc.gpsimd.memset(core.oneb[:], 1.0).then_inc(consts, 1)
                nc.gpsimd.memset(core.hmask[:], 1.0).then_inc(consts, 1)
                pool.wait_ge(consts, 4)
                nc.gpsimd.affine_select(out=core.ident[:], in_=core.ident[:], compare_op=ALU.not_equal,
                                        fill=1.0, base=0, pattern=[[-1, P]], channel_multiplier=1).then_inc(consts, 1)
                nc.gpsimd.affine_select(out=core.hmask[:], in_=core.hmask[:], compare_op=ALU.is_ge,
                                        fill=0.0, base=0, pattern=[[-8, H]], channel_multiplier=1).then_inc(consts, 1)
                pool.wait_ge(consts, 6)
                nc.gpsimd.affine_select(out=core.hmask[:], in_=core.hmask[:], compare_op=ALU.is_ge,
                                        fill=0.0, base=7, pattern=[[8, H]], channel_multiplier=-1).then_inc(consts, 1)
                nc.gpsimd.tensor_copy(core.identb[:], core.ident[:]).then_inc(ident_made, 1)

            @block.tensor
            def _(pe):
                pe.wait_ge(ctx_in, 16)
                pe.wait_ge(ident_made, 1)
                for k in range(2 * B):
                    last = nc.tensor.transpose(core.psum[:, k // 4, (k % 4) * KC:(k % 4 + 1) * KC],
                                               ctx_rows[:, k, :], core.ident[0:KC, 0:KC])
                last.then_inc(ctx_ps, 1)

            @block.scalar
            def _(act):
                act.wait_ge(gate_in, 32)
                nc.scalar.activation(core.gate[:], core.gate[:], ACT.Tanh)
                act.wait_ge(ctx_ps, 1)
                for k in range(2):
                    nc.scalar.activation(core.ctxT[:, k * 4 * KC:(k + 1) * 4 * KC],
                                         core.psum[:, k, 0:4 * KC], ACT.Copy).then_inc(ctx_made, 1)

            @block.vector
            def _(dve):
                for n in range(NT):
                    if n % 4 == 0:
                        dve.wait_ge(x_in[n // 4], 16)
                    nc.vector.bn_stats(parts[:, n, :], core.resid[:, n, :]).then_inc(parts_made, 1)
                for n in range(NT):
                    dve.wait_ge(parts_made, n + 1)
                    last = nc.vector.bn_aggr(core.stat[:, n, :], parts[:, n, :])
                last.then_inc(parts_made, 1)


class View:

    def __init__(self, ap):
        self.ap = ap

    def __getitem__(self, key):
        return self.ap[key] if key != slice(None) else self.ap


class Steps:

    def __init__(self, eng, sem, per_trip, trip):
        self.eng, self.sem, self.per, self.trip, self.n = eng, sem, per_trip, trip, 0

    def step(self, ins):
        self.n += 1
        ins.then_inc(self.sem, 1)
        return self.n

    def done(self, n=None):
        self.eng.wait_ge(self.sem, at(self.trip, self.per, self.n if n is None else n))

    def close(self):
        assert self.n == self.per, f"{self.n} steps a trip, not {self.per}"


def rows_rstd(core, name, dve_sem, act_sem, rms=False):
    nc = core.nc

    def vector(dve):
        if rms:
            nc.vector.tensor_tensor(core.rstd[:], core.stat[:, :, 0], core.stat[:, :, 0], ALU.mult).then_inc(core.squares, 1)
            dve.wait_ge(core.squares, 1)
            nc.vector.scalar_tensor_tensor(out=core.std[:], in0=core.rstd[:], scalar=LN_EPS, in1=core.stat[:, :, 1],
                                           op0=ALU.add, op1=ALU.add).then_inc(dve_sem, 1)
        else:
            nc.vector.tensor_scalar(core.std[:], core.stat[:, :, 1], LN_EPS, None, ALU.add).then_inc(dve_sem, 1)
        dve.wait_ge(act_sem, 1)
        nc.vector.reciprocal(core.rstd[:], core.std[:]).then_inc(dve_sem, 1)
        dve.wait_ge(dve_sem, 2)

    def scalar(act):
        act.wait_ge(dve_sem, 1)
        nc.scalar.activation(core.std[:], core.std[:], ACT.Sqrt).then_inc(act_sem, 1)

    return vector, scalar


def cross_attention(core, L, w, gate, stride, kind, loaded, n_loads, late_loads=()):
    nc = core.nc
    rope, masked, renorm = kind == "rope", kind == "mask", kind == "norm"
    dk = 8 if stride == 32 else 64
    G = P // stride
    NG = H // G
    E = H * dk
    dva = dk + 1
    HPU = 4 if stride == 32 else 1
    NU = H // HPU
    UPU = 2 * HPU
    LAG = 1 if stride == 32 else 2
    RING = (LAG + 1) * UPU
    OC = E // P
    scale = 128.0 ** -0.5 if kind == "plain" else float(dk) ** -0.5
    half = NG // 2
    NR = 2 * NG
    VH = max(1, E // 512)
    psum = core.psum
    s = {n: nc.alloc_semaphore(f"{L}_{n}") for n in (
        "prep", "var", "sd", "vec", "xn", "xt_ps", "ctxb", "proj", "freed", "sc", "mx", "mp",
        "mt_ps", "mt", "s2", "pt", "pv", "pvx", "on", "ot_ps", "ot", "out", "added", "rms_v", "rms_s", "rms_a", "kt")}

    with ExitStack() as scope:
        def sb(name, shape, dt=F32):
            return scope.enter_context(nc.sbuf_tensor(f"{L}_{name}", shape, dt))

        xn = sb("xn", [P, QT, D])
        xnT = sb("xnT", [P, SEQ])
        ctxb = sb("ctxb", [P, CTX])
        qT = sb("qT", [P, NG, SEQ])
        kT = sb("kT", [P, NG, CTX])
        va = sb("va", [KC, 2, H, dva])
        negmax = sb("negmax", [P, QT, H])
        rest = sb("rest", [P, QT, H])
        mparts = sb("mparts", [P, QT, H, stride], BF16)
        mT = sb("mT", [P, NG, SEQ], BF16)
        pT = sb("pT", [KC, RING, SEQ])
        rsum = sb("rsum", [P, QT, H])
        on = sb("on", [P, QT, E])
        oT = sb("oT", [P, OC, SEQ])
        parts = sb("parts", [P, QT, 6])
        mv = sb("mv", [P, QT, 2])
        new = sb("new", [P, QT, D])
        pool_done = sb("pool_done", [1, 1])
        if rope:
            qs = sb("qs", [P, QT * H, dk])
            ks = sb("ks", [KC, 2 * H, dk])
            tmp = sb("tmp", [P, QT * H, dk])
            tmpb = sb("tmpb", [P, QT * H, dk])
            ss = sb("ss", [P, QT * H])
            qp = sb("qp", [P, QT, H, stride])
            kp = sb("kp", [KC, 2, H, stride])
        else:
            wq, wk = w["wq"], w["wk"]
        if stride == 32 and not rope:
            wqp = sb("wqp", [P, H, stride])
            wkp = sb("wkp", [P, H, stride])
            wq = wqp[:].rearrange("p h s -> p (h s)")
            wk = wkp[:].rearrange("p h s -> p (h s)")
        wv = w["wv"]
        if kind == "plain":
            wvf = sb("wvf", [P, H, dk])
            wv = wvf[:].rearrange("p h s -> p (h s)")
        if masked:
            m_f = sb("m_f", [P, B * CTX])
            pen = sb("pen", [P, B * CTX])
            pen2 = sb("pen2", [P, B * CTX])
            penb = sb("penb", [P, 3, B * CTX], BF16)
            krow = sb("krow", [P, B * CTX], BF16)
            krowb = sb("krowb", [P, CTX], BF16)
        if renorm:
            y = sb("y", [P, QT, D])
            sdv = sb("sdv", [P, QT])
        stats_v, stats_s = rows_rstd(core, L, s["var"], s["sd"])

        units = [("x", 0)]
        if rope:
            units += [("q", 0), ("k", 0)] + [("v", (c, 0)) for c in range(2)]
            units += [("qt", g) for g in range(NG)] + [("kt", g) for g in range(NG)]
        else:
            units += [("q", g) for g in range(NG)] + [("k", g) for g in range(NG)]
            units += [("v", (c, h)) for c in range(2) for h in range(VH)]
        NUNIT = len(units)
        bank = {u: n % 4 for n, u in enumerate(units)}
        DVE_STEPS = {"rope": 41, "mask": 22, "plain": 21, "norm": 49}[kind]

        with nc.Block() as block:

            @block.sync
            def _(sp):
                for dst, src, sem, _ in late_loads:
                    sp.dma_start(dst, src).then_inc(sem, 16)

            @block.gpsimd
            def _(pool):
                prep = []
                prep.append(nc.gpsimd.memset(mparts[:], 0.0))
                prep.append(nc.gpsimd.memset(va[:], 1.0))
                if rope:
                    prep.append(nc.gpsimd.memset(qp[:], 0.0))
                    prep.append(nc.gpsimd.memset(kp[:], 0.0))
                if stride == 32 and not rope:
                    prep.append(nc.gpsimd.memset(wqp[:], 0.0))
                    prep.append(nc.gpsimd.memset(wkp[:], 0.0))
                for ins in prep:
                    ins.then_inc(s["prep"], 1)
                n = len(prep)
                pool.wait_ge(s["prep"], n)
                pool.wait_ge(loaded, 16 * n_loads)
                if masked:
                    nc.gpsimd.memset(mparts[:, :, :, 3:6], 1.0).then_inc(s["prep"], 1)
                    n += 1
                if kind == "mask":
                    for dst, src in ((wqp, w["wq"]), (wkp, w["wk"])):
                        nc.gpsimd.tensor_copy(dst[:, :, 0:dk], src[:].rearrange("p (h d) -> p h d", d=dk)).then_inc(s["prep"], 1)
                        n += 1
                if kind == "plain":
                    hm = core.hmask[:].unsqueeze(2).to_broadcast([P, H, dk])
                    for dst, src in ((wqp, w["wq"]), (wkp, w["wk"]), (wvf, w["wv"])):
                        nc.gpsimd.tensor_tensor(dst[:, :, 0:dk], src[:].unsqueeze(1).to_broadcast([P, H, dk]), hm,
                                                ALU.mult).then_inc(s["prep"], 1)
                        n += 1
                pool.wait_ge(s["prep"], n)
                nc.gpsimd.memset(pool_done[:], 0.0).then_inc(s["kt"], 1)

            @block.tensor
            def _(pe):
                pe.wait_ge(s["kt"], 1)
                with pe.Fori(0, B) as b:
                    def free(name, arg):
                        n = units.index((name, arg))
                        if n >= 4:
                            pe.wait_ge(s["freed"], at(b, NUNIT, n - 3))
                        return psum[:, n % 4, :]

                    pe.wait_ge(s["xn"], at(b, 1, 1))
                    for t in range(QT):
                        last = nc.tensor.transpose(psum[:, 0, t * P:(t + 1) * P], xn[:, t, :], core.ident[:])
                    last.then_inc(s["proj"], 1)
                    pe.wait_ge(s["ctxb"], at(b, 1, 1))
                    pe.wait_ge(s["freed"], at(b, NUNIT, 1))
                    for what, a in units[1:]:
                        out = free(what, a)
                        if what == "q" and rope:
                            for t in range(QT):
                                last = nc.tensor.matmul(out[:, t * P:(t + 1) * P], xnT[:, t * P:(t + 1) * P], w["wq"][:],
                                                        start=True, stop=True)
                        elif what == "q":
                            last = nc.tensor.matmul(out, wq[:, a * P:(a + 1) * P], xnT[:], start=True, stop=True)
                        elif what == "k" and rope:
                            for c in range(2):
                                last = nc.tensor.matmul(out[0:KC, c * P:(c + 1) * P], ctxb[:, c * KC:(c + 1) * KC],
                                                        w["wk"][:], start=True, stop=True)
                        elif what == "k":
                            last = nc.tensor.matmul(out[:, 0:CTX], wk[:, a * P:(a + 1) * P], ctxb[:], start=True, stop=True)
                        elif what == "v":
                            c, hh = a
                            n = min(E, 512)
                            last = nc.tensor.matmul(out[0:KC, 0:n], ctxb[:, c * KC:(c + 1) * KC],
                                                    wv[:, hh * 512:hh * 512 + n], start=True, stop=rope)
                            if not rope:
                                last = nc.tensor.matmul(out[0:KC, 0:n], core.ones[0:1, 0:KC],
                                                        w["bv"][0:1, hh * 512:hh * 512 + n], start=False, stop=True)
                        elif what == "qt":
                            if a == 0:
                                pe.wait_ge(s["rms_v"], at(b, 2, 1))
                            for t in range(QT):
                                last = nc.tensor.transpose(out[:, t * P:(t + 1) * P],
                                                           qp[:, t, a * G:(a + 1) * G, :].rearrange("p h s -> p (h s)"), core.ident[:])
                        elif what == "kt":
                            if a == 0:
                                pe.wait_ge(s["rms_v"], at(b, 2, 2))
                            for c in range(2):
                                last = nc.tensor.transpose(out[:, c * KC:(c + 1) * KC],
                                                           kp[:, c, a * G:(a + 1) * G, :].rearrange("p h s -> p (h s)"),
                                                           core.ident[0:KC, 0:KC])
                        last.then_inc(s["proj"], 1)
                    pe.wait_ge(s["freed"], at(b, NUNIT, NUNIT))
                    if masked:
                        pe.wait_ge(s["rms_v"], at(b, NG, NG))

                    def score_round(g, pair):
                        r = 2 * g + pair
                        back = 1 if G == 4 else 2
                        if r >= back:
                            pe.wait_ge(s["mx"], at(b, NR, r - back + 1))
                        for q in range(2):
                            t = 2 * pair + q
                            for j in range(G):
                                rows = slice(stride * j, stride * j + dk)
                                bk = j if G == 4 else 2 * (r % 2) + j
                                last = nc.tensor.matmul(psum[:, bk, q * CTX:(q + 1) * CTX], qT[rows, g, t * P:(t + 1) * P],
                                                        kT[rows, g, :], start=True, stop=not masked)
                                if masked:
                                    rows = slice(stride * j, stride * j + stride)
                                    last = nc.tensor.matmul(psum[:, bk, q * CTX:(q + 1) * CTX], w["sel"][rows, :],
                                                            krowb[rows, :], start=False, stop=True)
                        last.then_inc(s["sc"], 1)

                    def max_rows(hf):
                        pe.wait_ge(s["mp"], at(b, 2, hf + 1))
                        for k in range(half // 2):
                            if hf or k:
                                pe.wait_ge(s["mt"], at(b, NG // 2, hf * (half // 2) + k))
                            bb = psum[:, 7, :].bitcast(BF16)
                            for gg in range(2):
                                g = hf * half + 2 * k + gg
                                for t in range(QT):
                                    last = nc.tensor.transpose(bb[:, (gg * QT + t) * P:(gg * QT + t + 1) * P],
                                                               mparts[:, t, g * G:(g + 1) * G, :].rearrange("p h s -> p (h s)"),
                                                               core.identb[:])
                            last.then_inc(s["mt_ps"], 1)

                    def scoresT(u):
                        for k in range(UPU):
                            n = u * UPU + k
                            h, c = u * HPU + k % HPU, k // HPU
                            g, j = h // G, h % G
                            if n >= 3:
                                pe.wait_ge(s["pt"], at(b, 2 * H, n - 2))
                            rows = slice(stride * j, stride * j + dk)
                            full = slice(stride * j, stride * j + stride)
                            out = psum[0:KC, 4 + n % 3, :]
                            one = krowb[full, c * KC:(c + 1) * KC] if masked else core.oneb[full, 0:KC]
                            nc.tensor.matmul(out, kT[rows, g, c * KC:(c + 1) * KC], qT[rows, g, :], start=True, stop=False)
                            nc.tensor.matmul(out, one, mT[full, g, :], start=False, stop=True).then_inc(s["s2"], 1)

                    def values(u):
                        pe.wait_ge(s["pt"], at(b, 2 * H, (u + 1) * UPU))
                        if u:
                            pe.wait_ge(s["pvx"], at(b, NU, u))
                        for k in range(HPU):
                            h = u * HPU + k
                            for t in range(QT):
                                o = (t * HPU + k) * dva
                                for c in range(2):
                                    slot = (u * UPU + c * HPU + k) % RING
                                    last = nc.tensor.matmul(psum[:, 7, o:o + dva], pT[:, slot, t * P:(t + 1) * P],
                                                            va[:, c, h, :], start=(c == 0), stop=(c == 1))
                        last.then_inc(s["pv"], 1)

                    for g in range(NG):
                        score_round(g, 0)
                        score_round(g, 1)
                    max_rows(0)
                    max_rows(1)
                    pe.wait_ge(s["mt"], at(b, NG // 2, NG // 2))
                    for u in range(NU + LAG):
                        if u < NU:
                            scoresT(u)
                        if u >= LAG:
                            values(u - LAG)
                    pe.wait_ge(s["pvx"], at(b, NU, NU))
                    for c in range(OC):
                        if c >= 4:
                            pe.wait_ge(s["ot"], at(b, OC, c - 3))
                        for t in range(QT):
                            last = nc.tensor.transpose(psum[:, c % 4, t * P:(t + 1) * P], on[:, t, c * P:(c + 1) * P], core.ident[:])
                        last.then_inc(s["ot_ps"], 1)
                    pe.wait_ge(s["ot"], at(b, OC, OC))
                    for t in range(QT):
                        for c in range(OC):
                            last = nc.tensor.matmul(psum[:, 7, t * P:(t + 1) * P], oT[:, c, t * P:(t + 1) * P],
                                                    w["wo"][:, c * P:(c + 1) * P], start=(c == 0), stop=(rope and c == OC - 1))
                        if not rope:
                            last = nc.tensor.matmul(psum[:, 7, t * P:(t + 1) * P], core.ones[0:1, :], w["bo"][0:1, :],
                                                    start=False, stop=True)
                    last.then_inc(s["out"], 1)

            @block.scalar
            def _(act):
                stats_s(act)
                with act.Fori(0, B) as b:
                    for n, (what, a) in enumerate(units):
                        src = psum[:, n % 4, :]
                        act.wait_ge(s["proj"], at(b, NUNIT, n + 1))
                        if what == "x":
                            ins = nc.scalar.activation(xnT[:], src, ACT.Copy)
                        elif what == "q" and rope:
                            ins = nc.scalar.activation(qs[:].rearrange("p h d -> p (h d)"), src, ACT.Copy)
                        elif what == "q":
                            ins = nc.scalar.activation(qT[:, a, :], src, ACT.Identity, bias=w["bq"][:, a:a + 1])
                        elif what == "k" and rope:
                            ins = nc.scalar.activation(ks[:].rearrange("p h d -> p (h d)"), src[0:KC, 0:2 * P], ACT.Copy)
                        elif what == "k":
                            ins = nc.scalar.activation(kT[:, a, :], src[:, 0:CTX], ACT.Identity, bias=w["bk"][:, a:a + 1])
                        elif what == "v":
                            c, hh = a
                            nh = min(E, 512) // dk
                            ins = nc.scalar.activation(va[:, c, hh * nh:(hh + 1) * nh, 0:dk],
                                                       src[0:KC, 0:nh * dk].rearrange("p (h d) -> p h d", d=dk), ACT.Copy)
                        elif what == "qt":
                            ins = nc.scalar.activation(qT[:, a, :], src, ACT.Copy)
                        elif what == "kt":
                            ins = nc.scalar.activation(kT[:, a, :], src[:, 0:CTX], ACT.Copy)
                        ins.then_inc(s["freed"], 1)
                        if rope and what in ("q", "k"):
                            act.wait_ge(s["rms_s"], at(b, 2, 1 if what == "q" else 2))
                            rows = P if what == "q" else KC
                            cols = QT * H if what == "q" else 2 * H
                            nc.scalar.activation(ss[0:rows, 0:cols], ss[0:rows, 0:cols], ACT.Sqrt).then_inc(s["rms_a"], 1)
                    for n in range(2 * H):
                        u = n // UPU
                        act.wait_ge(s["s2"], at(b, 2 * H, n + 1))
                        if n % UPU == 0 and u > LAG:
                            act.wait_ge(s["pv"], at(b, NU, u - LAG))
                        nc.scalar.activation(pT[:, n % RING, :], psum[0:KC, 4 + n % 3, :], ACT.Exp, scale=scale).then_inc(s["pt"], 1)
                    for c in range(OC):
                        act.wait_ge(s["ot_ps"], at(b, OC, c + 1))
                        nc.scalar.activation(oT[:, c, :], psum[:, c % 4, :], ACT.Copy).then_inc(s["ot"], 1)
                    if renorm:
                        act.wait_ge(s["rms_s"], at(b, 1, 1))
                        nc.scalar.activation(sdv[:], sdv[:], ACT.Sqrt).then_inc(s["rms_a"], 1)

            @block.vector
            def _(dve):
                stats_v(dve)
                dve.wait_ge(loaded, 16 * n_loads)
                if masked:
                    V0 = s["added"]
                    MASK_FILL = -1e8 / scale
                    nc.vector.tensor_copy(m_f[:], w["mask"][:]).then_inc(V0, 1)
                    dve.wait_ge(V0, 1)
                    nc.vector.tensor_scalar(pen[:], m_f[:], 1.0, -MASK_FILL, ALU.subtract, ALU.mult).then_inc(V0, 1)
                    dve.wait_ge(V0, 2)
                    nc.vector.tensor_copy(penb[:, 0, :], pen[:]).then_inc(V0, 1)
                    dve.wait_ge(V0, 3)
                    nc.vector.tensor_tensor(pen2[:], pen[:], penb[:, 0, :], ALU.subtract).then_inc(V0, 1)
                    dve.wait_ge(V0, 4)
                    nc.vector.tensor_copy(penb[:, 1, :], pen2[:]).then_inc(V0, 1)
                    dve.wait_ge(V0, 5)
                    nc.vector.tensor_tensor(penb[:, 2, :], pen2[:], penb[:, 1, :], ALU.subtract).then_inc(V0, 1)
                    dve.wait_ge(V0, 6)
                    nc.vector.tensor_scalar(pen[:], penb[:, 0, :], w["rows"][:, 1:2], w["rows"][:, 0:1], ALU.mult, ALU.add).then_inc(V0, 1)
                    for r in range(1, 3):
                        dve.wait_ge(V0, 6 + r)
                        nc.vector.scalar_tensor_tensor(out=(pen, pen2, krow)[r][:], in0=penb[:, r, :], scalar=w["rows"][:, r + 1:r + 2],
                                                       in1=(None, pen, pen2)[r][:], op0=ALU.mult, op1=ALU.add).then_inc(V0, 1)
                    dve.wait_ge(V0, 9)
                    nc.vector.tensor_scalar(w["sel"][:], core.oneb[:], w["rows"][:, 4:5], None, ALU.mult).then_inc(V0, 1)
                    dve.wait_ge(V0, 10)
                with dve.Fori(0, B) as b:
                    v = Steps(dve, s["vec"], DVE_STEPS, b)

                    for t in range(QT):
                        n = b * QT + t
                        ins = nc.vector.tensor_scalar(xn[:, t, :], core.resid[:, bass.ds(n, 1), :].rearrange("p a d -> p (a d)"),
                                                      core.stat[:, bass.ds(n, 1), 0:1].rearrange("p a d -> p (a d)"),
                                                      core.rstd[:, bass.ds(n, 1)], ALU.subtract, ALU.mult)
                    ins.then_inc(s["xn"], 1)
                    nc.vector.tensor_copy(ctxb[:], core.ctxT[:, bass.ds(b * CTX, CTX)]).then_inc(s["ctxb"], 1)
                    if masked:
                        v.step(nc.vector.tensor_copy(krowb[:], krow[:, bass.ds(b * CTX, CTX)]))
                        v.done()
                        for g in range(NG):
                            dve.wait_ge(s["freed"], at(b, NUNIT, units.index(("k", g)) + 1))
                            nc.vector.tensor_tensor(kT[:, g, :], kT[:, g, :], m_f[:, bass.ds(b * CTX, CTX)], ALU.mult).then_inc(s["rms_v"], 1)
                    if rope:
                        for k, (x, rows, nt, xp, cs, sn, wn, unit) in enumerate((
                                (qs, P, QT, qp, w["qcos"], w["qsin"], w["qn"], 1), (ks, KC, 2, kp, w["kcos"], w["ksin"], w["kn"], 2))):
                            nh = nt * H
                            dve.wait_ge(s["freed"], at(b, NUNIT, unit + 1))
                            full = [rows, nh, dk]
                            v.step(nc.vector.tensor_tensor(tmp[0:rows, 0:nh, :], x[:], x[:], ALU.mult))
                            v.done()
                            v.step(nc.vector.tensor_reduce(ss[0:rows, 0:nh], tmp[0:rows, 0:nh, :], X_AXIS, ALU.add))
                            v.done()
                            nc.vector.tensor_scalar(ss[0:rows, 0:nh], ss[0:rows, 0:nh], 1.0 / dk, 1e-6, ALU.mult, ALU.add).then_inc(s["rms_s"], 1)
                            dve.wait_ge(s["rms_a"], at(b, 2, k + 1))
                            v.step(nc.vector.reciprocal(ss[0:rows, 0:nh], ss[0:rows, 0:nh]))
                            v.done()
                            v.step(nc.vector.tensor_tensor(tmp[0:rows, 0:nh, :], x[:], ss[0:rows, 0:nh].unsqueeze(2).to_broadcast(full), ALU.mult))
                            v.done()
                            v.step(nc.vector.tensor_tensor(x[:], tmp[0:rows, 0:nh, :], wn[0:rows, :].unsqueeze(1).to_broadcast(full), ALU.mult))
                            v.done()
                            xv = x[:].rearrange("p (t h) d -> p t h d", h=H)
                            av = tmp[0:rows, 0:nh, :].rearrange("p (t h) d -> p t h d", h=H)
                            bv = tmpb[0:rows, 0:nh, :].rearrange("p (t h) d -> p t h d", h=H)
                            shape = [rows, nt, H, dk // 2]
                            cb = cs[0:rows, :, :].unsqueeze(2).to_broadcast(shape)
                            sbn = sn[0:rows, :, :].unsqueeze(2).to_broadcast(shape)
                            lo, hi = slice(0, dk // 2), slice(dk // 2, dk)
                            v.step(nc.vector.tensor_tensor(av[:, :, :, lo], xv[:, :, :, lo], cb, ALU.mult))
                            v.step(nc.vector.tensor_tensor(av[:, :, :, hi], xv[:, :, :, hi], cb, ALU.mult))
                            v.step(nc.vector.tensor_tensor(bv[:, :, :, lo], xv[:, :, :, hi], sbn, ALU.mult))
                            v.step(nc.vector.tensor_tensor(bv[:, :, :, hi], xv[:, :, :, lo], sbn, ALU.mult))
                            v.done()
                            xpv = xp[0:rows, 0:nt, :, :]
                            v.step(nc.vector.tensor_tensor(xpv[:, :, :, lo], av[:, :, :, lo], bv[:, :, :, lo], ALU.subtract))
                            v.done()
                            nc.vector.tensor_tensor(xpv[:, :, :, hi], av[:, :, :, hi], bv[:, :, :, hi], ALU.add).then_inc(s["rms_v"], 1)
                            dve.wait_ge(s["rms_v"], at(b, 2, k + 1))

                    for g in range(NG):
                        for pair in range(2):
                            r = 2 * g + pair
                            dve.wait_ge(s["sc"], at(b, NR, r + 1))
                            bk = slice(0, 4) if G == 4 else slice(2 * (r % 2), 2 * (r % 2) + 2)
                            nc.vector.tensor_reduce(
                                negmax[:, 2 * pair:2 * pair + 2, g * G:(g + 1) * G].rearrange("p t h -> p h t"),
                                psum[:, bk, 0:2 * CTX].rearrange("p k (t c) -> p k t c", c=CTX),
                                X_AXIS, ALU.max, negate=True).then_inc(s["mx"], 1)
                        if g % half == half - 1:
                            hf = g // half
                            hs = slice(hf * half * G, (hf + 1) * half * G)
                            dve.wait_ge(s["mx"], at(b, NR, 2 * g + 2))
                            mpv = mparts[:, :, hs, :]
                            v.step(nc.vector.tensor_copy(mpv[:, :, :, 0], negmax[:, :, hs]))
                            v.done()
                            v.step(nc.vector.tensor_tensor(rest[:, :, hs], negmax[:, :, hs], mpv[:, :, :, 0], ALU.subtract))
                            v.done()
                            v.step(nc.vector.tensor_copy(mpv[:, :, :, 1], rest[:, :, hs]))
                            v.done()
                            nc.vector.tensor_tensor(mpv[:, :, :, 2], rest[:, :, hs], mpv[:, :, :, 1], ALU.subtract).then_inc(s["mp"], 1)
                    for k in range(NG // 2):
                        dve.wait_ge(s["mt_ps"], at(b, NG // 2, k + 1))
                        nc.vector.tensor_copy(mT[:, 2 * k:2 * k + 2, :].rearrange("p g q -> p (g q)"),
                                              psum[:, 7, :].bitcast(BF16)).then_inc(s["mt"], 1)
                    for u in range(NU):
                        dve.wait_ge(s["pv"], at(b, NU, u + 1))
                        pv = psum[:, 7, 0:QT * HPU * dva].rearrange("p (t h e) -> p t h e", h=HPU, e=dva)
                        hs = slice(u * HPU, (u + 1) * HPU)
                        v.step(nc.vector.reciprocal(rsum[:, :, hs], pv[:, :, :, dk]))
                        v.done()
                        nc.vector.tensor_tensor(on[:, :, u * HPU * dk:(u + 1) * HPU * dk].rearrange("p t (h e) -> p t h e", e=dk),
                                                pv[:, :, :, 0:dk], rsum[:, :, hs].unsqueeze(3).to_broadcast([P, QT, HPU, dk]),
                                                ALU.mult).then_inc(s["pvx"], 1)
                    dve.wait_ge(s["out"], at(b, 1, 1))
                    if renorm:
                        v.step(nc.vector.tensor_tensor(y[:], psum[:, 7, :].rearrange("p (t d) -> p t d", d=D), xn[:], ALU.add))
                        v.done()
                        for t in range(QT):
                            v.step(nc.vector.bn_stats(parts[:, t, :], y[:, t, :]))
                        v.done()
                        nc.vector.memset(rsum[:, 0, 0:1], 0.0)
                        for t in range(QT):
                            v.step(nc.vector.bn_aggr(mv[:, t, :], parts[:, t, :]))
                        v.done()
                        nc.vector.tensor_scalar(sdv[:], mv[:, :, 1], LN_EPS, None, ALU.add).then_inc(s["rms_s"], 1)
                        dve.wait_ge(s["rms_a"], at(b, 1, 1))
                        v.step(nc.vector.reciprocal(sdv[:], sdv[:]))
                        v.done()
                        for t in range(QT):
                            v.step(nc.vector.tensor_scalar(y[:, t, :], y[:, t, :], mv[:, t, 0:1], sdv[:, t:t + 1], ALU.subtract, ALU.mult))
                        v.done()
                        v.step(nc.vector.tensor_tensor(y[:], y[:], w["gamma"][:].unsqueeze(1).to_broadcast([P, QT, D]), ALU.mult))
                        v.done()
                        v.step(nc.vector.tensor_tensor(y[:], y[:], w["beta"][:].unsqueeze(1).to_broadcast([P, QT, D]), ALU.add))
                        v.done()
                        src = y[:].rearrange("p t d -> p (t d)")
                    else:
                        src = psum[:, 7, :]
                    update_rows(core, v, b, src, gate, new, parts, mv)
                    v.close()


def update_rows(core, v, b, src, gate, new, parts, mv, base=None, dest=None):
    nc = core.nc
    rb = (dest or core.resid)[:, bass.ds(b * QT, QT), :].rearrange("p t d -> p (t d)")
    nw = new[:].rearrange("p t d -> p (t d)")
    v.step(nc.vector.scalar_tensor_tensor(out=nw, in0=src, scalar=1.0 if gate is None else core.gate[:, gate:gate + 1],
                                          in1=rb if base is None else base,
                                          op0=ALU.mult, op1=ALU.add))
    v.done()
    for t in range(QT):
        v.step(nc.vector.bn_stats(parts[:, t, :], new[:, t, :]))
    v.done()
    v.step(nc.vector.tensor_scalar(rb, nw, 1.0, None, ALU.mult))
    for t in range(QT):
        v.step(nc.vector.bn_aggr(mv[:, t, :], parts[:, t, :]))
    v.done()
    v.step(nc.vector.tensor_scalar(core.stat[:, bass.ds(b * QT, QT), :], mv[:], 1.0, None, ALU.mult))
    v.done()


def experts(core, L, w, gate, E, items, loaded, n_loads, glu, capacity=0, biased=False, extra=None, x1=None):
    nc, psum = core.nc, core.psum
    NC = E + (extra is not None)
    NL = E + (extra == "sigmoid")
    NI = len(items)
    NUN = sum(len(u) for u, _ in items)
    ND = sum(len(d) for _, d in items) + biased
    MU = max(len(u) for u, _ in items)
    RING = 2 * MU
    SETS = 2 if glu else 4
    first_unit = [sum(len(u) for u, _ in items[:i]) for i in range(NI + 1)]
    first_down = [biased + sum(len(d) for _, d in items[:i]) for i in range(NI + 1)]
    STEPS = 28 + (2 if extra == "sigmoid" else 0) + (2 if capacity else 0)
    s = {n: nc.alloc_semaphore(f"{L}_{n}") for n in (
        "var", "sd", "vec", "xn", "xt_ps", "xt", "lg_ps", "gap", "th", "mask", "rank_ps", "comb", "ct_ps", "ct",
        "up", "silu", "hid", "down", "acc", "const")}

    with ExitStack() as scope:
        def sb(name, shape, dt=F32):
            return scope.enter_context(nc.sbuf_tensor(f"{L}_{name}", shape, dt))

        xn = sb("xn", [P, QT, D])
        xnT = sb("xnT", [P, SEQ])
        lg = sb("lg", [P, QT, NL])
        lg2 = sb("lg2", [P, QT, E])
        eq = sb("eq", [P, QT, E])
        score = sb("score", [P, QT, E])
        rev = sb("rev", [P, E])
        oh = sb("oh", [P, 2, QT, E])
        top = sb("top", [P, 2, QT])
        pick = sb("pick", [P, QT])
        gap = sb("gap", [P, 2, QT])
        wt = sb("wt", [P, 2, QT])
        comb = sb("comb", [P, QT, NC])
        acc = sb("acc", [P, QT, D])
        new = sb("new", [P, QT, D])
        parts = sb("parts", [P, QT, 6])
        mv = sb("mv", [P, QT, 2])
        hid = sb("hid", [P, RING, SEQ])
        if glu:
            sg = sb("sg", [P, 2, SEQ])
        if capacity:
            mask = sb("mask", [P, QT, E], BF16)
            before = sb("before", [P, E], BF16)
            tri = sb("tri", [P, P], BF16)
            picks = sb("picks", [P, E])
        if biased:
            cT = sb("cT", [E, SEQ])
        stats_v, stats_s = rows_rstd(core, L, s["var"], s["sd"], rms=x1 is not None)

        with nc.Block() as block:

            @block.gpsimd
            def _(pool):
                for e in range(E):
                    nc.gpsimd.memset(rev[:, e:e + 1], float(E - e)).then_inc(s["const"], 1)
                n = E
                if extra == "one":
                    nc.gpsimd.memset(comb[:], 1.0).then_inc(s["const"], 1)
                    n += 1
                if capacity:
                    nc.gpsimd.memset(tri[:], 1.0).then_inc(s["const"], 1)
                    nc.gpsimd.memset(before[:], 0.0).then_inc(s["const"], 1)
                    n += 2
                    pool.wait_ge(s["const"], n)
                    nc.gpsimd.affine_select(out=tri[:], in_=tri[:], compare_op=ALU.is_ge, fill=0.0, base=0,
                                            pattern=[[1, P]], channel_multiplier=-1).then_inc(s["const"], 1)

            n_const = E + (extra == "one") + (3 if capacity else 0)

            @block.tensor
            def _(pe):
                pe.wait_ge(loaded, 16 * n_loads)
                pe.wait_ge(s["const"], n_const)
                with pe.Fori(0, B) as b:
                    def router():
                        pe.wait_ge(s["xn"], at(b, 1, 1))
                        for t in range(QT):
                            last = nc.tensor.transpose(psum[:, 7, t * P:(t + 1) * P], xn[:, t, :], core.ident[:])
                        last.then_inc(s["xt_ps"], 1)
                        pe.wait_ge(s["xt"], at(b, 1, 1))
                        for t in range(QT):
                            out = psum[:, 7, t * NL:(t + 1) * NL]
                            last = nc.tensor.matmul(out, xnT[:, t * P:(t + 1) * P], w["gate"][:], start=True, stop="gate_b" not in w)
                            if "gate_b" in w:
                                last = nc.tensor.matmul(out, core.ones[0:1, :], w["gate_b"][:], start=False, stop=True)
                        last.then_inc(s["lg_ps"], 1)

                    def ranks():
                        pe.wait_ge(s["mask"], at(b, 1, 1))
                        for t in range(QT):
                            out = psum[:, 7, t * E:(t + 1) * E]
                            nc.tensor.matmul(out, tri[:], mask[:, t, :], start=True, stop=False)
                            for k in range(t):
                                nc.tensor.matmul(out, core.oneb[:], mask[:, k, :], start=False, stop=False)
                            last = nc.tensor.matmul(out, core.oneb[:], before[:], start=False, stop=True)
                        last.then_inc(s["rank_ps"], 1)

                    def second_biases():
                        pe.wait_ge(s["comb"], at(b, 1, 1))
                        for t in range(QT):
                            last = nc.tensor.transpose(psum[0:E, 7, t * P:(t + 1) * P], comb[:, t, 0:E], core.ident[:])
                        last.then_inc(s["ct_ps"], 1)
                        pe.wait_ge(s["ct"], at(b, 1, 1))
                        for t in range(QT):
                            last = nc.tensor.matmul(psum[:, 4, t * P:(t + 1) * P], cT[:, t * P:(t + 1) * P], w["b2"][:],
                                                    start=True, stop=True)
                        last.then_inc(s["down"], 1)

                    def up(i):
                        for k, (wg, wu, rows, _) in enumerate(items[i][0]):
                            n = first_unit[i] + k
                            if n >= SETS:
                                pe.wait_ge(s["hid"], at(b, NUN, n - SETS + 1))
                            if glu:
                                nc.tensor.matmul(psum[0:rows, 2 * (n % 2), :], wg, xnT[:], start=True, stop=True)
                                last = nc.tensor.matmul(psum[0:rows, 2 * (n % 2) + 1, :], wu, xnT[:], start=True, stop=True)
                            else:
                                last = nc.tensor.matmul(psum[0:rows, n % 4, :], wg, xnT[:], start=True, stop=True)
                            last.then_inc(s["up"], 1)

                    def down(i):
                        for k, (_, terms) in enumerate(items[i][1]):
                            n = first_down[i] + k
                            if k == 0:
                                pe.wait_ge(s["hid"], at(b, NUN, first_unit[i + 1]))
                            if n >= 3:
                                pe.wait_ge(s["acc"], at(b, ND, n - 2))
                            for t in range(QT):
                                for m, (u, rows, w2) in enumerate(terms):
                                    slot = (first_unit[i] + u) % RING
                                    last = nc.tensor.matmul(psum[:, 4 + n % 3, t * P:(t + 1) * P],
                                                            hid[rows, slot, t * P:(t + 1) * P], w2,
                                                            start=(m == 0), stop=(m == len(terms) - 1))
                            last.then_inc(s["down"], 1)

                    router()
                    up(0)
                    if capacity:
                        ranks()
                    for i in range(NI):
                        if i + 1 < NI:
                            up(i + 1)
                        if i == 0 and biased:
                            second_biases()
                        down(i)

            @block.scalar
            def _(act):
                stats_s(act)
                act.wait_ge(loaded, 16 * n_loads)
                with act.Fori(0, B) as b:
                    act.wait_ge(s["xt_ps"], at(b, 1, 1))
                    nc.scalar.activation(xnT[:], psum[:, 7, :], ACT.Copy).then_inc(s["xt"], 1)

                    def unit(i, k):
                        _, _, rows, bias = items[i][0][k]
                        n = first_unit[i] + k
                        act.wait_ge(s["up"], at(b, NUN, n + 1))
                        if glu:
                            if n >= 2:
                                act.wait_ge(s["hid"], at(b, NUN, n - 1))
                            nc.scalar.activation(sg[0:rows, n % 2, :], psum[0:rows, 2 * (n % 2), :], ACT.Silu).then_inc(s["silu"], 1)
                        else:
                            if k == 0 and i >= 2:
                                act.wait_ge(s["down"], at(b, ND, first_down[i - 1]))
                            nc.scalar.activation(hid[0:rows, n % RING, :], psum[0:rows, n % 4, :], ACT.Relu,
                                                 bias=bias).then_inc(s["hid"], 1)

                    for k in range(len(items[0][0])):
                        unit(0, k)
                    act.wait_ge(s["gap"], at(b, 1, 1))
                    nc.scalar.activation(gap[:], gap[:], ACT.Tanh, scale=0.5).then_inc(s["th"], 1)
                    for i in range(1, NI):
                        for k in range(len(items[i][0])):
                            unit(i, k)

            @block.vector
            def _(dve):
                stats_v(dve)
                dve.wait_ge(loaded, 16 * n_loads)
                dve.wait_ge(s["const"], n_const)
                if extra != "sigmoid":
                    nc.vector.memset(gap[:], 0.0).then_inc(s["var"], 1)
                    dve.wait_ge(s["var"], 3)
                with dve.Fori(0, B) as b:
                    v = Steps(dve, s["vec"], STEPS, b)
                    for t in range(QT):
                        n = b * QT + t
                        if x1 is None:
                            ins = nc.vector.tensor_scalar(xn[:, t, :], core.resid[:, bass.ds(n, 1), :].rearrange("p a d -> p (a d)"),
                                                          core.stat[:, bass.ds(n, 1), 0:1].rearrange("p a d -> p (a d)"),
                                                          core.rstd[:, bass.ds(n, 1)], ALU.subtract, ALU.mult)
                        else:
                            ins = nc.vector.scalar_tensor_tensor(out=xn[:, t, :], in0=x1[:, bass.ds(n, 1), :].rearrange("p a d -> p (a d)"),
                                                                 scalar=core.rstd[:, bass.ds(n, 1)], in1=w["ln2"][:],
                                                                 op0=ALU.mult, op1=ALU.mult)
                    ins.then_inc(s["xn"], 1)
                    dve.wait_ge(s["lg_ps"], at(b, 1, 1))
                    v.step(nc.vector.tensor_copy(lg[:], psum[:, 7, 0:QT * NL].rearrange("p (t e) -> p t e", e=NL)))
                    v.done()
                    le = lg[:, :, 0:E]
                    revb = rev[:].unsqueeze(1).to_broadcast([P, QT, E])

                    def across(x):
                        return x.unsqueeze(2).to_broadcast([P, QT, E])

                    src = le
                    for r in range(2):
                        v.step(nc.vector.tensor_reduce(top[:, r, :], src, X_AXIS, ALU.max))
                        v.done()
                        v.step(nc.vector.tensor_tensor(eq[:], src, across(top[:, r, :]), ALU.is_equal))
                        v.done()
                        v.step(nc.vector.tensor_tensor(score[:], eq[:], revb, ALU.mult))
                        v.done()
                        v.step(nc.vector.tensor_reduce(pick[:], score[:], X_AXIS, ALU.max))
                        v.done()
                        v.step(nc.vector.tensor_tensor(oh[:, r, :, :], revb, across(pick[:]), ALU.is_equal))
                        v.done()
                        if r == 0:
                            v.step(nc.vector.scalar_tensor_tensor(out=lg2[:], in0=oh[:, 0, :, :], scalar=-3e38, in1=le,
                                                                  op0=ALU.mult, op1=ALU.add))
                            v.done()
                            src = lg2[:]
                    if capacity:
                        v.step(nc.vector.tensor_tensor(mask[:], oh[:, 0, :, :], oh[:, 1, :, :], ALU.add))
                        v.done()
                        nc.vector.tensor_reduce(picks[:], mask[:].rearrange("p t e -> p e t"), X_AXIS, ALU.add).then_inc(s["mask"], 1)
                    if extra == "sigmoid":
                        v.step(nc.vector.tensor_copy(gap[:, 1, :], lg[:, :, E]))
                    nc.vector.tensor_tensor(gap[:, 0, :], top[:, 0, :], top[:, 1, :], ALU.subtract).then_inc(s["gap"], 1)
                    dve.wait_ge(s["th"], at(b, 1, 1))
                    v.step(nc.vector.tensor_scalar(wt[:, 0, :], gap[:, 0, :], 0.5, 0.5, ALU.mult, ALU.add))
                    v.step(nc.vector.tensor_scalar(wt[:, 1, :], gap[:, 0, :], -0.5, 0.5, ALU.mult, ALU.add))
                    v.done()
                    v.step(nc.vector.tensor_tensor(eq[:], oh[:, 0, :, :], across(wt[:, 0, :]), ALU.mult))
                    v.step(nc.vector.tensor_tensor(score[:], oh[:, 1, :, :], across(wt[:, 1, :]), ALU.mult))
                    v.done()
                    if extra == "sigmoid":
                        v.step(nc.vector.tensor_scalar(comb[:, :, E], gap[:, 1, :], 0.5, 0.5, ALU.mult, ALU.add))
                    v.step(nc.vector.tensor_tensor(comb[:, :, 0:E], eq[:], score[:], ALU.add))
                    v.done()
                    if capacity:
                        dve.wait_ge(s["rank_ps"], at(b, 1, 1))
                        v.step(nc.vector.tensor_scalar(eq[:], psum[:, 7, 0:QT * E].rearrange("p (t e) -> p t e", e=E),
                                                       float(capacity), None, ALU.is_le))
                        v.done()
                        nc.vector.tensor_tensor(before[:], before[:], picks[:], ALU.add)
                        nc.vector.tensor_tensor(comb[:], comb[:], eq[:], ALU.mult).then_inc(s["comb"], 1)
                        dve.wait_ge(s["comb"], at(b, 1, 1))
                    if biased:
                        dve.wait_ge(s["ct_ps"], at(b, 1, 1))
                        nc.vector.tensor_copy(cT[:], psum[0:E, 7, :]).then_inc(s["ct"], 1)

                    def product(i):
                        for k, (_, _, rows, _) in enumerate(items[i][0]):
                            n = first_unit[i] + k
                            dve.wait_ge(s["silu"], at(b, NUN, n + 1))
                            if k == 0 and i >= 2:
                                dve.wait_ge(s["down"], at(b, ND, first_down[i - 1]))
                            nc.vector.tensor_tensor(hid[0:rows, n % RING, :], sg[0:rows, n % 2, :],
                                                    psum[0:rows, 2 * (n % 2) + 1, :], ALU.mult).then_inc(s["hid"], 1)

                    def accumulate(n, col):
                        dve.wait_ge(s["down"], at(b, ND, n + 1))
                        if n:
                            dve.wait_ge(s["acc"], at(b, ND, n))
                        for t in range(QT):
                            ps = psum[:, 4 + n % 3, t * P:(t + 1) * P]
                            if col is None:
                                ins = nc.vector.tensor_copy(acc[:, t, :], ps)
                            elif n or x1 is not None:
                                base = acc[:, t, :] if n else x1[:, bass.ds(b * QT + t, 1), :].rearrange("p a d -> p (a d)")
                                ins = nc.vector.scalar_tensor_tensor(out=acc[:, t, :], in0=ps, scalar=comb[:, t, col:col + 1],
                                                                     in1=base, op0=ALU.mult, op1=ALU.add)
                            else:
                                ins = nc.vector.tensor_scalar(acc[:, t, :], ps, comb[:, t, col:col + 1], None, ALU.mult)
                        ins.then_inc(s["acc"], 1)

                    if glu:
                        product(0)
                    if biased:
                        accumulate(0, None)
                    for i in range(NI):
                        if glu and i + 1 < NI:
                            product(i + 1)
                        for k, (col, _) in enumerate(items[i][1]):
                            accumulate(first_down[i] + k, col)
                    dve.wait_ge(s["acc"], at(b, ND, ND))
                    update_rows(core, v, b, acc[:].rearrange("p t d -> p (t d)"), gate, new, parts, mv)
                    v.close()


def causal_attention(core, L, w, x1, loaded, n_loads):
    nc, psum = core.nc, core.psum
    DK, NOPE, ROPE, R = 64, 32, 32, 16
    G, NG = 2, 8
    DVA = NOPE + 1
    LAG, RING = 1, 8
    scale = float(DK) ** -0.5
    NR = NG * QT
    s = {n: nc.alloc_semaphore(f"{L}_{n}") for n in (
        "var", "sd", "vec", "ms", "rms", "xr", "proj", "freed", "qrot", "krot", "kfull", "sc", "mx", "mp", "mt_ps", "mt",
        "s2", "pt", "pv", "pvx", "ot_ps", "ot", "out", "const")}
    units = [("x", 0), ("lat", 0), ("kr", 0)] + [("kv", t) for t in range(QT)]
    units += [("q", (t, h)) for t in range(QT) for h in range(2)]
    units += [("kt", g) for g in range(NG)] + [("qt", g) for g in range(NG)]
    NUNIT = len(units)
    NS2 = H * QT
    STEPS = 90

    with ExitStack() as scope:
        def sb(name, shape, dt=F32):
            return scope.enter_context(nc.sbuf_tensor(f"{L}_{name}", shape, dt))

        y = sb("y", [P, QT, D])
        xr = sb("xr", [P, QT, D])
        xrT = sb("xrT", [P, SEQ])
        lat = sb("lat", [R, SEQ])
        krow = sb("krow", [P, QT, ROPE])
        krr = sb("krr", [P, QT, ROPE])
        qwork = sb("qwork", [P, RING * SEQ])
        qp = qwork[:].rearrange("p (t h e) -> p t h e", t=QT, e=DK)
        pT = qwork[:].rearrange("p (r q) -> p r q", q=SEQ)
        kwork = View(core.projections[:].rearrange("p a e -> p (a e)"))
        kp = kwork[:].rearrange("p (t h e) -> p t h e", t=QT, e=DK)
        on = kwork[:, 0:QT * H * NOPE].rearrange("p (t e) -> p t e", t=QT)
        oT = kwork[:, QT * H * NOPE:].rearrange("p (c q) -> p c q", q=SEQ)
        qT = sb("qT", [P, NG, SEQ])
        kT = sb("kT", [P, NG, SEQ])
        va = sb("va", [P, QT, H, DVA])
        ra = sb("ra", [P, 2, H, ROPE // 2])
        rb = sb("rb", [P, 2, H, ROPE // 2])
        negmax = sb("negmax", [P, QT, H])
        rest = sb("rest", [P, QT, H])
        mparts = sb("mparts", [P, QT, H, DK], BF16)
        mT = sb("mT", [P, NG, SEQ], BF16)
        rsum = sb("rsum", [P, QT, H])
        parts = sb("parts", [P, QT, 6])
        mv = sb("mv", [P, QT, 2])
        ms = sb("ms", [P, QT])
        new = sb("new", [P, QT, D])
        future = sb("future", [P, P], BF16)
        futureT = sb("futureT", [P, P], BF16)
        unit = sb("unit", [P, ROPE])
        stats_v, stats_s = rows_rstd(core, L, s["var"], s["sd"])

        with nc.Block() as block:

            @block.gpsimd
            def _(pool):
                nc.gpsimd.memset(mparts[:], 0.0).then_inc(s["const"], 1)
                nc.gpsimd.memset(va[:], 1.0).then_inc(s["const"], 1)
                nc.gpsimd.memset(future[:], 0.0).then_inc(s["const"], 1)
                nc.gpsimd.memset(futureT[:], 0.0).then_inc(s["const"], 1)
                nc.gpsimd.memset(unit[:], 1.0).then_inc(s["const"], 1)
                pool.wait_ge(s["const"], 5)
                nc.gpsimd.affine_select(out=future[:], in_=future[:], compare_op=ALU.is_ge, fill=-1e30, base=0,
                                        pattern=[[-1, P]], channel_multiplier=1).then_inc(s["const"], 1)
                nc.gpsimd.affine_select(out=futureT[:], in_=futureT[:], compare_op=ALU.is_ge, fill=-1e30, base=0,
                                        pattern=[[1, P]], channel_multiplier=-1).then_inc(s["const"], 1)
                with pool.Fori(0, B) as b:
                    pool.wait_ge(s["krot"], at(b, 1, 1))
                    nc.gpsimd.tensor_tensor(kp[:, :, :, NOPE:DK], krr[:].unsqueeze(2).to_broadcast([P, QT, H, ROPE]),
                                            unit[:].unsqueeze(1).unsqueeze(1).to_broadcast([P, QT, H, ROPE]), ALU.mult).then_inc(s["kfull"], 1)

            @block.tensor
            def _(pe):
                pe.wait_ge(loaded, 16 * n_loads)
                pe.wait_ge(s["const"], 7)
                with pe.Fori(0, B) as b:
                    pe.wait_ge(s["xr"], at(b, 1, 1))
                    for n, (what, a) in enumerate(units):
                        out = psum[:, n % 4, :]
                        if what == "lat":
                            pe.wait_ge(s["freed"], at(b, NUNIT, 1))
                        if n >= 4:
                            pe.wait_ge(s["freed"], at(b, NUNIT, n - 3))
                        if what == "x":
                            for t in range(QT):
                                last = nc.tensor.transpose(out[:, t * P:(t + 1) * P], xr[:, t, :], core.ident[:])
                        elif what == "lat":
                            last = nc.tensor.matmul(out[0:R, :], w["wkva"][:, 0:R], xrT[:], start=True, stop=True)
                        elif what == "kr":
                            for t in range(QT):
                                last = nc.tensor.matmul(out[:, t * ROPE:(t + 1) * ROPE], xrT[:, t * P:(t + 1) * P],
                                                        w["wkva"][:, R:R + ROPE], start=True, stop=True)
                        elif what == "kv":
                            if a == 0:
                                pe.wait_ge(s["freed"], at(b, NUNIT, 2))
                            last = nc.tensor.matmul(out, lat[:, a * P:(a + 1) * P], w["wkvb"][:], start=True, stop=True)
                        elif what == "q":
                            t, h = a
                            last = nc.tensor.matmul(out, xrT[:, t * P:(t + 1) * P], w["wq"][:, h * 512:(h + 1) * 512],
                                                    start=True, stop=True)
                        else:
                            if a == 0:
                                pe.wait_ge(s["kfull" if what == "kt" else "qrot"], at(b, 1, 1) if what == "kt" else at(b, QT, QT))
                                if what == "kt":
                                    pe.wait_ge(s["freed"], at(b, NUNIT, 7))
                            src = kp if what == "kt" else qp
                            for t in range(QT):
                                last = nc.tensor.transpose(out[:, t * P:(t + 1) * P],
                                                           src[:, t, a * G:(a + 1) * G, :].rearrange("p h e -> p (h e)"), core.ident[:])
                        last.then_inc(s["proj"], 1)
                    pe.wait_ge(s["freed"], at(b, NUNIT, NUNIT))

                    for g in range(NG):
                        for t in range(QT):
                            r = g * QT + t
                            n = (t + 1) * P
                            if r >= 2:
                                pe.wait_ge(s["mx"], at(b, NR, r - 1))
                            for j in range(G):
                                rows = slice(DK * j, DK * (j + 1))
                                bk = 2 * (r % 2) + j
                                nc.tensor.matmul(psum[:, bk, 0:n], qT[rows, g, t * P:n], kT[rows, g, 0:n],
                                                 start=True, stop=True)
                            for j in range(G):
                                bk = 2 * (r % 2) + j
                                last = nc.tensor.matmul(psum[:, bk, t * P:n], core.identb[:], future[:], start=False, stop=True,
                                                        skip_group_check=True)
                            last.then_inc(s["sc"], 1)
                    for k in range(NG // 2):
                        if k % 2 == 0:
                            pe.wait_ge(s["mp"], at(b, 2, k // 2 + 1))
                        if k:
                            pe.wait_ge(s["mt"], at(b, NG // 2, k))
                        bb = psum[:, 7, :].bitcast(BF16)
                        for gg in range(2):
                            g = 2 * k + gg
                            for t in range(QT):
                                last = nc.tensor.transpose(bb[:, (gg * QT + t) * P:(gg * QT + t + 1) * P],
                                                           mparts[:, t, g * G:(g + 1) * G, :].rearrange("p h s -> p (h s)"), core.identb[:])
                        last.then_inc(s["mt_ps"], 1)
                    pe.wait_ge(s["mt"], at(b, NG // 2, NG // 2))

                    def scoresT(h):
                        g, j = h // G, h % G
                        rows = slice(DK * j, DK * (j + 1))
                        for k in range(QT):
                            n = h * QT + k
                            q0 = k * P
                            if n >= 3:
                                pe.wait_ge(s["pt"], at(b, NS2, n - 2))
                            out = psum[:, 4 + n % 3, q0:SEQ]
                            nc.tensor.matmul(out, kT[rows, g, q0:q0 + P], qT[rows, g, q0:SEQ], start=True, stop=False)
                            nc.tensor.matmul(out, core.oneb[rows, :], mT[rows, g, q0:SEQ], start=False, stop=True)
                            nc.tensor.matmul(psum[:, 4 + n % 3, q0:q0 + P], core.identb[:], futureT[:], start=False, stop=True,
                                             skip_group_check=True).then_inc(s["s2"], 1)

                    def values(h):
                        pe.wait_ge(s["pt"], at(b, NS2, (h + 1) * QT))
                        if h:
                            pe.wait_ge(s["pvx"], at(b, H, h))
                        for t in range(QT):
                            for k in range(t + 1):
                                last = nc.tensor.matmul(psum[:, 7, t * DVA:(t + 1) * DVA], pT[:, (h * QT + k) % RING, t * P:(t + 1) * P],
                                                        va[:, k, h, :], start=(k == 0), stop=(k == t))
                        last.then_inc(s["pv"], 1)

                    for h in range(H + LAG):
                        if h < H:
                            scoresT(h)
                        if h >= LAG:
                            values(h - LAG)
                    pe.wait_ge(s["pvx"], at(b, H, H))
                    for c in range(4):
                        for t in range(QT):
                            last = nc.tensor.transpose(psum[:, c, t * P:(t + 1) * P], on[:, t, c * P:(c + 1) * P], core.ident[:])
                        last.then_inc(s["ot_ps"], 1)
                    pe.wait_ge(s["ot"], at(b, 4, 4))
                    for t in range(QT):
                        for c in range(4):
                            last = nc.tensor.matmul(psum[:, 7, t * P:(t + 1) * P], oT[:, c, t * P:(t + 1) * P],
                                                    w["wo"][:, c, :], start=(c == 0), stop=(c == 3))
                    last.then_inc(s["out"], 1)

            @block.scalar
            def _(act):
                stats_s(act)
                act.wait_ge(s["const"], 7)
                with act.Fori(0, B) as b:
                    act.wait_ge(s["ms"], at(b, 1, 1))
                    nc.scalar.activation(ms[:], ms[:], ACT.Sqrt).then_inc(s["rms"], 1)
                    for n, (what, a) in enumerate(units):
                        src = psum[:, n % 4, :]
                        act.wait_ge(s["proj"], at(b, NUNIT, n + 1))
                        if what == "x":
                            ins = nc.scalar.activation(xrT[:], src, ACT.Copy)
                        elif what == "lat":
                            ins = nc.scalar.activation(lat[:], src[0:R, :], ACT.Copy)
                        elif what == "kr":
                            ins = nc.scalar.activation(krow[:].rearrange("p t e -> p (t e)"), src[:, 0:QT * ROPE], ACT.Copy)
                        elif what == "kv":
                            kv = src.rearrange("p (h e) -> p h e", e=NOPE)
                            nc.scalar.activation(kp[:, a, :, 0:NOPE], kv, ACT.Copy)
                            ins = nc.scalar.activation(va[:, a, :, 0:NOPE], kv, ACT.Copy)
                        elif what == "q":
                            t, h = a
                            ins = nc.scalar.activation(qp[:, t, 8 * h:8 * h + 8, :], src.rearrange("p (h e) -> p h e", e=DK), ACT.Copy)
                        elif what == "kt":
                            ins = nc.scalar.activation(kT[:, a, :], src, ACT.Copy)
                        else:
                            ins = nc.scalar.activation(qT[:, a, :], src, ACT.Copy)
                        ins.then_inc(s["freed"], 1)
                    for n in range(NS2):
                        h, k = n // QT, n % QT
                        act.wait_ge(s["s2"], at(b, NS2, n + 1))
                        if k == 0 and h > LAG:
                            act.wait_ge(s["pv"], at(b, H, h - LAG))
                        nc.scalar.activation(pT[:, n % RING, k * P:SEQ], psum[:, 4 + n % 3, k * P:SEQ], ACT.Exp, scale=scale).then_inc(s["pt"], 1)
                    for c in range(4):
                        act.wait_ge(s["ot_ps"], at(b, 4, c + 1))
                        nc.scalar.activation(oT[:, c, :], psum[:, c, :], ACT.Copy).then_inc(s["ot"], 1)

            @block.vector
            def _(dve):
                stats_v(dve)
                dve.wait_ge(loaded, 16 * n_loads)
                with dve.Fori(0, B) as b:
                    v = Steps(dve, s["vec"], STEPS, b)
                    for t in range(QT):
                        n = b * QT + t
                        v.step(nc.vector.tensor_scalar(y[:, t, :], core.resid[:, bass.ds(n, 1), :].rearrange("p a d -> p (a d)"),
                                                       core.stat[:, bass.ds(n, 1), 0:1].rearrange("p a d -> p (a d)"),
                                                       core.rstd[:, bass.ds(n, 1)], ALU.subtract, ALU.mult))
                    v.done()
                    for t in range(QT):
                        v.step(nc.vector.bn_stats(parts[:, t, :], y[:, t, :]))
                    v.done()
                    nc.vector.memset(rsum[:, 0, 0:1], 0.0)
                    for t in range(QT):
                        v.step(nc.vector.bn_aggr(mv[:, t, :], parts[:, t, :]))
                    v.done()
                    v.step(nc.vector.tensor_tensor(ms[:], mv[:, :, 0], mv[:, :, 0], ALU.mult))
                    v.done()
                    nc.vector.scalar_tensor_tensor(out=ms[:], in0=ms[:], scalar=LN_EPS, in1=mv[:, :, 1],
                                                   op0=ALU.add, op1=ALU.add).then_inc(s["ms"], 1)
                    dve.wait_ge(s["rms"], at(b, 1, 1))
                    v.step(nc.vector.reciprocal(ms[:], ms[:]))
                    v.done()
                    for t in range(QT):
                        ins = nc.vector.scalar_tensor_tensor(out=xr[:, t, :], in0=y[:, t, :], scalar=ms[:, t:t + 1],
                                                             in1=w["ln1"][:], op0=ALU.mult, op1=ALU.mult)
                    ins.then_inc(s["xr"], 1)

                    def rotate(dst, src, cos, sin, shape, sem):
                        n, hh, half = shape[1:]
                        a, c = ra[:, 0, 0:hh, :], ra[:, 1, 0:hh, :]
                        d, e = rb[:, 0, 0:hh, :], rb[:, 1, 0:hh, :]
                        x0, x1_ = src[:, :, 0::2], src[:, :, 1::2]
                        cb = cos.unsqueeze(1).to_broadcast([P, hh, half])
                        sb_ = sin.unsqueeze(1).to_broadcast([P, hh, half])
                        v.step(nc.vector.tensor_tensor(a, x0, cb, ALU.mult))
                        v.step(nc.vector.tensor_tensor(d, x1_, sb_, ALU.mult))
                        v.step(nc.vector.tensor_tensor(c, x0, sb_, ALU.mult))
                        v.step(nc.vector.tensor_tensor(e, x1_, cb, ALU.mult))
                        v.done()
                        v.step(nc.vector.tensor_tensor(dst[:, :, 0::2], a, d, ALU.subtract))
                        ins = nc.vector.tensor_tensor(dst[:, :, 1::2], c, e, ALU.add)
                        if sem is None:
                            v.step(ins)
                            v.done()
                        else:
                            return ins

                    dve.wait_ge(s["freed"], at(b, NUNIT, 3))
                    for t in range(QT):
                        ins = rotate(krr[:, t, :].unsqueeze(1), krow[:, t, :].unsqueeze(1), w["cos"][:, t, :], w["sin"][:, t, :],
                                     (P, 1, 1, ROPE // 2), None if t < QT - 1 else True)
                    ins.then_inc(s["krot"], 1)
                    dve.wait_ge(s["krot"], at(b, 1, 1))
                    for t in range(QT):
                        dve.wait_ge(s["freed"], at(b, NUNIT, 7 + 2 * (t + 1)))
                        rotate(qp[:, t, :, NOPE:DK], qp[:, t, :, NOPE:DK], w["cos"][:, t, :], w["sin"][:, t, :],
                               (P, 1, H, ROPE // 2), True).then_inc(s["qrot"], 1)
                        dve.wait_ge(s["qrot"], at(b, QT, t + 1))

                    for g in range(NG):
                        for t in range(QT):
                            r = g * QT + t
                            n = (t + 1) * P
                            dve.wait_ge(s["sc"], at(b, NR, r + 1))
                            bk = 2 * (r % 2)
                            nc.vector.tensor_reduce(negmax[:, t, g * G:(g + 1) * G], psum[:, bk:bk + 2, 0:n],
                                                    X_AXIS, ALU.max, negate=True).then_inc(s["mx"], 1)
                        if g % 4 == 3:
                            hs = slice((g - 3) * G, (g + 1) * G)
                            dve.wait_ge(s["mx"], at(b, NR, (g + 1) * QT))
                            v.step(nc.vector.tensor_copy(mparts[:, :, hs, 0], negmax[:, :, hs]))
                            v.done()
                            v.step(nc.vector.tensor_tensor(rest[:, :, hs], negmax[:, :, hs], mparts[:, :, hs, 0], ALU.subtract))
                            v.done()
                            v.step(nc.vector.tensor_copy(mparts[:, :, hs, 1], rest[:, :, hs]))
                            v.done()
                            nc.vector.tensor_tensor(mparts[:, :, hs, 2], rest[:, :, hs], mparts[:, :, hs, 1], ALU.subtract).then_inc(s["mp"], 1)
                    for k in range(NG // 2):
                        dve.wait_ge(s["mt_ps"], at(b, NG // 2, k + 1))
                        nc.vector.tensor_copy(mT[:, 2 * k:2 * k + 2, :].rearrange("p g q -> p (g q)"),
                                              psum[:, 7, :].bitcast(BF16)).then_inc(s["mt"], 1)
                    for h in range(H):
                        dve.wait_ge(s["pv"], at(b, H, h + 1))
                        pv = psum[:, 7, 0:QT * DVA].rearrange("p (t e) -> p t e", e=DVA)
                        v.step(nc.vector.reciprocal(rsum[:, :, h:h + 1], pv[:, :, NOPE:DVA]))
                        v.done()
                        nc.vector.tensor_tensor(on[:, :, h * NOPE:(h + 1) * NOPE], pv[:, :, 0:NOPE],
                                                rsum[:, :, h:h + 1].to_broadcast([P, QT, NOPE]), ALU.mult).then_inc(s["pvx"], 1)
                    dve.wait_ge(s["out"], at(b, 1, 1))
                    update_rows(core, v, b, psum[:, 7, :], None, new, parts, mv, base=y[:].rearrange("p t d -> p (t d)"), dest=x1)
                    v.close()


def store(core, io):
    stored = core.sem("stored")
    with core.nc.Block() as block:

        @block.sync
        def _(sp):
            sp.dma_start(io["out"].rearrange("b (t p) d -> p (b t) d", p=P), core.resid[:]).then_inc(stored, 16)
            sp.wait_ge(stored, 16)


def row(ap):
    return ap.rearrange("(a n) -> a n", a=1)


def build(nc, io):
    with ExitStack() as ctx:
        core = Core(nc, ctx)
        loads, late_loads, layers = [], [], []

        def load(L, w, sem, name, shape, src, dt=F32, dst=None):
            late = L in ("L2a", "L2f", "L3f") and name != "swd"
            if name not in w and late:
                n = int(np.prod(shape[1:]))
                view = core.arena[0:shape[0], core.arena_used:core.arena_used + n]
                core.arena_used += n
                assert core.arena_used <= core.arena.shape[1]
                if len(shape) == 3:
                    view = view.rearrange("p (a b) -> p a b", b=shape[2])
                w[name] = View(view)
            if name not in w:
                w[name] = core.sb(f"{L}_{name}", shape, dt)
            (late_loads if late else loads).append((w[name][:] if dst is None else dst(w[name]), src, sem, len(layers)))

        L, w, sem = "L0x", {}, core.sem("L0x_loaded")
        n0 = len(loads) + len(late_loads)
        for n in ("q", "k", "v", "o"):
            load(L, w, sem, "w" + n, [D, D], io[f"L0_xattn_W{n}"])
        load(L, w, sem, "qn", [P, 8], io["L0_xattn_q_norm_w"].partition_broadcast(P))
        load(L, w, sem, "kn", [P, 8], io["L0_xattn_k_norm_w"].partition_broadcast(P))
        for n in ("qcos", "qsin"):
            load(L, w, sem, n, [P, QT, 4], io[n])
        for n in ("kcos", "ksin"):
            load(L, w, sem, n, [KC, 2, 4], io[n])
        a = (L, w, sem, len(loads) + len(late_loads) - n0)
        layers.append(lambda a=a: cross_attention(core, a[0], a[1], 0, 32, "rope", a[2], a[3]))

        L, w, sem = "L0f", {}, core.sem("L0f_loaded")
        n0 = len(loads) + len(late_loads)
        load(L, w, sem, "gate", [P, 8], io["L0_ffn_gate_w"])
        load(L, w, sem, "gate_b", [1, 8], row(io["L0_ffn_gate_b"]))
        load(L, w, sem, "b1", [P, 8, 4], io["L0_ffn_b1"])
        load(L, w, sem, "b2", [8, D], io["L0_ffn_b2"])
        core.arena = core.sb("expert_arena", [P, 2 * 8 * 512])
        core.arena_used = 0
        w["w1"] = View(core.arena[:, 0:4096].rearrange("p (e f) -> p e f", e=8))
        w["w2"] = View(core.arena[:, 4096:8192].rearrange("p (e c d) -> p e c d", e=8, c=4))
        for e in range(8):
            load(L, w, sem, "w1", [P, 8, 512], io["L0_ffn_w1"][e], dst=lambda x, e=e: x[:, e, :])
            load(L, w, sem, "w2", [P, 8, 4, D], io["L0_ffn_w2"][e].rearrange("(c p) d -> p c d", p=P), dst=lambda x, e=e: x[:, e, :, :])
        items = [([(w["w1"][:, e, c * P:(c + 1) * P], None, P, w["b1"][:, e, c:c + 1]) for c in range(4)],
                  [(e, [(c, slice(0, P), w["w2"][:, e, c, :]) for c in range(4)])]) for e in range(8)]
        a = (L, w, sem, len(loads) + len(late_loads) - n0, items)
        layers.append(lambda a=a: experts(core, a[0], a[1], 4, 8, a[4], a[2], a[3], glu=False,
                                          capacity=int(1.25 * B * SEQ / 8), biased=True))

        L, w, sem = "L1x", {}, core.sem("L1x_loaded")
        n0 = len(loads) + len(late_loads)
        core.projections = core.sb("projections", [P, 4, H * 64])
        for k, n in enumerate(("q", "k", "v")):
            w["w" + n] = View(core.projections[:, k, :])
            load(L, w, sem, "w" + n, [D, H * 64], io[f"L1_xattn_W{n}"])
        w["wo"] = View(core.projections[:, 3, :].rearrange("p (c d) -> p c d", d=D))
        load(L, w, sem, "wo", [P, 8, D], io["L1_xattn_Wo"].rearrange("(c p) d -> p c d", p=P))
        w["wo"] = w["wo"][:].rearrange("p c d -> p (c d)")
        for n in ("q", "k"):
            load(L, w, sem, "b" + n, [P, 8], io[f"L1_xattn_b{n}"])
        load(L, w, sem, "bv", [1, H * 64], row(io["L1_xattn_bv"]))
        load(L, w, sem, "bo", [1, D], row(io["L1_xattn_bo"]))
        load(L, w, sem, "gamma", [P, D], io["L1_xattn_ln_gamma"].partition_broadcast(P))
        load(L, w, sem, "beta", [P, D], io["L1_xattn_ln_beta"].partition_broadcast(P))
        a = (L, w, sem, len(loads) + len(late_loads) - n0)
        layers.append(lambda a=a: cross_attention(core, a[0], a[1], 1, 64, "norm", a[2], a[3],
                                                  [x for x in late_loads if x[3] < LAYERS]))

        L, w, sem = "L1f", {}, core.sem("L1f_loaded")
        n0 = len(loads) + len(late_loads)
        load(L, w, sem, "gate", [P, 8], io["L1_ffn_gate_w"])
        for e in range(8):
            load(L, w, sem, "gu", [P, 8, 512], io["L1_ffn_gate_up_w"][e], dst=lambda x, e=e: x[:, e, :])
            load(L, w, sem, "dn", [P, 8, 2, D], io["L1_ffn_down_w"][e].rearrange("(c p) d -> p c d", p=P), dst=lambda x, e=e: x[:, e, :, :])
        items = [([(w["gu"][:, e, c * P:(c + 1) * P], w["gu"][:, e, 256 + c * P:256 + (c + 1) * P], P, None) for c in range(2)],
                  [(e, [(c, slice(0, P), w["dn"][:, e, c, :]) for c in range(2)])]) for e in range(8)]
        a = (L, w, sem, len(loads) + len(late_loads) - n0, items)
        layers.append(lambda a=a: experts(core, a[0], a[1], 5, 8, a[4], a[2], a[3], glu=True))

        L, w, sem = "L2x", {}, core.sem("L2x_loaded")
        n0 = len(loads) + len(late_loads)
        for n in ("q", "k", "v", "o"):
            load(L, w, sem, "w" + n, [D, D], io[f"L2_xattn_W{n}"])
        for n in ("q", "k"):
            bias = w["b" + n] = core.sb(f"L2x_b{n}", [P, 4])
            for j in range(4):
                loads.append((bias[32 * j:32 * j + 8, :], io[f"L2_xattn_b{n}"][j], sem, len(layers)))
        load(L, w, sem, "bv", [1, D], row(io["L2_xattn_bv"]))
        load(L, w, sem, "bo", [1, D], row(io["L2_xattn_bo"]))
        load(L, w, sem, "mask", [P, B * CTX], io["mask"].partition_broadcast(P), dt=U8)
        load(L, w, sem, "rows", [P, 5], io["rows"])
        w["sel"] = core.sb("L2x_sel", [P, P], BF16)
        core.padded += [w["bq"], w["bk"]]
        a = (L, w, sem, len(loads) + len(late_loads) - n0)
        layers.append(lambda a=a: cross_attention(core, a[0], a[1], 2, 32, "mask", a[2], a[3]))

        x1 = core.sb("x1", [P, NT, D])
        L, w, sem = "L2a", {}, core.sem("L2a_loaded")
        n0 = len(loads) + len(late_loads)
        load(L, w, sem, "wq", [P, H * 64], io["L2_ffn_Wq"])
        load(L, w, sem, "wkva", [P, 48], io["L2_ffn_Wkva"])
        load(L, w, sem, "wkvb", [16, 512], io["L2_ffn_Wkvb"])
        load(L, w, sem, "wo", [P, 4, D], io["L2_ffn_Wo"])
        load(L, w, sem, "ln1", [P, D], io["L2_ffn_w_ln1"].partition_broadcast(P))
        load(L, w, sem, "cos", [P, QT, 16], io["scos"])
        load(L, w, sem, "sin", [P, QT, 16], io["ssin"])
        a = (L, w, sem, len(loads) + len(late_loads) - n0)
        L, w, sem = "L2f", {}, core.sem("L2f_loaded")
        n0 = len(loads) + len(late_loads)
        load(L, w, sem, "gate", [P, 8], io["L2_ffn_Wgate"])
        load(L, w, sem, "gate_b", [1, 8], row(io["L2_ffn_expert_bias"]))
        load(L, w, sem, "ln2", [P, D], io["L2_ffn_w_ln2"].partition_broadcast(P))
        load(L, w, sem, "wg", [P, 9, 64], io["L2_ffn_Wg"].rearrange("e c i -> c e i"), dst=lambda x: x[:, 0:8, :])
        load(L, w, sem, "wg", [P, 9, 64], io["L2_ffn_sWg"].rearrange("e c i -> c e i"), dst=lambda x: x[:, 8:9, :])
        load(L, w, sem, "wu", [P, 9, 64], io["L2_ffn_Wu"].rearrange("e c i -> c e i"), dst=lambda x: x[:, 0:8, :])
        load(L, w, sem, "wu", [P, 9, 64], io["L2_ffn_sWu"].rearrange("e c i -> c e i"), dst=lambda x: x[:, 8:9, :])
        load(L, w, sem, "wd", [P, 5, D], io["L2_ffn_Wd"].rearrange("(a e) i d -> (e i) a d", e=2), dst=lambda x: x[:, 0:4, :])
        load(L, w, sem, "wd", [P, 5, D], io["L2_ffn_sWd"][0], dst=lambda x: x[0:64, 4, :])
        lo, hi = slice(0, 64), slice(64, 128)

        def pair(wg, wu, wd, i):
            return ([(wg[:, 2 * i:2 * i + 2, :].rearrange("p e i -> p (e i)"), wu[:, 2 * i:2 * i + 2, :].rearrange("p e i -> p (e i)"), P, None)],
                    [(2 * i, [(0, lo, wd[lo, i, :])]), (2 * i + 1, [(0, hi, wd[hi, i, :])])])

        items = [pair(w["wg"], w["wu"], w["wd"], i) for i in range(4)]
        items.append(([(w["wg"][:, 8, :], w["wu"][:, 8, :], 64, None)], [(8, [(0, lo, w["wd"][lo, 4, :])])]))
        a2 = (L, w, sem, len(loads) + len(late_loads) - n0, items)

        def level2(a=a, a2=a2):
            with nc.cleanup_on_exit():
                causal_attention(core, a[0], a[1], x1, a[2], a[3])
            experts(core, a2[0], a2[1], 6, 8, a2[4], a2[2], a2[3], glu=True, extra="one", x1=x1)

        layers.append(level2)

        L, w, sem = "L3x", {}, core.sem("L3x_loaded")
        n0 = len(loads) + len(late_loads)
        for n in ("q", "k", "v"):
            load(L, w, sem, "w" + n, [P, 8], io[f"L3_xattn_w{n}"])
        load(L, w, sem, "wo", [D, D], io["L3_xattn_wo"])
        for n in ("q", "k"):
            bias = w["b" + n] = core.sb(f"L3x_b{n}", [P, 4])
            for j in range(4):
                loads.append((bias[32 * j:32 * j + 8, :], io[f"L3_xattn_b{n}"], sem, len(layers)))
        core.padded += [w["bq"], w["bk"]]
        load(L, w, sem, "bv", [1, D], row(io["L3_xattn_bv"]))
        load(L, w, sem, "bo", [1, D], row(io["L3_xattn_bo"]))
        a = (L, w, sem, len(loads) + len(late_loads) - n0)
        layers.append(lambda a=a: cross_attention(core, a[0], a[1], 3, 32, "plain", a[2], a[3]))

        L, w, sem = "L3f", {}, core.sem("L3f_loaded")
        n0 = len(loads) + len(late_loads)
        load(L, w, sem, "gate", [P, 17], io["L3_ffn_gate_w"], dst=lambda x: x[:, 0:16])
        load(L, w, sem, "gate", [P, 17], io["L3_ffn_shared_gate_w"], dst=lambda x: x[:, 16:17])
        gu = io["L3_ffn_w_gate_up"].rearrange("e c i -> c e i")
        load(L, w, sem, "wg", [P, 16, 64], gu[:, :, 0:64])
        load(L, w, sem, "wu", [P, 16, 64], gu[:, :, 64:128])
        load(L, w, sem, "wd", [P, 8, D], io["L3_ffn_w_down"].rearrange("(a e) i d -> (e i) a d", e=2))
        load(L, w, sem, "swg", [P, 352], io["L3_ffn_shared_w_gate"])
        load(L, w, sem, "swu", [P, 352], io["L3_ffn_shared_w_up"])
        swd = io["L3_ffn_shared_w_down"]
        load(L, w, sem, "swd", [P, 3, D], swd[0:256, :].rearrange("(c p) d -> p c d", p=P), dst=lambda x: x[:, 0:2, :])
        load(L, w, sem, "swd", [P, 3, D], swd[256:352, :], dst=lambda x: x[0:96, 2, :])
        items = [pair(w["wg"], w["wu"], w["wd"], i) for i in range(8)]
        widths = [P, P, 96]
        items.append(([(w["swg"][:, k * P:k * P + m], w["swu"][:, k * P:k * P + m], m, None) for k, m in enumerate(widths)],
                      [(16, [(k, slice(0, m), w["swd"][0:m, k, :]) for k, m in enumerate(widths)])]))
        a = (L, w, sem, len(loads) + len(late_loads) - n0, items)
        layers.append(lambda a=a: experts(core, a[0], a[1], 7, 16, a[4], a[2], a[3], glu=True, extra="sigmoid"))

        setup(core, io, [x for x in loads if x[3] < LAYERS])
        for layer in layers[:LAYERS]:
            with nc.cleanup_on_exit():
                layer()
        store(core, io)



def kernel(**inputs):
    import concourse.bacc as _bacc
    from concourse.bass_utils import run_bass_kernel_spmd as _run

    c = {k: np.asarray(v) for k, v in inputs.items()}
    t = np.ascontiguousarray
    arrays = {
        "x": c["x"], "ctx": c["ctx_1024"], "g_xattn": c["g_xattn"], "g_ffn": c["g_ffn"],
    }
    for n in "qkvo":
        arrays[f"L0_xattn_W{n}"] = t(c[f"L0_xattn_W{n}"].T)
    arrays["L0_xattn_q_norm_w"] = c["L0_xattn_q_norm_w"]
    arrays["L0_xattn_k_norm_w"] = c["L0_xattn_k_norm_w"]

    for n in ("gate_w", "gate_b", "w1", "w2", "b2"):
        arrays[f"L0_ffn_{n}"] = c[f"L0_ffn_{n}"]
    arrays["L0_ffn_b1"] = c["L0_ffn_b1"].reshape(8, 4, P).transpose(2, 0, 1)
    for n in ("Wq", "Wk", "Wv", "Wo", "bv", "bo", "ln_gamma", "ln_beta"):
        arrays[f"L1_xattn_{n}"] = c[f"L1_xattn_{n}"]
    for n in ("bq", "bk"):
        arrays[f"L1_xattn_{n}"] = c[f"L1_xattn_{n}"].reshape(8, P).T
    for n in ("gate_w", "gate_up_w", "down_w"):
        arrays[f"L1_ffn_{n}"] = c[f"L1_ffn_{n}"]

    for n in "qkvo":
        arrays[f"L2_xattn_W{n}"] = c[f"L2_xattn_W{n}"].T
    for n in ("bv", "bo"):
        arrays[f"L2_xattn_{n}"] = c[f"L2_xattn_{n}"]
    for n in ("bq", "bk"):
        arrays[f"L2_xattn_{n}"] = c[f"L2_xattn_{n}"].reshape(4, 4, 8).transpose(1, 2, 0)
    arrays["mask"] = c["mask_BxS2_bf1"].reshape(-1).view(np.uint8)
    rows = np.zeros((P, 5), np.float32)
    for p in range(P):
        rows[p, 0] = p % 32 < 3
        rows[p, 4] = 3 <= p % 32 < 6
        for r in range(3):
            rows[p, 1 + r] = p % 32 == 3 + r
    arrays["rows"] = rows
    for n in ("Wq", "Wkva", "Wkvb", "w_ln1", "w_ln2", "Wgate", "expert_bias", "Wg", "Wu", "Wd", "sWg", "sWu", "sWd"):
        arrays[f"L2_ffn_{n}"] = c[f"L2_ffn_{n}"]
    arrays["L2_ffn_Wo"] = c["L2_ffn_Wo"].reshape(4, 4, 64, D)[:, :, 0:32].transpose(1, 2, 0, 3).reshape(P, 4, D)
    for n in "qkv":
        a = c[f"L3_xattn_w{n}"].T
        arrays[f"L3_xattn_w{n}"] = np.broadcast_to(a[None], (H, 8, 8)).reshape(P, 8)
    arrays["L3_xattn_wo"] = c["L3_xattn_wo"].T
    for n in ("bq", "bk"):
        arrays[f"L3_xattn_{n}"] = np.broadcast_to(c[f"L3_xattn_{n}"][:, None], (8, 4))
    arrays["L3_xattn_bv"] = np.broadcast_to(c["L3_xattn_bv"][None], (H, 8)).reshape(-1)
    arrays["L3_xattn_bo"] = c["L3_xattn_bo"]
    for n in ("gate_w", "shared_w_gate", "shared_w_up", "shared_w_down", "shared_gate_w"):
        arrays[f"L3_ffn_{n}"] = c[f"L3_ffn_{n}"].T
    for n in ("w_gate_up", "w_down"):
        arrays[f"L3_ffn_{n}"] = c[f"L3_ffn_{n}"]

    def table(n, theta, dim, rows):
        f = np.float32(theta) ** (-np.arange(0, dim, 2, dtype=np.float32) / np.float32(dim))
        ang = np.arange(n, dtype=np.float32)[:, None] * f[None, :].astype(np.float32)
        ang = ang.reshape(n // rows, rows, dim // 2).transpose(1, 0, 2)
        return t(np.cos(ang).astype(np.float32)), t(np.sin(ang).astype(np.float32))

    arrays["qcos"], arrays["qsin"] = table(SEQ, 32.0, 8, P)
    arrays["kcos"], arrays["ksin"] = table(CTX, 1000.0, 8, KC)
    arrays["scos"], arrays["ssin"] = table(SEQ, 100000.0, 32, P)

    nc = _bacc.Bacc("TRN2", target_bir_lowering=False, num_devices=1)
    feed, io = {}, {}
    for name, a in arrays.items():
        a = t(a)
        feed[f"in_{name}"] = a
        io[name] = nc.dram_tensor(f"in_{name}", a.shape, mybir.dt.from_np(a.dtype), kind="ExternalInput").ap()
    io["out"] = nc.dram_tensor("out_x", (B, SEQ, D), F32, kind="ExternalOutput").ap()
    build(nc, io)
    r = _run(nc, [feed], core_ids=[0])
    return r.results[0]["out_x"]
```

```python
from contextlib import ExitStack

import concourse.bass as bass
from concourse import mybir
import numpy as np

F32 = mybir.dt.float32
BF16 = mybir.dt.bfloat16
U8 = mybir.dt.uint8
ALU = mybir.AluOpType
ACT = mybir.ActivationFunctionType
X_AXIS = mybir.AxisListType.X

LAYERS = 8
P = 128
D = 128
B = 4
SEQ = 512
QT = SEQ // P
NT = B * QT
CTX = 154
KC = CTX // 2
H = 16
LN_EPS = 1e-5


def at(trip, per_trip, n):
    return trip * per_trip + n


class Core:

    def __init__(self, nc, ctx):
        self.nc, self.ctx = nc, ctx
        self.resid = self.sb("resid", [P, NT, D])
        self.stat = self.sb("stat", [P, NT, 2])
        self.std = self.sb("std", [P, NT])
        self.rstd = self.sb("rstd", [P, NT])
        self.ident = self.sb("ident", [P, P])
        self.identb = self.sb("identb", [P, P], BF16)
        self.ones = self.sb("ones", [1, P])
        self.oneb = self.sb("oneb", [P, P], BF16)
        self.hmask = self.sb("hmask", [P, H])
        self.ctxT = self.sb("ctxT", [P, B * CTX])
        self.gate = self.sb("gate", [P, 8])
        self.padded = []
        self.squares = self.sem("squares")
        self.psum = ctx.enter_context(nc.psum_tensor("psum", [P, 8, 512], F32))

    def sb(self, name, shape, dt=F32):
        return self.ctx.enter_context(self.nc.sbuf_tensor(name, shape, dt))

    def sem(self, name):
        return self.ctx.enter_context(self.nc.semaphore(name))


def setup(core, io, loads):
    nc = core.nc
    with ExitStack() as scope:
        ctx_rows = scope.enter_context(nc.sbuf_tensor("ctx_rows", [KC, 2 * B, D], F32))
        parts = scope.enter_context(nc.sbuf_tensor("setup_parts", [P, NT, 6], F32))
        x_in = [core.sem(f"x_in{b}") for b in range(B)]
        ctx_in, gate_in = core.sem("ctx_in"), core.sem("gate_in")
        consts, ident_made = core.sem("consts"), core.sem("ident_made")
        ctx_ps, ctx_made = core.sem("ctx_ps"), core.sem("ctx_made")
        parts_made = core.sem("parts_made")
        zeroed = core.sem("zeroed")
        with nc.Block() as block:

            @block.sync
            def _(sp):
                sp.dma_start(ctx_rows[:], io["ctx"].rearrange("b (c p) d -> p (b c) d", p=KC)).then_inc(ctx_in, 16)
                xv = io["x"].rearrange("b (t p) d -> p (b t) d", p=P)
                for b in range(B):
                    sp.dma_start(core.resid[:, 4 * b:4 * b + 4, :], xv[:, 4 * b:4 * b + 4, :]).then_inc(x_in[b], 16)
                sp.dma_start(core.gate[:, 0:4], io["g_xattn"].partition_broadcast(P)).then_inc(gate_in, 16)
                sp.dma_start(core.gate[:, 4:8], io["g_ffn"].partition_broadcast(P)).then_inc(gate_in, 16)
                sp.wait_ge(zeroed, len(core.padded))
                for dst, src, sem, _ in loads:
                    sp.dma_start(dst, src).then_inc(sem, 16)

            @block.gpsimd
            def _(pool):
                for small in core.padded:
                    nc.gpsimd.memset(small[:], 0.0).then_inc(zeroed, 1)
                nc.gpsimd.memset(core.ident[:], 0.0).then_inc(consts, 1)
                nc.gpsimd.memset(core.ones[:], 1.0).then_inc(consts, 1)
                nc.gpsimd.memset(core.oneb[:], 1.0).then_inc(consts, 1)
                nc.gpsimd.memset(core.hmask[:], 1.0).then_inc(consts, 1)
                pool.wait_ge(consts, 4)
                nc.gpsimd.affine_select(out=core.ident[:], in_=core.ident[:], compare_op=ALU.not_equal,
                                        fill=1.0, base=0, pattern=[[-1, P]], channel_multiplier=1).then_inc(consts, 1)
                nc.gpsimd.affine_select(out=core.hmask[:], in_=core.hmask[:], compare_op=ALU.is_ge,
                                        fill=0.0, base=0, pattern=[[-8, H]], channel_multiplier=1).then_inc(consts, 1)
                pool.wait_ge(consts, 6)
                nc.gpsimd.affine_select(out=core.hmask[:], in_=core.hmask[:], compare_op=ALU.is_ge,
                                        fill=0.0, base=7, pattern=[[8, H]], channel_multiplier=-1).then_inc(consts, 1)
                nc.gpsimd.tensor_copy(core.identb[:], core.ident[:]).then_inc(ident_made, 1)

            @block.tensor
            def _(pe):
                pe.wait_ge(ctx_in, 16)
                pe.wait_ge(ident_made, 1)
                for k in range(2 * B):
                    last = nc.tensor.transpose(core.psum[:, k // 4, (k % 4) * KC:(k % 4 + 1) * KC],
                                               ctx_rows[:, k, :], core.ident[0:KC, 0:KC])
                last.then_inc(ctx_ps, 1)

            @block.scalar
            def _(act):
                act.wait_ge(gate_in, 32)
                nc.scalar.activation(core.gate[:], core.gate[:], ACT.Tanh)
                act.wait_ge(ctx_ps, 1)
                for k in range(2):
                    nc.scalar.activation(core.ctxT[:, k * 4 * KC:(k + 1) * 4 * KC],
                                         core.psum[:, k, 0:4 * KC], ACT.Copy).then_inc(ctx_made, 1)

            @block.vector
            def _(dve):
                for n in range(NT):
                    if n % 4 == 0:
                        dve.wait_ge(x_in[n // 4], 16)
                    nc.vector.bn_stats(parts[:, n, :], core.resid[:, n, :]).then_inc(parts_made, 1)
                for n in range(NT):
                    dve.wait_ge(parts_made, n + 1)
                    last = nc.vector.bn_aggr(core.stat[:, n, :], parts[:, n, :])
                last.then_inc(parts_made, 1)


class View:

    def __init__(self, ap):
        self.ap = ap

    def __getitem__(self, key):
        return self.ap[key] if key != slice(None) else self.ap


class Steps:

    def __init__(self, eng, sem, per_trip, trip):
        self.eng, self.sem, self.per, self.trip, self.n = eng, sem, per_trip, trip, 0

    def step(self, ins):
        self.n += 1
        ins.then_inc(self.sem, 1)
        return self.n

    def done(self, n=None):
        self.eng.wait_ge(self.sem, at(self.trip, self.per, self.n if n is None else n))

    def close(self):
        assert self.n == self.per, f"{self.n} steps a trip, not {self.per}"


def rows_rstd(core, name, dve_sem, act_sem, rms=False):
    nc = core.nc

    def vector(dve):
        if rms:
            nc.vector.tensor_tensor(core.rstd[:], core.stat[:, :, 0], core.stat[:, :, 0], ALU.mult).then_inc(core.squares, 1)
            dve.wait_ge(core.squares, 1)
            nc.vector.scalar_tensor_tensor(out=core.std[:], in0=core.rstd[:], scalar=LN_EPS, in1=core.stat[:, :, 1],
                                           op0=ALU.add, op1=ALU.add).then_inc(dve_sem, 1)
        else:
            nc.vector.tensor_scalar(core.std[:], core.stat[:, :, 1], LN_EPS, None, ALU.add).then_inc(dve_sem, 1)
        dve.wait_ge(act_sem, 1)
        nc.vector.reciprocal(core.rstd[:], core.std[:]).then_inc(dve_sem, 1)
        dve.wait_ge(dve_sem, 2)

    def scalar(act):
        act.wait_ge(dve_sem, 1)
        nc.scalar.activation(core.std[:], core.std[:], ACT.Sqrt).then_inc(act_sem, 1)

    return vector, scalar


def cross_attention(core, L, w, gate, stride, kind, loaded, n_loads, late_loads=()):
    nc = core.nc
    rope, masked, renorm = kind == "rope", kind == "mask", kind == "norm"
    dk = 8 if stride == 32 else 64
    G = P // stride
    NG = H // G
    E = H * dk
    dva = dk + 1
    HPU = 4 if stride == 32 else 1
    NU = H // HPU
    UPU = 2 * HPU
    LAG = 1 if stride == 32 else 2
    RING = (LAG + 1) * UPU
    OC = E // P
    scale = 128.0 ** -0.5 if kind == "plain" else float(dk) ** -0.5
    half = NG // 2
    NR = 2 * NG
    VH = max(1, E // 512)
    psum = core.psum
    s = {n: nc.alloc_semaphore(f"{L}_{n}") for n in (
        "prep", "var", "sd", "vec", "xn", "xt_ps", "ctxb", "proj", "freed", "sc", "mx", "mp",
        "mt_ps", "mt", "s2", "pt", "pv", "pvx", "on", "ot_ps", "ot", "out", "added", "rms_v", "rms_s", "rms_a", "kt")}

    with ExitStack() as scope:
        def sb(name, shape, dt=F32):
            return scope.enter_context(nc.sbuf_tensor(f"{L}_{name}", shape, dt))

        xn = sb("xn", [P, QT, D])
        xnT = sb("xnT", [P, SEQ])
        ctxb = sb("ctxb", [P, CTX])
        qT = sb("qT", [P, NG, SEQ])
        kT = sb("kT", [P, NG, CTX])
        va = sb("va", [KC, 2, H, dva])
        negmax = sb("negmax", [P, QT, H])
        rest = sb("rest", [P, QT, H])
        mparts = sb("mparts", [P, QT, H, stride], BF16)
        mT = sb("mT", [P, NG, SEQ], BF16)
        pT = sb("pT", [KC, RING, SEQ])
        rsum = sb("rsum", [P, QT, H])
        on = sb("on", [P, QT, E])
        oT = sb("oT", [P, OC, SEQ])
        parts = sb("parts", [P, QT, 6])
        mv = sb("mv", [P, QT, 2])
        new = sb("new", [P, QT, D])
        pool_done = sb("pool_done", [1, 1])
        if rope:
            qs = sb("qs", [P, QT * H, dk])
            ks = sb("ks", [KC, 2 * H, dk])
            tmp = sb("tmp", [P, QT * H, dk])
            tmpb = sb("tmpb", [P, QT * H, dk])
            ss = sb("ss", [P, QT * H])
            qp = sb("qp", [P, QT, H, stride])
            kp = sb("kp", [KC, 2, H, stride])
        else:
            wq, wk = w["wq"], w["wk"]
        if stride == 32 and not rope:
            wqp = sb("wqp", [P, H, stride])
            wkp = sb("wkp", [P, H, stride])
            wq = wqp[:].rearrange("p h s -> p (h s)")
            wk = wkp[:].rearrange("p h s -> p (h s)")
        wv = w["wv"]
        if kind == "plain":
            wvf = sb("wvf", [P, H, dk])
            wv = wvf[:].rearrange("p h s -> p (h s)")
        if masked:
            m_f = sb("m_f", [P, B * CTX])
            pen = sb("pen", [P, B * CTX])
            pen2 = sb("pen2", [P, B * CTX])
            penb = sb("penb", [P, 3, B * CTX], BF16)
            krow = sb("krow", [P, B * CTX], BF16)
            krowb = sb("krowb", [P, CTX], BF16)
        if renorm:
            y = sb("y", [P, QT, D])
            sdv = sb("sdv", [P, QT])
        stats_v, stats_s = rows_rstd(core, L, s["var"], s["sd"])

        units = [("x", 0)]
        if rope:
            units += [("q", 0), ("k", 0)] + [("v", (c, 0)) for c in range(2)]
            units += [("qt", g) for g in range(NG)] + [("kt", g) for g in range(NG)]
        else:
            units += [("q", g) for g in range(NG)] + [("k", g) for g in range(NG)]
            units += [("v", (c, h)) for c in range(2) for h in range(VH)]
        NUNIT = len(units)
        bank = {u: n % 4 for n, u in enumerate(units)}
        DVE_STEPS = {"rope": 41, "mask": 22, "plain": 21, "norm": 49}[kind]

        with nc.Block() as block:

            @block.sync
            def _(sp):
                for dst, src, sem, _ in late_loads:
                    sp.dma_start(dst, src).then_inc(sem, 16)

            @block.gpsimd
            def _(pool):
                prep = []
                prep.append(nc.gpsimd.memset(mparts[:], 0.0))
                prep.append(nc.gpsimd.memset(va[:], 1.0))
                if rope:
                    prep.append(nc.gpsimd.memset(qp[:], 0.0))
                    prep.append(nc.gpsimd.memset(kp[:], 0.0))
                if stride == 32 and not rope:
                    prep.append(nc.gpsimd.memset(wqp[:], 0.0))
                    prep.append(nc.gpsimd.memset(wkp[:], 0.0))
                for ins in prep:
                    ins.then_inc(s["prep"], 1)
                n = len(prep)
                pool.wait_ge(s["prep"], n)
                pool.wait_ge(loaded, 16 * n_loads)
                if masked:
                    nc.gpsimd.memset(mparts[:, :, :, 3:6], 1.0).then_inc(s["prep"], 1)
                    n += 1
                if kind == "mask":
                    for dst, src in ((wqp, w["wq"]), (wkp, w["wk"])):
                        nc.gpsimd.tensor_copy(dst[:, :, 0:dk], src[:].rearrange("p (h d) -> p h d", d=dk)).then_inc(s["prep"], 1)
                        n += 1
                if kind == "plain":
                    hm = core.hmask[:].unsqueeze(2).to_broadcast([P, H, dk])
                    for dst, src in ((wqp, w["wq"]), (wkp, w["wk"]), (wvf, w["wv"])):
                        nc.gpsimd.tensor_tensor(dst[:, :, 0:dk], src[:].unsqueeze(1).to_broadcast([P, H, dk]), hm,
                                                ALU.mult).then_inc(s["prep"], 1)
                        n += 1
                pool.wait_ge(s["prep"], n)
                nc.gpsimd.memset(pool_done[:], 0.0).then_inc(s["kt"], 1)

            @block.tensor
            def _(pe):
                pe.wait_ge(s["kt"], 1)
                with pe.Fori(0, B) as b:
                    def free(name, arg):
                        n = units.index((name, arg))
                        if n >= 4:
                            pe.wait_ge(s["freed"], at(b, NUNIT, n - 3))
                        return psum[:, n % 4, :]

                    pe.wait_ge(s["xn"], at(b, 1, 1))
                    for t in range(QT):
                        last = nc.tensor.transpose(psum[:, 0, t * P:(t + 1) * P], xn[:, t, :], core.ident[:])
                    last.then_inc(s["proj"], 1)
                    pe.wait_ge(s["ctxb"], at(b, 1, 1))
                    pe.wait_ge(s["freed"], at(b, NUNIT, 1))
                    for what, a in units[1:]:
                        out = free(what, a)
                        if what == "q" and rope:
                            for t in range(QT):
                                last = nc.tensor.matmul(out[:, t * P:(t + 1) * P], xnT[:, t * P:(t + 1) * P], w["wq"][:],
                                                        start=True, stop=True)
                        elif what == "q":
                            last = nc.tensor.matmul(out, wq[:, a * P:(a + 1) * P], xnT[:], start=True, stop=True)
                        elif what == "k" and rope:
                            for c in range(2):
                                last = nc.tensor.matmul(out[0:KC, c * P:(c + 1) * P], ctxb[:, c * KC:(c + 1) * KC],
                                                        w["wk"][:], start=True, stop=True)
                        elif what == "k":
                            last = nc.tensor.matmul(out[:, 0:CTX], wk[:, a * P:(a + 1) * P], ctxb[:], start=True, stop=True)
                        elif what == "v":
                            c, hh = a
                            n = min(E, 512)
                            last = nc.tensor.matmul(out[0:KC, 0:n], ctxb[:, c * KC:(c + 1) * KC],
                                                    wv[:, hh * 512:hh * 512 + n], start=True, stop=rope)
                            if not rope:
                                last = nc.tensor.matmul(out[0:KC, 0:n], core.ones[0:1, 0:KC],
                                                        w["bv"][0:1, hh * 512:hh * 512 + n], start=False, stop=True)
                        elif what == "qt":
                            if a == 0:
                                pe.wait_ge(s["rms_v"], at(b, 2, 1))
                            for t in range(QT):
                                last = nc.tensor.transpose(out[:, t * P:(t + 1) * P],
                                                           qp[:, t, a * G:(a + 1) * G, :].rearrange("p h s -> p (h s)"), core.ident[:])
                        elif what == "kt":
                            if a == 0:
                                pe.wait_ge(s["rms_v"], at(b, 2, 2))
                            for c in range(2):
                                last = nc.tensor.transpose(out[:, c * KC:(c + 1) * KC],
                                                           kp[:, c, a * G:(a + 1) * G, :].rearrange("p h s -> p (h s)"),
                                                           core.ident[0:KC, 0:KC])
                        last.then_inc(s["proj"], 1)
                    pe.wait_ge(s["freed"], at(b, NUNIT, NUNIT))
                    if masked:
                        pe.wait_ge(s["rms_v"], at(b, NG, NG))

                    def score_round(g, pair):
                        r = 2 * g + pair
                        back = 1 if G == 4 else 2
                        if r >= back:
                            pe.wait_ge(s["mx"], at(b, NR, r - back + 1))
                        for q in range(2):
                            t = 2 * pair + q
                            for j in range(G):
                                rows = slice(stride * j, stride * j + dk)
                                bk = j if G == 4 else 2 * (r % 2) + j
                                last = nc.tensor.matmul(psum[:, bk, q * CTX:(q + 1) * CTX], qT[rows, g, t * P:(t + 1) * P],
                                                        kT[rows, g, :], start=True, stop=not masked)
                                if masked:
                                    rows = slice(stride * j, stride * j + stride)
                                    last = nc.tensor.matmul(psum[:, bk, q * CTX:(q + 1) * CTX], w["sel"][rows, :],
                                                            krowb[rows, :], start=False, stop=True)
                        last.then_inc(s["sc"], 1)

                    def max_rows(hf):
                        pe.wait_ge(s["mp"], at(b, 2, hf + 1))
                        for k in range(half // 2):
                            if hf or k:
                                pe.wait_ge(s["mt"], at(b, NG // 2, hf * (half // 2) + k))
                            bb = psum[:, 7, :].bitcast(BF16)
                            for gg in range(2):
                                g = hf * half + 2 * k + gg
                                for t in range(QT):
                                    last = nc.tensor.transpose(bb[:, (gg * QT + t) * P:(gg * QT + t + 1) * P],
                                                               mparts[:, t, g * G:(g + 1) * G, :].rearrange("p h s -> p (h s)"),
                                                               core.identb[:])
                            last.then_inc(s["mt_ps"], 1)

                    def scoresT(u):
                        for k in range(UPU):
                            n = u * UPU + k
                            h, c = u * HPU + k % HPU, k // HPU
                            g, j = h // G, h % G
                            if n >= 3:
                                pe.wait_ge(s["pt"], at(b, 2 * H, n - 2))
                            rows = slice(stride * j, stride * j + dk)
                            full = slice(stride * j, stride * j + stride)
                            out = psum[0:KC, 4 + n % 3, :]
                            one = krowb[full, c * KC:(c + 1) * KC] if masked else core.oneb[full, 0:KC]
                            nc.tensor.matmul(out, kT[rows, g, c * KC:(c + 1) * KC], qT[rows, g, :], start=True, stop=False)
                            nc.tensor.matmul(out, one, mT[full, g, :], start=False, stop=True).then_inc(s["s2"], 1)

                    def values(u):
                        pe.wait_ge(s["pt"], at(b, 2 * H, (u + 1) * UPU))
                        if u:
                            pe.wait_ge(s["pvx"], at(b, NU, u))
                        for k in range(HPU):
                            h = u * HPU + k
                            for t in range(QT):
                                o = (t * HPU + k) * dva
                                for c in range(2):
                                    slot = (u * UPU + c * HPU + k) % RING
                                    last = nc.tensor.matmul(psum[:, 7, o:o + dva], pT[:, slot, t * P:(t + 1) * P],
                                                            va[:, c, h, :], start=(c == 0), stop=(c == 1))
                        last.then_inc(s["pv"], 1)

                    for g in range(NG):
                        score_round(g, 0)
                        score_round(g, 1)
                    max_rows(0)
                    max_rows(1)
                    pe.wait_ge(s["mt"], at(b, NG // 2, NG // 2))
                    for u in range(NU + LAG):
                        if u < NU:
                            scoresT(u)
                        if u >= LAG:
                            values(u - LAG)
                    pe.wait_ge(s["pvx"], at(b, NU, NU))
                    for c in range(OC):
                        if c >= 4:
                            pe.wait_ge(s["ot"], at(b, OC, c - 3))
                        for t in range(QT):
                            last = nc.tensor.transpose(psum[:, c % 4, t * P:(t + 1) * P], on[:, t, c * P:(c + 1) * P], core.ident[:])
                        last.then_inc(s["ot_ps"], 1)
                    pe.wait_ge(s["ot"], at(b, OC, OC))
                    for t in range(QT):
                        for c in range(OC):
                            last = nc.tensor.matmul(psum[:, 7, t * P:(t + 1) * P], oT[:, c, t * P:(t + 1) * P],
                                                    w["wo"][:, c * P:(c + 1) * P], start=(c == 0), stop=(rope and c == OC - 1))
                        if not rope:
                            last = nc.tensor.matmul(psum[:, 7, t * P:(t + 1) * P], core.ones[0:1, :], w["bo"][0:1, :],
                                                    start=False, stop=True)
                    last.then_inc(s["out"], 1)

            @block.scalar
            def _(act):
                stats_s(act)
                with act.Fori(0, B) as b:
                    for n, (what, a) in enumerate(units):
                        src = psum[:, n % 4, :]
                        act.wait_ge(s["proj"], at(b, NUNIT, n + 1))
                        if what == "x":
                            ins = nc.scalar.activation(xnT[:], src, ACT.Copy)
                        elif what == "q" and rope:
                            ins = nc.scalar.activation(qs[:].rearrange("p h d -> p (h d)"), src, ACT.Copy)
                        elif what == "q":
                            ins = nc.scalar.activation(qT[:, a, :], src, ACT.Identity, bias=w["bq"][:, a:a + 1])
                        elif what == "k" and rope:
                            ins = nc.scalar.activation(ks[:].rearrange("p h d -> p (h d)"), src[0:KC, 0:2 * P], ACT.Copy)
                        elif what == "k":
                            ins = nc.scalar.activation(kT[:, a, :], src[:, 0:CTX], ACT.Identity, bias=w["bk"][:, a:a + 1])
                        elif what == "v":
                            c, hh = a
                            nh = min(E, 512) // dk
                            ins = nc.scalar.activation(va[:, c, hh * nh:(hh + 1) * nh, 0:dk],
                                                       src[0:KC, 0:nh * dk].rearrange("p (h d) -> p h d", d=dk), ACT.Copy)
                        elif what == "qt":
                            ins = nc.scalar.activation(qT[:, a, :], src, ACT.Copy)
                        elif what == "kt":
                            ins = nc.scalar.activation(kT[:, a, :], src[:, 0:CTX], ACT.Copy)
                        ins.then_inc(s["freed"], 1)
                        if rope and what in ("q", "k"):
                            act.wait_ge(s["rms_s"], at(b, 2, 1 if what == "q" else 2))
                            rows = P if what == "q" else KC
                            cols = QT * H if what == "q" else 2 * H
                            nc.scalar.activation(ss[0:rows, 0:cols], ss[0:rows, 0:cols], ACT.Sqrt).then_inc(s["rms_a"], 1)
                    for n in range(2 * H):
                        u = n // UPU
                        act.wait_ge(s["s2"], at(b, 2 * H, n + 1))
                        if n % UPU == 0 and u > LAG:
                            act.wait_ge(s["pv"], at(b, NU, u - LAG))
                        nc.scalar.activation(pT[:, n % RING, :], psum[0:KC, 4 + n % 3, :], ACT.Exp, scale=scale).then_inc(s["pt"], 1)
                    for c in range(OC):
                        act.wait_ge(s["ot_ps"], at(b, OC, c + 1))
                        nc.scalar.activation(oT[:, c, :], psum[:, c % 4, :], ACT.Copy).then_inc(s["ot"], 1)
                    if renorm:
                        act.wait_ge(s["rms_s"], at(b, 1, 1))
                        nc.scalar.activation(sdv[:], sdv[:], ACT.Sqrt).then_inc(s["rms_a"], 1)

            @block.vector
            def _(dve):
                stats_v(dve)
                dve.wait_ge(loaded, 16 * n_loads)
                if masked:
                    V0 = s["added"]
                    MASK_FILL = -1e8 / scale
                    nc.vector.tensor_copy(m_f[:], w["mask"][:]).then_inc(V0, 1)
                    dve.wait_ge(V0, 1)
                    nc.vector.tensor_scalar(pen[:], m_f[:], 1.0, -MASK_FILL, ALU.subtract, ALU.mult).then_inc(V0, 1)
                    dve.wait_ge(V0, 2)
                    nc.vector.tensor_copy(penb[:, 0, :], pen[:]).then_inc(V0, 1)
                    dve.wait_ge(V0, 3)
                    nc.vector.tensor_tensor(pen2[:], pen[:], penb[:, 0, :], ALU.subtract).then_inc(V0, 1)
                    dve.wait_ge(V0, 4)
                    nc.vector.tensor_copy(penb[:, 1, :], pen2[:]).then_inc(V0, 1)
                    dve.wait_ge(V0, 5)
                    nc.vector.tensor_tensor(penb[:, 2, :], pen2[:], penb[:, 1, :], ALU.subtract).then_inc(V0, 1)
                    dve.wait_ge(V0, 6)
                    nc.vector.tensor_scalar(pen[:], penb[:, 0, :], w["rows"][:, 1:2], w["rows"][:, 0:1], ALU.mult, ALU.add).then_inc(V0, 1)
                    for r in range(1, 3):
                        dve.wait_ge(V0, 6 + r)
                        nc.vector.scalar_tensor_tensor(out=(pen, pen2, krow)[r][:], in0=penb[:, r, :], scalar=w["rows"][:, r + 1:r + 2],
                                                       in1=(None, pen, pen2)[r][:], op0=ALU.mult, op1=ALU.add).then_inc(V0, 1)
                    dve.wait_ge(V0, 9)
                    nc.vector.tensor_scalar(w["sel"][:], core.oneb[:], w["rows"][:, 4:5], None, ALU.mult).then_inc(V0, 1)
                    dve.wait_ge(V0, 10)
                with dve.Fori(0, B) as b:
                    v = Steps(dve, s["vec"], DVE_STEPS, b)

                    for t in range(QT):
                        n = b * QT + t
                        ins = nc.vector.tensor_scalar(xn[:, t, :], core.resid[:, bass.ds(n, 1), :].rearrange("p a d -> p (a d)"),
                                                      core.stat[:, bass.ds(n, 1), 0:1].rearrange("p a d -> p (a d)"),
                                                      core.rstd[:, bass.ds(n, 1)], ALU.subtract, ALU.mult)
                    ins.then_inc(s["xn"], 1)
                    nc.vector.tensor_copy(ctxb[:], core.ctxT[:, bass.ds(b * CTX, CTX)]).then_inc(s["ctxb"], 1)
                    if masked:
                        v.step(nc.vector.tensor_copy(krowb[:], krow[:, bass.ds(b * CTX, CTX)]))
                        v.done()
                        for g in range(NG):
                            dve.wait_ge(s["freed"], at(b, NUNIT, units.index(("k", g)) + 1))
                            nc.vector.tensor_tensor(kT[:, g, :], kT[:, g, :], m_f[:, bass.ds(b * CTX, CTX)], ALU.mult).then_inc(s["rms_v"], 1)
                    if rope:
                        for k, (x, rows, nt, xp, cs, sn, wn, unit) in enumerate((
                                (qs, P, QT, qp, w["qcos"], w["qsin"], w["qn"], 1), (ks, KC, 2, kp, w["kcos"], w["ksin"], w["kn"], 2))):
                            nh = nt * H
                            dve.wait_ge(s["freed"], at(b, NUNIT, unit + 1))
                            full = [rows, nh, dk]
                            v.step(nc.vector.tensor_tensor(tmp[0:rows, 0:nh, :], x[:], x[:], ALU.mult))
                            v.done()
                            v.step(nc.vector.tensor_reduce(ss[0:rows, 0:nh], tmp[0:rows, 0:nh, :], X_AXIS, ALU.add))
                            v.done()
                            nc.vector.tensor_scalar(ss[0:rows, 0:nh], ss[0:rows, 0:nh], 1.0 / dk, 1e-6, ALU.mult, ALU.add).then_inc(s["rms_s"], 1)
                            dve.wait_ge(s["rms_a"], at(b, 2, k + 1))
                            v.step(nc.vector.reciprocal(ss[0:rows, 0:nh], ss[0:rows, 0:nh]))
                            v.done()
                            v.step(nc.vector.tensor_tensor(tmp[0:rows, 0:nh, :], x[:], ss[0:rows, 0:nh].unsqueeze(2).to_broadcast(full), ALU.mult))
                            v.done()
                            v.step(nc.vector.tensor_tensor(x[:], tmp[0:rows, 0:nh, :], wn[0:rows, :].unsqueeze(1).to_broadcast(full), ALU.mult))
                            v.done()
                            xv = x[:].rearrange("p (t h) d -> p t h d", h=H)
                            av = tmp[0:rows, 0:nh, :].rearrange("p (t h) d -> p t h d", h=H)
                            bv = tmpb[0:rows, 0:nh, :].rearrange("p (t h) d -> p t h d", h=H)
                            shape = [rows, nt, H, dk // 2]
                            cb = cs[0:rows, :, :].unsqueeze(2).to_broadcast(shape)
                            sbn = sn[0:rows, :, :].unsqueeze(2).to_broadcast(shape)
                            lo, hi = slice(0, dk // 2), slice(dk // 2, dk)
                            v.step(nc.vector.tensor_tensor(av[:, :, :, lo], xv[:, :, :, lo], cb, ALU.mult))
                            v.step(nc.vector.tensor_tensor(av[:, :, :, hi], xv[:, :, :, hi], cb, ALU.mult))
                            v.step(nc.vector.tensor_tensor(bv[:, :, :, lo], xv[:, :, :, hi], sbn, ALU.mult))
                            v.step(nc.vector.tensor_tensor(bv[:, :, :, hi], xv[:, :, :, lo], sbn, ALU.mult))
                            v.done()
                            xpv = xp[0:rows, 0:nt, :, :]
                            v.step(nc.vector.tensor_tensor(xpv[:, :, :, lo], av[:, :, :, lo], bv[:, :, :, lo], ALU.subtract))
                            v.done()
                            nc.vector.tensor_tensor(xpv[:, :, :, hi], av[:, :, :, hi], bv[:, :, :, hi], ALU.add).then_inc(s["rms_v"], 1)
                            dve.wait_ge(s["rms_v"], at(b, 2, k + 1))

                    for g in range(NG):
                        for pair in range(2):
                            r = 2 * g + pair
                            dve.wait_ge(s["sc"], at(b, NR, r + 1))
                            bk = slice(0, 4) if G == 4 else slice(2 * (r % 2), 2 * (r % 2) + 2)
                            nc.vector.tensor_reduce(
                                negmax[:, 2 * pair:2 * pair + 2, g * G:(g + 1) * G].rearrange("p t h -> p h t"),
                                psum[:, bk, 0:2 * CTX].rearrange("p k (t c) -> p k t c", c=CTX),
                                X_AXIS, ALU.max, negate=True).then_inc(s["mx"], 1)
                        if g % half == half - 1:
                            hf = g // half
                            hs = slice(hf * half * G, (hf + 1) * half * G)
                            dve.wait_ge(s["mx"], at(b, NR, 2 * g + 2))
                            mpv = mparts[:, :, hs, :]
                            v.step(nc.vector.tensor_copy(mpv[:, :, :, 0], negmax[:, :, hs]))
                            v.done()
                            v.step(nc.vector.tensor_tensor(rest[:, :, hs], negmax[:, :, hs], mpv[:, :, :, 0], ALU.subtract))
                            v.done()
                            v.step(nc.vector.tensor_copy(mpv[:, :, :, 1], rest[:, :, hs]))
                            v.done()
                            nc.vector.tensor_tensor(mpv[:, :, :, 2], rest[:, :, hs], mpv[:, :, :, 1], ALU.subtract).then_inc(s["mp"], 1)
                    for k in range(NG // 2):
                        dve.wait_ge(s["mt_ps"], at(b, NG // 2, k + 1))
                        nc.vector.tensor_copy(mT[:, 2 * k:2 * k + 2, :].rearrange("p g q -> p (g q)"),
                                              psum[:, 7, :].bitcast(BF16)).then_inc(s["mt"], 1)
                    for u in range(NU):
                        dve.wait_ge(s["pv"], at(b, NU, u + 1))
                        pv = psum[:, 7, 0:QT * HPU * dva].rearrange("p (t h e) -> p t h e", h=HPU, e=dva)
                        hs = slice(u * HPU, (u + 1) * HPU)
                        v.step(nc.vector.reciprocal(rsum[:, :, hs], pv[:, :, :, dk]))
                        v.done()
                        nc.vector.tensor_tensor(on[:, :, u * HPU * dk:(u + 1) * HPU * dk].rearrange("p t (h e) -> p t h e", e=dk),
                                                pv[:, :, :, 0:dk], rsum[:, :, hs].unsqueeze(3).to_broadcast([P, QT, HPU, dk]),
                                                ALU.mult).then_inc(s["pvx"], 1)
                    dve.wait_ge(s["out"], at(b, 1, 1))
                    if renorm:
                        v.step(nc.vector.tensor_tensor(y[:], psum[:, 7, :].rearrange("p (t d) -> p t d", d=D), xn[:], ALU.add))
                        v.done()
                        for t in range(QT):
                            v.step(nc.vector.bn_stats(parts[:, t, :], y[:, t, :]))
                        v.done()
                        nc.vector.memset(rsum[:, 0, 0:1], 0.0)
                        for t in range(QT):
                            v.step(nc.vector.bn_aggr(mv[:, t, :], parts[:, t, :]))
                        v.done()
                        nc.vector.tensor_scalar(sdv[:], mv[:, :, 1], LN_EPS, None, ALU.add).then_inc(s["rms_s"], 1)
                        dve.wait_ge(s["rms_a"], at(b, 1, 1))
                        v.step(nc.vector.reciprocal(sdv[:], sdv[:]))
                        v.done()
                        for t in range(QT):
                            v.step(nc.vector.tensor_scalar(y[:, t, :], y[:, t, :], mv[:, t, 0:1], sdv[:, t:t + 1], ALU.subtract, ALU.mult))
                        v.done()
                        v.step(nc.vector.tensor_tensor(y[:], y[:], w["gamma"][:].unsqueeze(1).to_broadcast([P, QT, D]), ALU.mult))
                        v.done()
                        v.step(nc.vector.tensor_tensor(y[:], y[:], w["beta"][:].unsqueeze(1).to_broadcast([P, QT, D]), ALU.add))
                        v.done()
                        src = y[:].rearrange("p t d -> p (t d)")
                    else:
                        src = psum[:, 7, :]
                    update_rows(core, v, b, src, gate, new, parts, mv)
                    v.close()


def update_rows(core, v, b, src, gate, new, parts, mv, base=None, dest=None):
    nc = core.nc
    rb = (dest or core.resid)[:, bass.ds(b * QT, QT), :].rearrange("p t d -> p (t d)")
    nw = new[:].rearrange("p t d -> p (t d)")
    v.step(nc.vector.scalar_tensor_tensor(out=nw, in0=src, scalar=1.0 if gate is None else core.gate[:, gate:gate + 1],
                                          in1=rb if base is None else base,
                                          op0=ALU.mult, op1=ALU.add))
    v.done()
    for t in range(QT):
        v.step(nc.vector.bn_stats(parts[:, t, :], new[:, t, :]))
    v.done()
    v.step(nc.vector.tensor_scalar(rb, nw, 1.0, None, ALU.mult))
    for t in range(QT):
        v.step(nc.vector.bn_aggr(mv[:, t, :], parts[:, t, :]))
    v.done()
    v.step(nc.vector.tensor_scalar(core.stat[:, bass.ds(b * QT, QT), :], mv[:], 1.0, None, ALU.mult))
    v.done()


NK = 5
KP = NK * 32
KH = KP // 2
PART = 32
PAD_PENALTY = -1e30


def narrow_attention(core, L, w, gate, kind, loaded, n_loads):
    nc, psum = core.nc, core.psum
    rope, masked = kind == "rope", kind == "mask"
    DK, G, NG = 8, 4, 4
    DVA = DK + 1
    scale = 128.0 ** -0.5 if kind == "plain" else float(DK) ** -0.5
    RING = 2 * NK
    NX = NG * NK
    s = {n: nc.alloc_semaphore(f"{L}_{n}") for n in (
        "prep", "prepd", "var", "sd", "vec", "xn", "ctxr", "xt_ps", "xt", "q_ps", "k_ps", "v_ps", "q_raw", "k_raw", "rms_v", "rms_s",
        "q_f", "k_f", "q_hi", "k_hi", "q_rest", "k_rest", "q_mid", "k_mid", "q_lo", "k_lo", "q_dup", "k_dup", "q_st", "k_st",
        "kt_ps", "kt", "bd_a", "bd_b", "vbd", "qt_ps", "qa", "qb", "sc", "mx", "mp", "rt_ps", "rt", "s2", "pt", "pv", "pvs",
        "o_ps", "o", "ot_ps", "ot", "out")}

    with ExitStack() as scope:
        def sb(name, shape, dt=F32):
            return scope.enter_context(nc.sbuf_tensor(f"{L}_{name}", shape, dt))

        xn = sb("xn", [P, QT, D])
        xnT = sb("xnT", [P, SEQ])
        ctxr = sb("ctxr", [P, NK, G, 32])
        ctxp = sb("ctxp", [P, KP])
        qf = sb("qf", [P, QT * H, DK])
        kf = sb("kf", [KH, 2 * H, DK])
        qr = sb("qr", [P, QT * H, DK])
        kr = sb("kr", [KH, 2 * H, DK])
        qst = sb("qst", [P, 2, QT * H, PART], BF16)
        kst = sb("kst", [KH, 2, 2 * H, PART], BF16)
        qT = sb("qT", [P, 2, NG, SEQ], BF16)
        qmT = sb("qmT", [P, NG, SEQ], BF16)
        kT = sb("kT", [P, 2, NG, KP], BF16)
        bd = sb("bd", [P, 2, NG, NK, G, 32], BF16)
        vbd = sb("vbd", [P, NK * NG, G, DVA])
        quad = sb("quad", [P, G])
        quadb = sb("quadb", [P, G], BF16)
        one = sb("one", [P, 1])
        negmax = sb("negmax", [P, QT, H])
        neglast = sb("neglast", [P, QT, G])
        rest = sb("rest", [P, QT, G])
        pT = sb("pT", [P, RING, SEQ])
        oraw = sb("oraw", [G * DVA, 2, SEQ])
        rsum = sb("rsum", [P, QT, G])
        on = sb("on", [P, QT, D])
        oT = sb("oT", [P, SEQ])
        parts = sb("parts", [P, QT, 6])
        mv = sb("mv", [P, QT, 2])
        new = sb("new", [P, QT, D])
        if rope:
            ss = sb("ss", [P, QT * H])
            ra = sb("ra", [P, QT * H, DK])
            rb = sb("rb", [P, QT * H, DK])
        pen = sb("pen", [KH, B, 2])
        if kind == "plain":
            wq, wk, wv = (sb(f"blk{n}", [P, H, DK]) for n in "qkv")
            wq, wk, wv = (x[:].rearrange("p h d -> p (h d)") for x in (wq, wk, wv))
        else:
            wq, wk, wv = w["wq"][:], w["wk"][:], w["wv"][:]
        if masked:
            m_f = sb("m_f", [KH, B, 2])
            m_b = sb("m_b", [KH, 2])
        pen_r = sb("pen_r", [KH, B, 2])
        pen3 = sb("pen3", [KH, B, 2, 3], BF16)
        stats_v, stats_s = rows_rstd(core, L, s["var"], s["sd"])
        N_PREP = 8 + (3 if kind == "plain" else 0) + 1
        N_PREPD = 9 if masked else 6
        DVE_STEPS = {"rope": 55, "mask": 37, "plain": 35}[kind]

        with nc.Block() as block:

            @block.gpsimd
            def _(pool):
                for x, value in ((qst, 0.0), (kst, 0.0), (vbd, 0.0), (quad, 1.0), (one, 1.0), (ctxr, 0.0), (ctxp, 0.0)):
                    nc.gpsimd.memset(x[:], value).then_inc(s["prep"], 1)
                n = 7
                pool.wait_ge(s["prep"], n)
                nc.gpsimd.memset(qst[:, 0, :, 27:30], 1.0).then_inc(s["prep"], 1)
                nc.gpsimd.memset(kst[:, 0, :, 24:27], 1.0).then_inc(s["prepd"], 1)
                nc.gpsimd.affine_select(out=quad[:], in_=quad[:], compare_op=ALU.is_ge, fill=0.0, base=0,
                                        pattern=[[-32, G]], channel_multiplier=1).then_inc(s["prepd"], 1)
                pool.wait_ge(s["prepd"], 2)
                nc.gpsimd.affine_select(out=quad[:], in_=quad[:], compare_op=ALU.is_ge, fill=0.0, base=31,
                                        pattern=[[32, G]], channel_multiplier=-1).then_inc(s["prepd"], 1)
                if kind == "plain":
                    pool.wait_ge(loaded, 16 * n_loads)
                    hm = core.hmask[:].unsqueeze(2).to_broadcast([P, H, DK])
                    for dst, src in ((wq, w["wq"]), (wk, w["wk"]), (wv, w["wv"])):
                        nc.gpsimd.tensor_tensor(dst.rearrange("p (h d) -> p h d", d=DK), src[:].unsqueeze(1).to_broadcast([P, H, DK]),
                                                hm, ALU.mult).then_inc(s["prep"], 1)
                pool.wait_ge(s["prepd"], 3)
                nc.gpsimd.tensor_copy(quadb[:], quad[:]).then_inc(s["prep"], 1)
                pool.wait_ge(s["prep"], N_PREP)
                with pool.Fori(0, B) as b:
                    def copied(dst, src, sem):
                        rows, n = dst.shape[0], dst.shape[1]
                        nc.gpsimd.tensor_tensor(dst, src, core.oneb[0:rows, 0:1].unsqueeze(2).to_broadcast([rows, n, DK]),
                                                ALU.mult).then_inc(sem, 1)

                    pool.wait_ge(s["k_hi"], at(b, 1, 1))
                    copied(kst[:, 0, :, 16:24], kst[:, 0, :, 0:8], s["k_dup"])
                    copied(kst[:, 1, :, 16:24], kst[:, 0, :, 0:8], s["k_dup"])
                    pool.wait_ge(s["k_mid"], at(b, 1, 1))
                    copied(kst[:, 1, :, 0:8], kst[:, 0, :, 8:16], s["k_dup"])
                    pool.wait_ge(s["q_hi"], at(b, 1, 1))
                    copied(qst[:, 0, :, 8:16], qst[:, 0, :, 0:8], s["q_dup"])
                    copied(qst[:, 1, :, 8:16], qst[:, 0, :, 0:8], s["q_dup"])
                    pool.wait_ge(s["q_mid"], at(b, 1, 1))
                    copied(qst[:, 1, :, 0:8], qst[:, 0, :, 16:24], s["q_dup"])
                    pool.wait_ge(s["kt"], at(b, 2, 2))
                    for g in range(NG):
                        ins = nc.gpsimd.tensor_tensor(bd[:, 1, g], kT[:, 1, g, :].rearrange("p (c k) -> p c k", k=32).unsqueeze(2).to_broadcast([P, NK, G, 32]),
                                                      quadb[:].unsqueeze(1).unsqueeze(3).to_broadcast([P, NK, G, 32]), ALU.mult)
                        ins.then_inc(s["bd_b"], 1)

            @block.tensor
            def _(pe):
                pe.wait_ge(loaded, 16 * n_loads)
                pe.wait_ge(s["prep"], N_PREP)
                with pe.Fori(0, B) as b:
                    pe.wait_ge(s["ctxr"], at(b, 1, 1))
                    for c in range(2):
                        last = nc.tensor.matmul(psum[0:KH, 2, c * D:(c + 1) * D], ctxp[:, c * KH:(c + 1) * KH], wk, start=True, stop=True)
                    last.then_inc(s["k_ps"], 1)
                    for c in range(NK):
                        out = psum[:, 3, c * P:(c + 1) * P] if c < 4 else psum[:, 6, 0:P]
                        last = nc.tensor.matmul(out, ctxr[:, c].rearrange("p j k -> p (j k)"), wv, start=True, stop=rope)
                        if not rope:
                            last = nc.tensor.matmul(out, core.ones[0:1, :], w["bv"][:], start=False, stop=True)
                    last.then_inc(s["v_ps"], 1)
                    pe.wait_ge(s["xn"], at(b, 1, 1))
                    for t in range(QT):
                        last = nc.tensor.transpose(psum[:, 0, t * P:(t + 1) * P], xn[:, t, :], core.ident[:])
                    last.then_inc(s["xt_ps"], 1)
                    pe.wait_ge(s["xt"], at(b, 1, 1))
                    for t in range(QT):
                        last = nc.tensor.matmul(psum[:, 1, t * P:(t + 1) * P], xnT[:, t * P:(t + 1) * P], wq, start=True, stop=True)
                    last.then_inc(s["q_ps"], 1)
                    pe.wait_ge(s["k_dup"], at(b, 3, 3))
                    pe.wait_ge(s["k_lo"], at(b, 1, 1))
                    for x in range(2):
                        bb = psum[:, 4 + x, :].bitcast(BF16)
                        for g in range(NG):
                            for c in range(2):
                                last = nc.tensor.transpose(bb[:, g * KP + c * KH:g * KP + (c + 1) * KH],
                                                           kst[:, x, c * H + g * G:c * H + (g + 1) * G, :].rearrange("p h r -> p (h r)"),
                                                           core.identb[0:KH, 0:KH])
                        last.then_inc(s["kt_ps"], 1)
                    pe.wait_ge(s["q_dup"], at(b, 3, 3))
                    pe.wait_ge(s["q_lo"], at(b, 1, 1))
                    pe.wait_ge(s["vbd"], at(b, 1, 1))
                    for x in range(2):
                        for gg in range(2):
                            bb = psum[:, 2 * x + gg, :].bitcast(BF16)
                            for g in (2 * gg, 2 * gg + 1):
                                for t in range(QT):
                                    last = nc.tensor.transpose(bb[:, ((g % 2) * QT + t) * P:((g % 2) * QT + t + 1) * P],
                                                               qst[:, x, t * H + g * G:t * H + (g + 1) * G, :].rearrange("p h r -> p (h r)"),
                                                               core.identb[:])
                            last.then_inc(s["qt_ps"], 1)
                    pe.wait_ge(s["bd_a"], at(b, 1, 1))
                    pe.wait_ge(s["bd_b"], at(b, NG, NG))
                    pe.wait_ge(s["qa"], at(b, 2, 2))
                    pe.wait_ge(s["qb"], at(b, 2, 2))

                    def keys_of(x, g, c0, c1):
                        return bd[:, x, g, c0:c1].rearrange("p c j k -> p (c j k)")

                    def score_rounds(g):
                        for t in range(QT):
                            r = g * QT + t
                            if r >= 3:
                                pe.wait_ge(s["mx"], at(b, NG * (QT + 1), g * (QT + 1) + t - 2 if t >= 3 else (g - 1) * (QT + 1) + t + 2))
                            rows = slice(t * P, (t + 1) * P)
                            for x in range(2):
                                last = nc.tensor.matmul(psum[:, r % 3, :], qT[:, x, g, rows], keys_of(x, g, 0, 4), start=(x == 0), stop=(x == 1))
                            if t < QT - 1:
                                last.then_inc(s["sc"], 1)
                                continue
                            last.then_inc(s["sc"], 1)
                            if g:
                                pe.wait_ge(s["mx"], at(b, NG * (QT + 1), g * (QT + 1)))
                            for u in range(QT):
                                rows = slice(u * P, (u + 1) * P)
                                for x in range(2):
                                    last = nc.tensor.matmul(psum[:, 3, rows], qT[:, x, g, rows], keys_of(x, g, 4, 5), start=(x == 0), stop=(x == 1))
                            last.then_inc(s["sc"], 1)

                    def max_rows(g):
                        pe.wait_ge(s["mp"], at(b, NG, g + 1))
                        if g:
                            pe.wait_ge(s["rt"], at(b, NG, g))
                        if g >= 3:
                            pe.wait_ge(s["o"], at(b, NG, g - 2))
                        bb = psum[:, 7, :].bitcast(BF16)
                        for t in range(QT):
                            last = nc.tensor.transpose(bb[:, t * P:(t + 1) * P],
                                                       qst[:, 0, t * H + g * G:t * H + (g + 1) * G, :].rearrange("p h r -> p (h r)"), core.identb[:])
                        last.then_inc(s["rt_ps"], 1)

                    def scoresT(g, c):
                        n = g * NK + c
                        if c == 0:
                            pe.wait_ge(s["rt"], at(b, NG, g + 1))
                        if n >= 2:
                            pe.wait_ge(s["pt"], at(b, NX, n - 1))
                        for x in range(2):
                            last = nc.tensor.matmul(psum[:, 4 + n % 2, :], keys_of(x, g, c, c + 1), qmT[:, g, :] if x == 0 else qT[:, 1, g, :],
                                                    start=(x == 0), stop=(x == 1))
                        last.then_inc(s["s2"], 1)

                    def values(g, c):
                        n = g * NK + c
                        pe.wait_ge(s["pt"], at(b, NX, n + 1))
                        if c == 0 and g:
                            pe.wait_ge(s["pvs"], at(b, NG, g))
                        last = nc.tensor.matmul(psum[0:G * DVA, 6, :], vbd[:, c * NG + g].rearrange("p j e -> p (j e)"), pT[:, n % RING, :],
                                                start=(c == 0), stop=(c == NK - 1))
                        if c == NK - 1:
                            last.then_inc(s["pv"], 1)

                    def outputs(g):
                        pe.wait_ge(s["pvs"], at(b, NG, g + 1))
                        pe.wait_ge(s["rt"], at(b, NG, min(g + 3, NG)))
                        if g:
                            pe.wait_ge(s["o"], at(b, NG, g))
                        for t in range(QT):
                            last = nc.tensor.matmul(psum[:, 7, t * G * DVA:(t + 1) * G * DVA], oraw[:, g % 2, t * P:(t + 1) * P],
                                                    core.ident[0:G * DVA, 0:G * DVA], start=True, stop=True)
                        last.then_inc(s["o_ps"], 1)

                    for i in range(NG + 3):
                        if i < NG:
                            score_rounds(i)
                        if 1 <= i <= NG:
                            max_rows(i - 1)
                        if i >= 3:
                            outputs(i - 3)
                        for c in range(NK):
                            if 1 <= i <= NG:
                                scoresT(i - 1, c)
                            if 2 <= i <= NG + 1:
                                values(i - 2, c)
                    pe.wait_ge(s["o"], at(b, NG, NG))
                    for t in range(QT):
                        last = nc.tensor.transpose(psum[:, 7, t * P:(t + 1) * P], on[:, t, :], core.ident[:])
                    last.then_inc(s["ot_ps"], 1)
                    pe.wait_ge(s["ot"], at(b, 1, 1))
                    for t in range(QT):
                        last = nc.tensor.matmul(psum[:, 6, t * P:(t + 1) * P], oT[:, t * P:(t + 1) * P], w["wo"][:], start=True, stop=rope)
                        if not rope:
                            last = nc.tensor.matmul(psum[:, 6, t * P:(t + 1) * P], core.ones[0:1, :], w["bo"][:], start=False, stop=True)
                    last.then_inc(s["out"], 1)

            @block.scalar
            def _(act):
                stats_s(act)
                act.wait_ge(s["prep"], N_PREP)
                with act.Fori(0, B) as b:
                    if rope:
                        act.wait_ge(s["k_ps"], at(b, 1, 1))
                        nc.scalar.activation(kf[:].rearrange("p h d -> p (h d)"), psum[0:KH, 2, 0:2 * D], ACT.Copy).then_inc(s["k_raw"], 1)
                    act.wait_ge(s["xt_ps"], at(b, 1, 1))
                    nc.scalar.activation(xnT[:], psum[:, 0, :], ACT.Copy).then_inc(s["xt"], 1)
                    if rope:
                        act.wait_ge(s["q_ps"], at(b, 1, 1))
                        nc.scalar.activation(qf[:].rearrange("p h d -> p (h d)"), psum[:, 1, :], ACT.Copy).then_inc(s["q_raw"], 1)
                    for k, (f, r, st, hi, mid, fs, hs, rs, ms) in enumerate(((kf, kr, kst, 0, 8, "k_f", "k_hi", "k_rest", "k_mid"),
                                                                          (qf, qr, qst, 0, 16, "q_f", "q_hi", "q_rest", "q_mid"))):
                        if rope:
                            rows, cols = ((KH, 2 * H), (P, QT * H))[k]
                            act.wait_ge(s["rms_s"], at(b, 2, k + 1))
                            nc.scalar.activation(ss[0:rows, 0:cols], ss[0:rows, 0:cols], ACT.Sqrt).then_inc(s["rms_v"], 1)
                        act.wait_ge(s[fs], at(b, 1, 1))
                        nc.scalar.activation(st[:, 0, :, hi:hi + 8], f[:], ACT.Copy).then_inc(s[hs], 1)
                        act.wait_ge(s[rs], at(b, 1, 1))
                        nc.scalar.activation(st[:, 0, :, mid:mid + 8], r[:], ACT.Copy).then_inc(s[ms], 1)
                    for x in range(2):
                        act.wait_ge(s["kt_ps"], at(b, 2, x + 1))
                        nc.scalar.activation(kT[:, x].rearrange("p g k -> p (g k)"), psum[:, 4 + x, :].bitcast(BF16)[:, 0:NG * KP],
                                             ACT.Copy).then_inc(s["kt"], 1)
                    for gg in range(2):
                        act.wait_ge(s["qt_ps"], at(b, 4, gg + 1))
                        nc.scalar.activation(qT[:, 0, 2 * gg:2 * gg + 2, :].rearrange("p g q -> p (g q)"),
                                             psum[:, gg, :].bitcast(BF16), ACT.Copy).then_inc(s["qa"], 1)
                    for i in range(1, NG + 2):
                        if i <= NG:
                            g = i - 1
                            act.wait_ge(s["rt_ps"], at(b, NG, g + 1))
                            nc.scalar.activation(qmT[:, g, :], psum[:, 7, :].bitcast(BF16)[:, 0:SEQ], ACT.Copy).then_inc(s["rt"], 1)
                            for c in range(NK):
                                n = g * NK + c
                                act.wait_ge(s["s2"], at(b, NX, n + 1))
                                if c == 0 and g >= 2:
                                    act.wait_ge(s["pv"], at(b, NG, g - 1))
                                nc.scalar.activation(pT[:, n % RING, :], psum[:, 4 + n % 2, :], ACT.Exp, scale=scale).then_inc(s["pt"], 1)
                        if i >= 2:
                            g = i - 2
                            act.wait_ge(s["pv"], at(b, NG, g + 1))
                            if g >= 2:
                                act.wait_ge(s["o_ps"], at(b, NG, g - 1))
                            nc.scalar.activation(oraw[:, g % 2, :], psum[0:G * DVA, 6, :], ACT.Copy).then_inc(s["pvs"], 1)
                    act.wait_ge(s["ot_ps"], at(b, 1, 1))
                    nc.scalar.activation(oT[:], psum[:, 7, :], ACT.Copy).then_inc(s["ot"], 1)

            @block.vector
            def _(dve):
                stats_v(dve)
                dve.wait_ge(loaded, 16 * n_loads)
                dve.wait_ge(s["prep"], N_PREP)
                c = Steps(dve, s["prepd"], 0, 0)
                c.n = 3
                if masked:
                    c.step(nc.vector.tensor_copy(m_f[:], w["mask"][:].rearrange("k c b -> k b c")))
                    c.done()
                    c.step(nc.vector.tensor_scalar(pen[:], m_f[:], 1.0, 1e8 / scale, ALU.subtract, ALU.mult))
                    c.done()
                    c.step(nc.vector.tensor_tensor(pen[:], pen[:], w["pad"][:].unsqueeze(1).to_broadcast([KH, B, 2]), ALU.add))
                else:
                    c.step(nc.vector.tensor_copy(pen[:], w["pad"][:].unsqueeze(1).to_broadcast([KH, B, 2])))
                c.done()
                c.step(nc.vector.tensor_copy(pen3[:, :, :, 0], pen[:]))
                c.done()
                c.step(nc.vector.tensor_tensor(pen_r[:], pen[:], pen3[:, :, :, 0], ALU.subtract))
                c.done()
                c.step(nc.vector.tensor_copy(pen3[:, :, :, 1], pen_r[:]))
                c.done()
                c.step(nc.vector.tensor_tensor(pen3[:, :, :, 2], pen_r[:], pen3[:, :, :, 1], ALU.subtract))
                c.step(nc.vector.tensor_copy(vbd[:, :, :, DK], quad[:].unsqueeze(1).to_broadcast([P, NK * NG, G])))
                c.done()
                with dve.Fori(0, B) as b:
                    v = Steps(dve, s["vec"], DVE_STEPS, b)
                    cb = core.ctxT[:, bass.ds(b * CTX, CTX)]
                    v.step(nc.vector.tensor_scalar(ctxp[:, 0:CTX], cb, 1.0, None, ALU.mult))
                    v.done()
                    v.step(nc.vector.tensor_scalar(kst[:, 0, :, 27:30].rearrange("p (c h) r -> p c h r", h=H),
                                                   pen3[:, bass.ds(b, 1)].rearrange("p o c r -> p (o c) r").unsqueeze(2).to_broadcast([KH, 2, H, 3]),
                                                   1.0, None, ALU.mult))
                    if masked:
                        v.step(nc.vector.tensor_scalar(m_b[:], m_f[:, bass.ds(b, 1)].rearrange("p o c -> p (o c)"), 1.0, None, ALU.mult))
                    nc.vector.tensor_copy(ctxr[:], ctxp[:].rearrange("p (c k) -> p c k", k=32).unsqueeze(2).to_broadcast([P, NK, G, 32])).then_inc(s["ctxr"], 1)
                    for t in range(QT):
                        n = b * QT + t
                        ins = nc.vector.tensor_scalar(xn[:, t, :], core.resid[:, bass.ds(n, 1), :].rearrange("p a d -> p (a d)"),
                                                      core.stat[:, bass.ds(n, 1), 0:1].rearrange("p a d -> p (a d)"),
                                                      core.rstd[:, bass.ds(n, 1)], ALU.subtract, ALU.mult)
                    ins.then_inc(s["xn"], 1)

                    def rotated(k):
                        x, rows, nt, cs, sn, wn, raw = ((kf, KH, 2, w["kcos"], w["ksin"], w["kn"], "k_raw"),
                                                        (qf, P, QT, w["qcos"], w["qsin"], w["qn"], "q_raw"))[k]
                        nh = nt * H
                        full = [rows, nh, DK]
                        dve.wait_ge(s[raw], at(b, 1, 1))
                        tmp, tmpb = ra[0:rows, 0:nh, :], rb[0:rows, 0:nh, :]
                        v.step(nc.vector.tensor_tensor(tmp, x[:], x[:], ALU.mult))
                        v.done()
                        v.step(nc.vector.tensor_reduce(ss[0:rows, 0:nh], tmp, X_AXIS, ALU.add))
                        v.done()
                        nc.vector.tensor_scalar(ss[0:rows, 0:nh], ss[0:rows, 0:nh], 1.0 / DK, 1e-6, ALU.mult, ALU.add).then_inc(s["rms_s"], 1)
                        dve.wait_ge(s["rms_v"], at(b, 2, k + 1))
                        v.step(nc.vector.reciprocal(ss[0:rows, 0:nh], ss[0:rows, 0:nh]))
                        v.done()
                        v.step(nc.vector.tensor_tensor(tmp, x[:], ss[0:rows, 0:nh].unsqueeze(2).to_broadcast(full), ALU.mult))
                        v.done()
                        v.step(nc.vector.tensor_tensor(x[:], tmp, wn[0:rows, :].unsqueeze(1).to_broadcast(full), ALU.mult))
                        v.done()
                        xv = x[:].rearrange("p (t h) d -> p t h d", h=H)
                        av = tmp.rearrange("p (t h) d -> p t h d", h=H)
                        bv = tmpb.rearrange("p (t h) d -> p t h d", h=H)
                        shape = [rows, nt, H, DK // 2]
                        cb = cs[0:rows, :, :].unsqueeze(2).to_broadcast(shape)
                        sbn = sn[0:rows, :, :].unsqueeze(2).to_broadcast(shape)
                        lo, hi = slice(0, DK // 2), slice(DK // 2, DK)
                        v.step(nc.vector.tensor_tensor(av[:, :, :, lo], xv[:, :, :, lo], cb, ALU.mult))
                        v.step(nc.vector.tensor_tensor(av[:, :, :, hi], xv[:, :, :, hi], cb, ALU.mult))
                        v.step(nc.vector.tensor_tensor(bv[:, :, :, lo], xv[:, :, :, hi], sbn, ALU.mult))
                        v.step(nc.vector.tensor_tensor(bv[:, :, :, hi], xv[:, :, :, lo], sbn, ALU.mult))
                        v.done()
                        v.step(nc.vector.tensor_tensor(xv[:, :, :, lo], av[:, :, :, lo], bv[:, :, :, lo], ALU.subtract))
                        v.done()
                        nc.vector.tensor_tensor(xv[:, :, :, hi], av[:, :, :, hi], bv[:, :, :, hi], ALU.add).then_inc(s["k_f" if k == 0 else "q_f"], 1)
                        dve.wait_ge(s["k_f" if k == 0 else "q_f"], at(b, 1, 1))

                    def split(f, r, st, mid, lo_x, lo, hs, rs, ms, ls):
                        dve.wait_ge(s[hs], at(b, 1, 1))
                        nc.vector.tensor_tensor(r[:], f[:], st[:, 0, :, 0:8], ALU.subtract).then_inc(s[rs], 1)
                        dve.wait_ge(s[ms], at(b, 1, 1))
                        nc.vector.tensor_tensor(st[:, lo_x, :, lo:lo + 8], r[:], st[:, 0, :, mid:mid + 8], ALU.subtract).then_inc(s[ls], 1)

                    if rope:
                        rotated(0)
                    else:
                        dve.wait_ge(s["k_ps"], at(b, 1, 1))
                        kv = kf[:].rearrange("p (c h) d -> p c (h d)", c=2)
                        kp = psum[0:KH, 2, 0:2 * D].rearrange("p (c e) -> p c e", c=2)
                        kb = w["bk"][0:KH, :].unsqueeze(1).to_broadcast([KH, 2, D])
                        if masked:
                            v.step(nc.vector.tensor_tensor(kv, kp, kb, ALU.add))
                            v.done()
                            nc.vector.tensor_tensor(kv, kv, m_b[:].unsqueeze(2).to_broadcast([KH, 2, D]), ALU.mult).then_inc(s["k_f"], 1)
                        else:
                            nc.vector.tensor_tensor(kv, kp, kb, ALU.add).then_inc(s["k_f"], 1)
                    split(kf, kr, kst, 8, 1, 8, "k_hi", "k_rest", "k_mid", "k_lo")
                    if rope:
                        rotated(1)
                    else:
                        dve.wait_ge(s["q_ps"], at(b, 1, 1))
                        nc.vector.tensor_tensor(qf[:].rearrange("p (t h) d -> p t (h d)", h=H), psum[:, 1, :].rearrange("p (t e) -> p t e", e=D),
                                                w["bq"][:].unsqueeze(1).to_broadcast([P, QT, D]), ALU.add).then_inc(s["q_f"], 1)
                    v.step(nc.vector.memset(qst[:, 0, :, 24:27], 0.0))
                    split(qf, qr, qst, 16, 1, 16, "q_hi", "q_rest", "q_mid", "q_lo")
                    dve.wait_ge(s["v_ps"], at(b, 1, 1))
                    v.step(nc.vector.tensor_tensor(vbd[:, 0:4 * NG, :, 0:DK], psum[:, 3, :].rearrange("p (n j d) -> p n j d", j=G, d=DK),
                                                   quad[:].unsqueeze(1).unsqueeze(3).to_broadcast([P, 4 * NG, G, DK]), ALU.mult))
                    v.done()
                    nc.vector.tensor_tensor(vbd[:, 4 * NG:, :, 0:DK], psum[:, 6, 0:P].rearrange("p (n j d) -> p n j d", j=G, d=DK),
                                            quad[:].unsqueeze(1).unsqueeze(3).to_broadcast([P, NG, G, DK]), ALU.mult).then_inc(s["vbd"], 1)
                    dve.wait_ge(s["kt"], at(b, 2, 1))
                    for g in range(NG):
                        ins = nc.vector.tensor_tensor(bd[:, 0, g], kT[:, 0, g, :].rearrange("p (c k) -> p c k", k=32).unsqueeze(2).to_broadcast([P, NK, G, 32]),
                                                      quadb[:].unsqueeze(1).unsqueeze(3).to_broadcast([P, NK, G, 32]), ALU.mult)
                    ins.then_inc(s["bd_a"], 1)
                    for gg in range(2):
                        dve.wait_ge(s["qt_ps"], at(b, 4, 3 + gg))
                        nc.vector.tensor_copy(qT[:, 1, 2 * gg:2 * gg + 2, :].rearrange("p g q -> p (g q)"),
                                              psum[:, 2 + gg, :].bitcast(BF16)).then_inc(s["qb"], 1)

                    def maxima(g):
                        for t in range(QT):
                            dve.wait_ge(s["sc"], at(b, NG * (QT + 1), g * (QT + 1) + t + 1))
                            nc.vector.tensor_reduce(negmax[:, t, g * G:(g + 1) * G], psum[:, (g * QT + t) % 3, :].rearrange("p (c j k) -> p j c k", j=G, k=32),
                                                    mybir.AxisListType.XY, ALU.max, negate=True).then_inc(s["mx"], 1)
                        dve.wait_ge(s["sc"], at(b, NG * (QT + 1), (g + 1) * (QT + 1)))
                        nc.vector.tensor_reduce(neglast[:], psum[:, 3, :].rearrange("p (t j k) -> p t j k", j=G, k=32),
                                                X_AXIS, ALU.max, negate=True).then_inc(s["mx"], 1)
                        dve.wait_ge(s["mx"], at(b, NG * (QT + 1), (g + 1) * (QT + 1)))
                        nm = negmax[:, :, g * G:(g + 1) * G]
                        v.step(nc.vector.tensor_tensor(nm, nm, neglast[:], ALU.min))
                        v.done()
                        st = qst[:, 0].rearrange("p (t h) r -> p t h r", h=H)[:, :, g * G:(g + 1) * G, :]
                        v.step(nc.vector.tensor_copy(st[:, :, :, 24], nm))
                        v.done()
                        v.step(nc.vector.tensor_tensor(rest[:], nm, st[:, :, :, 24], ALU.subtract))
                        v.done()
                        v.step(nc.vector.tensor_copy(st[:, :, :, 25], rest[:]))
                        v.done()
                        nc.vector.tensor_tensor(st[:, :, :, 26], rest[:], st[:, :, :, 25], ALU.subtract).then_inc(s["mp"], 1)

                    def normalise(g):
                        dve.wait_ge(s["o_ps"], at(b, NG, g + 1))
                        o = psum[:, 7, 0:QT * G * DVA].rearrange("p (t j e) -> p t j e", j=G, e=DVA)
                        v.step(nc.vector.reciprocal(rsum[:], o[:, :, :, DK]))
                        v.done()
                        nc.vector.tensor_tensor(on[:, :, g * G * DK:(g + 1) * G * DK].rearrange("p t (j d) -> p t j d", d=DK), o[:, :, :, 0:DK],
                                                rsum[:].unsqueeze(3).to_broadcast([P, QT, G, DK]), ALU.mult).then_inc(s["o"], 1)

                    for i in range(NG + 3):
                        if i < NG:
                            maxima(i)
                        if i >= 3:
                            normalise(i - 3)
                    dve.wait_ge(s["out"], at(b, 1, 1))
                    update_rows(core, v, b, psum[:, 6, :], gate, new, parts, mv)
                    v.close()


def experts(core, L, w, gate, E, items, loaded, n_loads, glu, capacity=0, biased=False, extra=None, x1=None):
    nc, psum = core.nc, core.psum
    NC = E + (extra is not None)
    NL = E + (extra == "sigmoid")
    NI = len(items)
    NUN = sum(len(u) for u, _ in items)
    ND = sum(len(d) for _, d in items) + biased
    MU = max(len(u) for u, _ in items)
    RING = 2 * MU
    SETS = 2 if glu else 4
    first_unit = [sum(len(u) for u, _ in items[:i]) for i in range(NI + 1)]
    first_down = [biased + sum(len(d) for _, d in items[:i]) for i in range(NI + 1)]
    STEPS = 28 + (2 if extra == "sigmoid" else 0) + (2 if capacity else 0)
    s = {n: nc.alloc_semaphore(f"{L}_{n}") for n in (
        "var", "sd", "vec", "xn", "xt_ps", "xt", "lg_ps", "gap", "th", "mask", "rank_ps", "comb", "ct_ps", "ct",
        "up", "silu", "hid", "down", "acc", "const")}

    with ExitStack() as scope:
        def sb(name, shape, dt=F32):
            return scope.enter_context(nc.sbuf_tensor(f"{L}_{name}", shape, dt))

        xn = sb("xn", [P, QT, D])
        xnT = sb("xnT", [P, SEQ])
        lg = sb("lg", [P, QT, NL])
        lg2 = sb("lg2", [P, QT, E])
        eq = sb("eq", [P, QT, E])
        score = sb("score", [P, QT, E])
        rev = sb("rev", [P, E])
        oh = sb("oh", [P, 2, QT, E])
        top = sb("top", [P, 2, QT])
        pick = sb("pick", [P, QT])
        gap = sb("gap", [P, 2, QT])
        wt = sb("wt", [P, 2, QT])
        comb = sb("comb", [P, QT, NC])
        acc = sb("acc", [P, QT, D])
        new = sb("new", [P, QT, D])
        parts = sb("parts", [P, QT, 6])
        mv = sb("mv", [P, QT, 2])
        hid = sb("hid", [P, RING, SEQ])
        if glu:
            sg = sb("sg", [P, 2, SEQ])
        if capacity:
            mask = sb("mask", [P, QT, E], BF16)
            before = sb("before", [P, E], BF16)
            tri = sb("tri", [P, P], BF16)
            picks = sb("picks", [P, E])
        if biased:
            cT = sb("cT", [E, SEQ])
        stats_v, stats_s = rows_rstd(core, L, s["var"], s["sd"], rms=x1 is not None)

        with nc.Block() as block:

            @block.gpsimd
            def _(pool):
                for e in range(E):
                    nc.gpsimd.memset(rev[:, e:e + 1], float(E - e)).then_inc(s["const"], 1)
                n = E
                if extra == "one":
                    nc.gpsimd.memset(comb[:], 1.0).then_inc(s["const"], 1)
                    n += 1
                if capacity:
                    nc.gpsimd.memset(tri[:], 1.0).then_inc(s["const"], 1)
                    nc.gpsimd.memset(before[:], 0.0).then_inc(s["const"], 1)
                    n += 2
                    pool.wait_ge(s["const"], n)
                    nc.gpsimd.affine_select(out=tri[:], in_=tri[:], compare_op=ALU.is_ge, fill=0.0, base=0,
                                            pattern=[[1, P]], channel_multiplier=-1).then_inc(s["const"], 1)

            n_const = E + (extra == "one") + (3 if capacity else 0)

            @block.tensor
            def _(pe):
                pe.wait_ge(loaded, 16 * n_loads)
                pe.wait_ge(s["const"], n_const)
                with pe.Fori(0, B) as b:
                    def router():
                        pe.wait_ge(s["xn"], at(b, 1, 1))
                        for t in range(QT):
                            last = nc.tensor.transpose(psum[:, 7, t * P:(t + 1) * P], xn[:, t, :], core.ident[:])
                        last.then_inc(s["xt_ps"], 1)
                        pe.wait_ge(s["xt"], at(b, 1, 1))
                        for t in range(QT):
                            out = psum[:, 7, t * NL:(t + 1) * NL]
                            last = nc.tensor.matmul(out, xnT[:, t * P:(t + 1) * P], w["gate"][:], start=True, stop="gate_b" not in w)
                            if "gate_b" in w:
                                last = nc.tensor.matmul(out, core.ones[0:1, :], w["gate_b"][:], start=False, stop=True)
                        last.then_inc(s["lg_ps"], 1)

                    def ranks():
                        pe.wait_ge(s["mask"], at(b, 1, 1))
                        for t in range(QT):
                            out = psum[:, 7, t * E:(t + 1) * E]
                            nc.tensor.matmul(out, tri[:], mask[:, t, :], start=True, stop=False)
                            for k in range(t):
                                nc.tensor.matmul(out, core.oneb[:], mask[:, k, :], start=False, stop=False)
                            last = nc.tensor.matmul(out, core.oneb[:], before[:], start=False, stop=True)
                        last.then_inc(s["rank_ps"], 1)

                    def second_biases():
                        pe.wait_ge(s["comb"], at(b, 1, 1))
                        for t in range(QT):
                            last = nc.tensor.transpose(psum[0:E, 7, t * P:(t + 1) * P], comb[:, t, 0:E], core.ident[:])
                        last.then_inc(s["ct_ps"], 1)
                        pe.wait_ge(s["ct"], at(b, 1, 1))
                        for t in range(QT):
                            last = nc.tensor.matmul(psum[:, 4, t * P:(t + 1) * P], cT[:, t * P:(t + 1) * P], w["b2"][:],
                                                    start=True, stop=True)
                        last.then_inc(s["down"], 1)

                    def up(i):
                        for k, (wg, wu, rows, _) in enumerate(items[i][0]):
                            n = first_unit[i] + k
                            if n >= SETS:
                                pe.wait_ge(s["hid"], at(b, NUN, n - SETS + 1))
                            if glu:
                                nc.tensor.matmul(psum[0:rows, 2 * (n % 2), :], wg, xnT[:], start=True, stop=True)
                                last = nc.tensor.matmul(psum[0:rows, 2 * (n % 2) + 1, :], wu, xnT[:], start=True, stop=True)
                            else:
                                last = nc.tensor.matmul(psum[0:rows, n % 4, :], wg, xnT[:], start=True, stop=True)
                            last.then_inc(s["up"], 1)

                    def down(i):
                        for k, (_, terms) in enumerate(items[i][1]):
                            n = first_down[i] + k
                            if k == 0:
                                pe.wait_ge(s["hid"], at(b, NUN, first_unit[i + 1]))
                            if n >= 3:
                                pe.wait_ge(s["acc"], at(b, ND, n - 2))
                            for t in range(QT):
                                for m, (u, rows, w2) in enumerate(terms):
                                    slot = (first_unit[i] + u) % RING
                                    last = nc.tensor.matmul(psum[:, 4 + n % 3, t * P:(t + 1) * P],
                                                            hid[rows, slot, t * P:(t + 1) * P], w2,
                                                            start=(m == 0), stop=(m == len(terms) - 1))
                            last.then_inc(s["down"], 1)

                    router()
                    up(0)
                    if capacity:
                        ranks()
                    for i in range(NI):
                        if i + 1 < NI:
                            up(i + 1)
                        if i == 0 and biased:
                            second_biases()
                        down(i)

            @block.scalar
            def _(act):
                stats_s(act)
                act.wait_ge(loaded, 16 * n_loads)
                with act.Fori(0, B) as b:
                    act.wait_ge(s["xt_ps"], at(b, 1, 1))
                    nc.scalar.activation(xnT[:], psum[:, 7, :], ACT.Copy).then_inc(s["xt"], 1)

                    def unit(i, k):
                        _, _, rows, bias = items[i][0][k]
                        n = first_unit[i] + k
                        act.wait_ge(s["up"], at(b, NUN, n + 1))
                        if glu:
                            if n >= 2:
                                act.wait_ge(s["hid"], at(b, NUN, n - 1))
                            nc.scalar.activation(sg[0:rows, n % 2, :], psum[0:rows, 2 * (n % 2), :], ACT.Silu).then_inc(s["silu"], 1)
                        else:
                            if k == 0 and i >= 2:
                                act.wait_ge(s["down"], at(b, ND, first_down[i - 1]))
                            nc.scalar.activation(hid[0:rows, n % RING, :], psum[0:rows, n % 4, :], ACT.Relu,
                                                 bias=bias).then_inc(s["hid"], 1)

                    for k in range(len(items[0][0])):
                        unit(0, k)
                    act.wait_ge(s["gap"], at(b, 1, 1))
                    nc.scalar.activation(gap[:], gap[:], ACT.Tanh, scale=0.5).then_inc(s["th"], 1)
                    for i in range(1, NI):
                        for k in range(len(items[i][0])):
                            unit(i, k)

            @block.vector
            def _(dve):
                stats_v(dve)
                dve.wait_ge(loaded, 16 * n_loads)
                dve.wait_ge(s["const"], n_const)
                if extra != "sigmoid":
                    nc.vector.memset(gap[:], 0.0).then_inc(s["var"], 1)
                    dve.wait_ge(s["var"], 3)
                with dve.Fori(0, B) as b:
                    v = Steps(dve, s["vec"], STEPS, b)
                    for t in range(QT):
                        n = b * QT + t
                        if x1 is None:
                            ins = nc.vector.tensor_scalar(xn[:, t, :], core.resid[:, bass.ds(n, 1), :].rearrange("p a d -> p (a d)"),
                                                          core.stat[:, bass.ds(n, 1), 0:1].rearrange("p a d -> p (a d)"),
                                                          core.rstd[:, bass.ds(n, 1)], ALU.subtract, ALU.mult)
                        else:
                            ins = nc.vector.scalar_tensor_tensor(out=xn[:, t, :], in0=x1[:, bass.ds(n, 1), :].rearrange("p a d -> p (a d)"),
                                                                 scalar=core.rstd[:, bass.ds(n, 1)], in1=w["ln2"][:],
                                                                 op0=ALU.mult, op1=ALU.mult)
                    ins.then_inc(s["xn"], 1)
                    dve.wait_ge(s["lg_ps"], at(b, 1, 1))
                    v.step(nc.vector.tensor_copy(lg[:], psum[:, 7, 0:QT * NL].rearrange("p (t e) -> p t e", e=NL)))
                    v.done()
                    le = lg[:, :, 0:E]
                    revb = rev[:].unsqueeze(1).to_broadcast([P, QT, E])

                    def across(x):
                        return x.unsqueeze(2).to_broadcast([P, QT, E])

                    src = le
                    for r in range(2):
                        v.step(nc.vector.tensor_reduce(top[:, r, :], src, X_AXIS, ALU.max))
                        v.done()
                        v.step(nc.vector.tensor_tensor(eq[:], src, across(top[:, r, :]), ALU.is_equal))
                        v.done()
                        v.step(nc.vector.tensor_tensor(score[:], eq[:], revb, ALU.mult))
                        v.done()
                        v.step(nc.vector.tensor_reduce(pick[:], score[:], X_AXIS, ALU.max))
                        v.done()
                        v.step(nc.vector.tensor_tensor(oh[:, r, :, :], revb, across(pick[:]), ALU.is_equal))
                        v.done()
                        if r == 0:
                            v.step(nc.vector.scalar_tensor_tensor(out=lg2[:], in0=oh[:, 0, :, :], scalar=-3e38, in1=le,
                                                                  op0=ALU.mult, op1=ALU.add))
                            v.done()
                            src = lg2[:]
                    if capacity:
                        v.step(nc.vector.tensor_tensor(mask[:], oh[:, 0, :, :], oh[:, 1, :, :], ALU.add))
                        v.done()
                        nc.vector.tensor_reduce(picks[:], mask[:].rearrange("p t e -> p e t"), X_AXIS, ALU.add).then_inc(s["mask"], 1)
                    if extra == "sigmoid":
                        v.step(nc.vector.tensor_copy(gap[:, 1, :], lg[:, :, E]))
                    nc.vector.tensor_tensor(gap[:, 0, :], top[:, 0, :], top[:, 1, :], ALU.subtract).then_inc(s["gap"], 1)
                    dve.wait_ge(s["th"], at(b, 1, 1))
                    v.step(nc.vector.tensor_scalar(wt[:, 0, :], gap[:, 0, :], 0.5, 0.5, ALU.mult, ALU.add))
                    v.step(nc.vector.tensor_scalar(wt[:, 1, :], gap[:, 0, :], -0.5, 0.5, ALU.mult, ALU.add))
                    v.done()
                    v.step(nc.vector.tensor_tensor(eq[:], oh[:, 0, :, :], across(wt[:, 0, :]), ALU.mult))
                    v.step(nc.vector.tensor_tensor(score[:], oh[:, 1, :, :], across(wt[:, 1, :]), ALU.mult))
                    v.done()
                    if extra == "sigmoid":
                        v.step(nc.vector.tensor_scalar(comb[:, :, E], gap[:, 1, :], 0.5, 0.5, ALU.mult, ALU.add))
                    v.step(nc.vector.tensor_tensor(comb[:, :, 0:E], eq[:], score[:], ALU.add))
                    v.done()
                    if capacity:
                        dve.wait_ge(s["rank_ps"], at(b, 1, 1))
                        v.step(nc.vector.tensor_scalar(eq[:], psum[:, 7, 0:QT * E].rearrange("p (t e) -> p t e", e=E),
                                                       float(capacity), None, ALU.is_le))
                        v.done()
                        nc.vector.tensor_tensor(before[:], before[:], picks[:], ALU.add)
                        nc.vector.tensor_tensor(comb[:], comb[:], eq[:], ALU.mult).then_inc(s["comb"], 1)
                        dve.wait_ge(s["comb"], at(b, 1, 1))
                    if biased:
                        dve.wait_ge(s["ct_ps"], at(b, 1, 1))
                        nc.vector.tensor_copy(cT[:], psum[0:E, 7, :]).then_inc(s["ct"], 1)

                    def product(i):
                        for k, (_, _, rows, _) in enumerate(items[i][0]):
                            n = first_unit[i] + k
                            dve.wait_ge(s["silu"], at(b, NUN, n + 1))
                            if k == 0 and i >= 2:
                                dve.wait_ge(s["down"], at(b, ND, first_down[i - 1]))
                            nc.vector.tensor_tensor(hid[0:rows, n % RING, :], sg[0:rows, n % 2, :],
                                                    psum[0:rows, 2 * (n % 2) + 1, :], ALU.mult).then_inc(s["hid"], 1)

                    def accumulate(n, col):
                        dve.wait_ge(s["down"], at(b, ND, n + 1))
                        if n:
                            dve.wait_ge(s["acc"], at(b, ND, n))
                        for t in range(QT):
                            ps = psum[:, 4 + n % 3, t * P:(t + 1) * P]
                            if col is None:
                                ins = nc.vector.tensor_copy(acc[:, t, :], ps)
                            elif n or x1 is not None:
                                base = acc[:, t, :] if n else x1[:, bass.ds(b * QT + t, 1), :].rearrange("p a d -> p (a d)")
                                ins = nc.vector.scalar_tensor_tensor(out=acc[:, t, :], in0=ps, scalar=comb[:, t, col:col + 1],
                                                                     in1=base, op0=ALU.mult, op1=ALU.add)
                            else:
                                ins = nc.vector.tensor_scalar(acc[:, t, :], ps, comb[:, t, col:col + 1], None, ALU.mult)
                        ins.then_inc(s["acc"], 1)

                    if glu:
                        product(0)
                    if biased:
                        accumulate(0, None)
                    for i in range(NI):
                        if glu and i + 1 < NI:
                            product(i + 1)
                        for k, (col, _) in enumerate(items[i][1]):
                            accumulate(first_down[i] + k, col)
                    dve.wait_ge(s["acc"], at(b, ND, ND))
                    update_rows(core, v, b, acc[:].rearrange("p t d -> p (t d)"), gate, new, parts, mv)
                    v.close()


def causal_attention(core, L, w, x1, loaded, n_loads):
    nc, psum = core.nc, core.psum
    DK, NOPE, ROPE, R = 64, 32, 32, 16
    G, NG = 2, 8
    DVA = NOPE + 1
    LAG, RING = 1, 8
    scale = float(DK) ** -0.5
    NR = NG * QT
    s = {n: nc.alloc_semaphore(f"{L}_{n}") for n in (
        "var", "sd", "vec", "ms", "rms", "xr", "proj", "freed", "qrot", "krot", "kfull", "sc", "mx", "mp", "mt_ps", "mt",
        "s2", "pt", "pv", "pvx", "ot_ps", "ot", "out", "const")}
    units = [("x", 0), ("lat", 0), ("kr", 0)] + [("kv", t) for t in range(QT)]
    units += [("q", (t, h)) for t in range(QT) for h in range(2)]
    units += [("kt", g) for g in range(NG)] + [("qt", g) for g in range(NG)]
    NUNIT = len(units)
    NS2 = H * QT
    STEPS = 90

    with ExitStack() as scope:
        def sb(name, shape, dt=F32):
            return scope.enter_context(nc.sbuf_tensor(f"{L}_{name}", shape, dt))

        y = sb("y", [P, QT, D])
        xr = sb("xr", [P, QT, D])
        xrT = sb("xrT", [P, SEQ])
        lat = sb("lat", [R, SEQ])
        krow = sb("krow", [P, QT, ROPE])
        krr = sb("krr", [P, QT, ROPE])
        qwork = sb("qwork", [P, RING * SEQ])
        qp = qwork[:].rearrange("p (t h e) -> p t h e", t=QT, e=DK)
        pT = qwork[:].rearrange("p (r q) -> p r q", q=SEQ)
        kwork = View(core.projections[:].rearrange("p a e -> p (a e)"))
        kp = kwork[:].rearrange("p (t h e) -> p t h e", t=QT, e=DK)
        on = kwork[:, 0:QT * H * NOPE].rearrange("p (t e) -> p t e", t=QT)
        oT = kwork[:, QT * H * NOPE:].rearrange("p (c q) -> p c q", q=SEQ)
        qT = sb("qT", [P, NG, SEQ])
        kT = sb("kT", [P, NG, SEQ])
        va = sb("va", [P, QT, H, DVA])
        ra = sb("ra", [P, 2, H, ROPE // 2])
        rb = sb("rb", [P, 2, H, ROPE // 2])
        negmax = sb("negmax", [P, QT, H])
        rest = sb("rest", [P, QT, H])
        mparts = sb("mparts", [P, QT, H, DK], BF16)
        mT = sb("mT", [P, NG, SEQ], BF16)
        rsum = sb("rsum", [P, QT, H])
        parts = sb("parts", [P, QT, 6])
        mv = sb("mv", [P, QT, 2])
        ms = sb("ms", [P, QT])
        new = sb("new", [P, QT, D])
        future = sb("future", [P, P], BF16)
        futureT = sb("futureT", [P, P], BF16)
        unit = sb("unit", [P, ROPE])
        stats_v, stats_s = rows_rstd(core, L, s["var"], s["sd"])

        with nc.Block() as block:

            @block.gpsimd
            def _(pool):
                nc.gpsimd.memset(mparts[:], 0.0).then_inc(s["const"], 1)
                nc.gpsimd.memset(va[:], 1.0).then_inc(s["const"], 1)
                nc.gpsimd.memset(future[:], 0.0).then_inc(s["const"], 1)
                nc.gpsimd.memset(futureT[:], 0.0).then_inc(s["const"], 1)
                nc.gpsimd.memset(unit[:], 1.0).then_inc(s["const"], 1)
                pool.wait_ge(s["const"], 5)
                nc.gpsimd.affine_select(out=future[:], in_=future[:], compare_op=ALU.is_ge, fill=-1e30, base=0,
                                        pattern=[[-1, P]], channel_multiplier=1).then_inc(s["const"], 1)
                nc.gpsimd.affine_select(out=futureT[:], in_=futureT[:], compare_op=ALU.is_ge, fill=-1e30, base=0,
                                        pattern=[[1, P]], channel_multiplier=-1).then_inc(s["const"], 1)
                with pool.Fori(0, B) as b:
                    pool.wait_ge(s["krot"], at(b, 1, 1))
                    nc.gpsimd.tensor_tensor(kp[:, :, :, NOPE:DK], krr[:].unsqueeze(2).to_broadcast([P, QT, H, ROPE]),
                                            unit[:].unsqueeze(1).unsqueeze(1).to_broadcast([P, QT, H, ROPE]), ALU.mult).then_inc(s["kfull"], 1)

            @block.tensor
            def _(pe):
                pe.wait_ge(loaded, 16 * n_loads)
                pe.wait_ge(s["const"], 7)
                with pe.Fori(0, B) as b:
                    pe.wait_ge(s["xr"], at(b, 1, 1))
                    for n, (what, a) in enumerate(units):
                        out = psum[:, n % 4, :]
                        if what == "lat":
                            pe.wait_ge(s["freed"], at(b, NUNIT, 1))
                        if n >= 4:
                            pe.wait_ge(s["freed"], at(b, NUNIT, n - 3))
                        if what == "x":
                            for t in range(QT):
                                last = nc.tensor.transpose(out[:, t * P:(t + 1) * P], xr[:, t, :], core.ident[:])
                        elif what == "lat":
                            last = nc.tensor.matmul(out[0:R, :], w["wkva"][:, 0:R], xrT[:], start=True, stop=True)
                        elif what == "kr":
                            for t in range(QT):
                                last = nc.tensor.matmul(out[:, t * ROPE:(t + 1) * ROPE], xrT[:, t * P:(t + 1) * P],
                                                        w["wkva"][:, R:R + ROPE], start=True, stop=True)
                        elif what == "kv":
                            if a == 0:
                                pe.wait_ge(s["freed"], at(b, NUNIT, 2))
                            last = nc.tensor.matmul(out, lat[:, a * P:(a + 1) * P], w["wkvb"][:], start=True, stop=True)
                        elif what == "q":
                            t, h = a
                            last = nc.tensor.matmul(out, xrT[:, t * P:(t + 1) * P], w["wq"][:, h * 512:(h + 1) * 512],
                                                    start=True, stop=True)
                        else:
                            if a == 0:
                                pe.wait_ge(s["kfull" if what == "kt" else "qrot"], at(b, 1, 1) if what == "kt" else at(b, QT, QT))
                                if what == "kt":
                                    pe.wait_ge(s["freed"], at(b, NUNIT, 7))
                            src = kp if what == "kt" else qp
                            for t in range(QT):
                                last = nc.tensor.transpose(out[:, t * P:(t + 1) * P],
                                                           src[:, t, a * G:(a + 1) * G, :].rearrange("p h e -> p (h e)"), core.ident[:])
                        last.then_inc(s["proj"], 1)
                    pe.wait_ge(s["freed"], at(b, NUNIT, NUNIT))

                    for g in range(NG):
                        for t in range(QT):
                            r = g * QT + t
                            n = (t + 1) * P
                            if r >= 2:
                                pe.wait_ge(s["mx"], at(b, NR, r - 1))
                            for j in range(G):
                                rows = slice(DK * j, DK * (j + 1))
                                bk = 2 * (r % 2) + j
                                nc.tensor.matmul(psum[:, bk, 0:n], qT[rows, g, t * P:n], kT[rows, g, 0:n],
                                                 start=True, stop=True)
                            for j in range(G):
                                bk = 2 * (r % 2) + j
                                last = nc.tensor.matmul(psum[:, bk, t * P:n], core.identb[:], future[:], start=False, stop=True,
                                                        skip_group_check=True)
                            last.then_inc(s["sc"], 1)
                    for k in range(NG // 2):
                        if k % 2 == 0:
                            pe.wait_ge(s["mp"], at(b, 2, k // 2 + 1))
                        if k:
                            pe.wait_ge(s["mt"], at(b, NG // 2, k))
                        bb = psum[:, 7, :].bitcast(BF16)
                        for gg in range(2):
                            g = 2 * k + gg
                            for t in range(QT):
                                last = nc.tensor.transpose(bb[:, (gg * QT + t) * P:(gg * QT + t + 1) * P],
                                                           mparts[:, t, g * G:(g + 1) * G, :].rearrange("p h s -> p (h s)"), core.identb[:])
                        last.then_inc(s["mt_ps"], 1)
                    pe.wait_ge(s["mt"], at(b, NG // 2, NG // 2))

                    def scoresT(h):
                        g, j = h // G, h % G
                        rows = slice(DK * j, DK * (j + 1))
                        for k in range(QT):
                            n = h * QT + k
                            q0 = k * P
                            if n >= 3:
                                pe.wait_ge(s["pt"], at(b, NS2, n - 2))
                            out = psum[:, 4 + n % 3, q0:SEQ]
                            nc.tensor.matmul(out, kT[rows, g, q0:q0 + P], qT[rows, g, q0:SEQ], start=True, stop=False)
                            nc.tensor.matmul(out, core.oneb[rows, :], mT[rows, g, q0:SEQ], start=False, stop=True)
                            nc.tensor.matmul(psum[:, 4 + n % 3, q0:q0 + P], core.identb[:], futureT[:], start=False, stop=True,
                                             skip_group_check=True).then_inc(s["s2"], 1)

                    def values(h):
                        pe.wait_ge(s["pt"], at(b, NS2, (h + 1) * QT))
                        if h:
                            pe.wait_ge(s["pvx"], at(b, H, h))
                        for t in range(QT):
                            for k in range(t + 1):
                                last = nc.tensor.matmul(psum[:, 7, t * DVA:(t + 1) * DVA], pT[:, (h * QT + k) % RING, t * P:(t + 1) * P],
                                                        va[:, k, h, :], start=(k == 0), stop=(k == t))
                        last.then_inc(s["pv"], 1)

                    for h in range(H + LAG):
                        if h < H:
                            scoresT(h)
                        if h >= LAG:
                            values(h - LAG)
                    pe.wait_ge(s["pvx"], at(b, H, H))
                    for c in range(4):
                        for t in range(QT):
                            last = nc.tensor.transpose(psum[:, c, t * P:(t + 1) * P], on[:, t, c * P:(c + 1) * P], core.ident[:])
                        last.then_inc(s["ot_ps"], 1)
                    pe.wait_ge(s["ot"], at(b, 4, 4))
                    for t in range(QT):
                        for c in range(4):
                            last = nc.tensor.matmul(psum[:, 7, t * P:(t + 1) * P], oT[:, c, t * P:(t + 1) * P],
                                                    w["wo"][:, c, :], start=(c == 0), stop=(c == 3))
                    last.then_inc(s["out"], 1)

            @block.scalar
            def _(act):
                stats_s(act)
                act.wait_ge(s["const"], 7)
                with act.Fori(0, B) as b:
                    act.wait_ge(s["ms"], at(b, 1, 1))
                    nc.scalar.activation(ms[:], ms[:], ACT.Sqrt).then_inc(s["rms"], 1)
                    for n, (what, a) in enumerate(units):
                        src = psum[:, n % 4, :]
                        act.wait_ge(s["proj"], at(b, NUNIT, n + 1))
                        if what == "x":
                            ins = nc.scalar.activation(xrT[:], src, ACT.Copy)
                        elif what == "lat":
                            ins = nc.scalar.activation(lat[:], src[0:R, :], ACT.Copy)
                        elif what == "kr":
                            ins = nc.scalar.activation(krow[:].rearrange("p t e -> p (t e)"), src[:, 0:QT * ROPE], ACT.Copy)
                        elif what == "kv":
                            kv = src.rearrange("p (h e) -> p h e", e=NOPE)
                            nc.scalar.activation(kp[:, a, :, 0:NOPE], kv, ACT.Copy)
                            ins = nc.scalar.activation(va[:, a, :, 0:NOPE], kv, ACT.Copy)
                        elif what == "q":
                            t, h = a
                            ins = nc.scalar.activation(qp[:, t, 8 * h:8 * h + 8, :], src.rearrange("p (h e) -> p h e", e=DK), ACT.Copy)
                        elif what == "kt":
                            ins = nc.scalar.activation(kT[:, a, :], src, ACT.Copy)
                        else:
                            ins = nc.scalar.activation(qT[:, a, :], src, ACT.Copy)
                        ins.then_inc(s["freed"], 1)
                    for n in range(NS2):
                        h, k = n // QT, n % QT
                        act.wait_ge(s["s2"], at(b, NS2, n + 1))
                        if k == 0 and h > LAG:
                            act.wait_ge(s["pv"], at(b, H, h - LAG))
                        nc.scalar.activation(pT[:, n % RING, k * P:SEQ], psum[:, 4 + n % 3, k * P:SEQ], ACT.Exp, scale=scale).then_inc(s["pt"], 1)
                    for c in range(4):
                        act.wait_ge(s["ot_ps"], at(b, 4, c + 1))
                        nc.scalar.activation(oT[:, c, :], psum[:, c, :], ACT.Copy).then_inc(s["ot"], 1)

            @block.vector
            def _(dve):
                stats_v(dve)
                dve.wait_ge(loaded, 16 * n_loads)
                with dve.Fori(0, B) as b:
                    v = Steps(dve, s["vec"], STEPS, b)
                    for t in range(QT):
                        n = b * QT + t
                        v.step(nc.vector.tensor_scalar(y[:, t, :], core.resid[:, bass.ds(n, 1), :].rearrange("p a d -> p (a d)"),
                                                       core.stat[:, bass.ds(n, 1), 0:1].rearrange("p a d -> p (a d)"),
                                                       core.rstd[:, bass.ds(n, 1)], ALU.subtract, ALU.mult))
                    v.done()
                    for t in range(QT):
                        v.step(nc.vector.bn_stats(parts[:, t, :], y[:, t, :]))
                    v.done()
                    nc.vector.memset(rsum[:, 0, 0:1], 0.0)
                    for t in range(QT):
                        v.step(nc.vector.bn_aggr(mv[:, t, :], parts[:, t, :]))
                    v.done()
                    v.step(nc.vector.tensor_tensor(ms[:], mv[:, :, 0], mv[:, :, 0], ALU.mult))
                    v.done()
                    nc.vector.scalar_tensor_tensor(out=ms[:], in0=ms[:], scalar=LN_EPS, in1=mv[:, :, 1],
                                                   op0=ALU.add, op1=ALU.add).then_inc(s["ms"], 1)
                    dve.wait_ge(s["rms"], at(b, 1, 1))
                    v.step(nc.vector.reciprocal(ms[:], ms[:]))
                    v.done()
                    for t in range(QT):
                        ins = nc.vector.scalar_tensor_tensor(out=xr[:, t, :], in0=y[:, t, :], scalar=ms[:, t:t + 1],
                                                             in1=w["ln1"][:], op0=ALU.mult, op1=ALU.mult)
                    ins.then_inc(s["xr"], 1)

                    def rotate(dst, src, cos, sin, shape, sem):
                        n, hh, half = shape[1:]
                        a, c = ra[:, 0, 0:hh, :], ra[:, 1, 0:hh, :]
                        d, e = rb[:, 0, 0:hh, :], rb[:, 1, 0:hh, :]
                        x0, x1_ = src[:, :, 0::2], src[:, :, 1::2]
                        cb = cos.unsqueeze(1).to_broadcast([P, hh, half])
                        sb_ = sin.unsqueeze(1).to_broadcast([P, hh, half])
                        v.step(nc.vector.tensor_tensor(a, x0, cb, ALU.mult))
                        v.step(nc.vector.tensor_tensor(d, x1_, sb_, ALU.mult))
                        v.step(nc.vector.tensor_tensor(c, x0, sb_, ALU.mult))
                        v.step(nc.vector.tensor_tensor(e, x1_, cb, ALU.mult))
                        v.done()
                        v.step(nc.vector.tensor_tensor(dst[:, :, 0::2], a, d, ALU.subtract))
                        ins = nc.vector.tensor_tensor(dst[:, :, 1::2], c, e, ALU.add)
                        if sem is None:
                            v.step(ins)
                            v.done()
                        else:
                            return ins

                    dve.wait_ge(s["freed"], at(b, NUNIT, 3))
                    for t in range(QT):
                        ins = rotate(krr[:, t, :].unsqueeze(1), krow[:, t, :].unsqueeze(1), w["cos"][:, t, :], w["sin"][:, t, :],
                                     (P, 1, 1, ROPE // 2), None if t < QT - 1 else True)
                    ins.then_inc(s["krot"], 1)
                    dve.wait_ge(s["krot"], at(b, 1, 1))
                    for t in range(QT):
                        dve.wait_ge(s["freed"], at(b, NUNIT, 7 + 2 * (t + 1)))
                        rotate(qp[:, t, :, NOPE:DK], qp[:, t, :, NOPE:DK], w["cos"][:, t, :], w["sin"][:, t, :],
                               (P, 1, H, ROPE // 2), True).then_inc(s["qrot"], 1)
                        dve.wait_ge(s["qrot"], at(b, QT, t + 1))

                    for g in range(NG):
                        for t in range(QT):
                            r = g * QT + t
                            n = (t + 1) * P
                            dve.wait_ge(s["sc"], at(b, NR, r + 1))
                            bk = 2 * (r % 2)
                            nc.vector.tensor_reduce(negmax[:, t, g * G:(g + 1) * G], psum[:, bk:bk + 2, 0:n],
                                                    X_AXIS, ALU.max, negate=True).then_inc(s["mx"], 1)
                        if g % 4 == 3:
                            hs = slice((g - 3) * G, (g + 1) * G)
                            dve.wait_ge(s["mx"], at(b, NR, (g + 1) * QT))
                            v.step(nc.vector.tensor_copy(mparts[:, :, hs, 0], negmax[:, :, hs]))
                            v.done()
                            v.step(nc.vector.tensor_tensor(rest[:, :, hs], negmax[:, :, hs], mparts[:, :, hs, 0], ALU.subtract))
                            v.done()
                            v.step(nc.vector.tensor_copy(mparts[:, :, hs, 1], rest[:, :, hs]))
                            v.done()
                            nc.vector.tensor_tensor(mparts[:, :, hs, 2], rest[:, :, hs], mparts[:, :, hs, 1], ALU.subtract).then_inc(s["mp"], 1)
                    for k in range(NG // 2):
                        dve.wait_ge(s["mt_ps"], at(b, NG // 2, k + 1))
                        nc.vector.tensor_copy(mT[:, 2 * k:2 * k + 2, :].rearrange("p g q -> p (g q)"),
                                              psum[:, 7, :].bitcast(BF16)).then_inc(s["mt"], 1)
                    for h in range(H):
                        dve.wait_ge(s["pv"], at(b, H, h + 1))
                        pv = psum[:, 7, 0:QT * DVA].rearrange("p (t e) -> p t e", e=DVA)
                        v.step(nc.vector.reciprocal(rsum[:, :, h:h + 1], pv[:, :, NOPE:DVA]))
                        v.done()
                        nc.vector.tensor_tensor(on[:, :, h * NOPE:(h + 1) * NOPE], pv[:, :, 0:NOPE],
                                                rsum[:, :, h:h + 1].to_broadcast([P, QT, NOPE]), ALU.mult).then_inc(s["pvx"], 1)
                    dve.wait_ge(s["out"], at(b, 1, 1))
                    update_rows(core, v, b, psum[:, 7, :], None, new, parts, mv, base=y[:].rearrange("p t d -> p (t d)"), dest=x1)
                    v.close()


def store(core, io):
    stored = core.sem("stored")
    with core.nc.Block() as block:

        @block.sync
        def _(sp):
            sp.dma_start(io["out"].rearrange("b (t p) d -> p (b t) d", p=P), core.resid[:]).then_inc(stored, 16)
            sp.wait_ge(stored, 16)


def row(ap):
    return ap.rearrange("(a n) -> a n", a=1)


def build(nc, io):
    with ExitStack() as ctx:
        core = Core(nc, ctx)
        loads, late_loads, layers = [], [], []

        def load(L, w, sem, name, shape, src, dt=F32, dst=None):
            late = L in ("L2a", "L2f", "L3f") and name != "swd"
            if name not in w and late:
                n = int(np.prod(shape[1:]))
                view = core.arena[0:shape[0], core.arena_used:core.arena_used + n]
                core.arena_used += n
                assert core.arena_used <= core.arena.shape[1]
                if len(shape) == 3:
                    view = view.rearrange("p (a b) -> p a b", b=shape[2])
                w[name] = View(view)
            if name not in w:
                w[name] = core.sb(f"{L}_{name}", shape, dt)
            (late_loads if late else loads).append((w[name][:] if dst is None else dst(w[name]), src, sem, len(layers)))

        L, w, sem = "L0x", {}, core.sem("L0x_loaded")
        n0 = len(loads) + len(late_loads)
        for n in ("q", "k", "v", "o"):
            load(L, w, sem, "w" + n, [D, D], io[f"L0_xattn_W{n}"])
        load(L, w, sem, "qn", [P, 8], io["L0_xattn_q_norm_w"].partition_broadcast(P))
        load(L, w, sem, "kn", [P, 8], io["L0_xattn_k_norm_w"].partition_broadcast(P))
        for n in ("qcos", "qsin"):
            load(L, w, sem, n, [P, QT, 4], io[n])
        for n in ("kcos", "ksin"):
            load(L, w, sem, n, [KH, 2, 4], io[n])
        load(L, w, sem, "pad", [KH, 2], io["pad"])
        pad = w["pad"]
        a = (L, w, sem, len(loads) + len(late_loads) - n0)
        layers.append(lambda a=a: narrow_attention(core, a[0], a[1], 0, "rope", a[2], a[3]))

        L, w, sem = "L0f", {}, core.sem("L0f_loaded")
        n0 = len(loads) + len(late_loads)
        load(L, w, sem, "gate", [P, 8], io["L0_ffn_gate_w"])
        load(L, w, sem, "gate_b", [1, 8], row(io["L0_ffn_gate_b"]))
        load(L, w, sem, "b1", [P, 8, 4], io["L0_ffn_b1"])
        load(L, w, sem, "b2", [8, D], io["L0_ffn_b2"])
        core.arena = core.sb("expert_arena", [P, 2 * 8 * 512])
        core.arena_used = 0
        w["w1"] = View(core.arena[:, 0:4096].rearrange("p (e f) -> p e f", e=8))
        w["w2"] = View(core.arena[:, 4096:8192].rearrange("p (e c d) -> p e c d", e=8, c=4))
        for e in range(8):
            load(L, w, sem, "w1", [P, 8, 512], io["L0_ffn_w1"][e], dst=lambda x, e=e: x[:, e, :])
            load(L, w, sem, "w2", [P, 8, 4, D], io["L0_ffn_w2"][e].rearrange("(c p) d -> p c d", p=P), dst=lambda x, e=e: x[:, e, :, :])
        items = [([(w["w1"][:, e, c * P:(c + 1) * P], None, P, w["b1"][:, e, c:c + 1]) for c in range(4)],
                  [(e, [(c, slice(0, P), w["w2"][:, e, c, :]) for c in range(4)])]) for e in range(8)]
        a = (L, w, sem, len(loads) + len(late_loads) - n0, items)
        layers.append(lambda a=a: experts(core, a[0], a[1], 4, 8, a[4], a[2], a[3], glu=False,
                                          capacity=int(1.25 * B * SEQ / 8), biased=True))

        L, w, sem = "L1x", {}, core.sem("L1x_loaded")
        n0 = len(loads) + len(late_loads)
        core.projections = core.sb("projections", [P, 4, H * 64])
        for k, n in enumerate(("q", "k", "v")):
            w["w" + n] = View(core.projections[:, k, :])
            load(L, w, sem, "w" + n, [D, H * 64], io[f"L1_xattn_W{n}"])
        w["wo"] = View(core.projections[:, 3, :].rearrange("p (c d) -> p c d", d=D))
        load(L, w, sem, "wo", [P, 8, D], io["L1_xattn_Wo"].rearrange("(c p) d -> p c d", p=P))
        w["wo"] = w["wo"][:].rearrange("p c d -> p (c d)")
        for n in ("q", "k"):
            load(L, w, sem, "b" + n, [P, 8], io[f"L1_xattn_b{n}"])
        load(L, w, sem, "bv", [1, H * 64], row(io["L1_xattn_bv"]))
        load(L, w, sem, "bo", [1, D], row(io["L1_xattn_bo"]))
        load(L, w, sem, "gamma", [P, D], io["L1_xattn_ln_gamma"].partition_broadcast(P))
        load(L, w, sem, "beta", [P, D], io["L1_xattn_ln_beta"].partition_broadcast(P))
        a = (L, w, sem, len(loads) + len(late_loads) - n0)
        layers.append(lambda a=a: cross_attention(core, a[0], a[1], 1, 64, "norm", a[2], a[3],
                                                  [x for x in late_loads if x[3] < LAYERS]))

        L, w, sem = "L1f", {}, core.sem("L1f_loaded")
        n0 = len(loads) + len(late_loads)
        load(L, w, sem, "gate", [P, 8], io["L1_ffn_gate_w"])
        for e in range(8):
            load(L, w, sem, "gu", [P, 8, 512], io["L1_ffn_gate_up_w"][e], dst=lambda x, e=e: x[:, e, :])
            load(L, w, sem, "dn", [P, 8, 2, D], io["L1_ffn_down_w"][e].rearrange("(c p) d -> p c d", p=P), dst=lambda x, e=e: x[:, e, :, :])
        items = [([(w["gu"][:, e, c * P:(c + 1) * P], w["gu"][:, e, 256 + c * P:256 + (c + 1) * P], P, None) for c in range(2)],
                  [(e, [(c, slice(0, P), w["dn"][:, e, c, :]) for c in range(2)])]) for e in range(8)]
        a = (L, w, sem, len(loads) + len(late_loads) - n0, items)
        layers.append(lambda a=a: experts(core, a[0], a[1], 5, 8, a[4], a[2], a[3], glu=True))

        L, w, sem = "L2x", {}, core.sem("L2x_loaded")
        n0 = len(loads) + len(late_loads)
        for n in ("q", "k", "v", "o"):
            load(L, w, sem, "w" + n, [D, D], io[f"L2_xattn_W{n}"])
        for n in ("q", "k"):
            load(L, w, sem, "b" + n, [P, D], io[f"L2_xattn_b{n}"].partition_broadcast(P))
        load(L, w, sem, "bv", [1, D], row(io["L2_xattn_bv"]))
        load(L, w, sem, "bo", [1, D], row(io["L2_xattn_bo"]))
        load(L, w, sem, "mask", [KH, 2, B], io["mask"][0:KH, :], dt=U8, dst=lambda x: x[:, 0, :])
        load(L, w, sem, "mask", [KH, 2, B], io["mask"][KH:CTX, :], dst=lambda x: x[0:CTX - KH, 1, :])
        core.padded.append(w["mask"])
        w["pad"] = pad
        a = (L, w, sem, len(loads) + len(late_loads) - n0)
        layers.append(lambda a=a: narrow_attention(core, a[0], a[1], 2, "mask", a[2], a[3]))

        x1 = core.sb("x1", [P, NT, D])
        L, w, sem = "L2a", {}, core.sem("L2a_loaded")
        n0 = len(loads) + len(late_loads)
        load(L, w, sem, "wq", [P, H * 64], io["L2_ffn_Wq"])
        load(L, w, sem, "wkva", [P, 48], io["L2_ffn_Wkva"])
        load(L, w, sem, "wkvb", [16, 512], io["L2_ffn_Wkvb"])
        load(L, w, sem, "wo", [P, 4, D], io["L2_ffn_Wo"])
        load(L, w, sem, "ln1", [P, D], io["L2_ffn_w_ln1"].partition_broadcast(P))
        load(L, w, sem, "cos", [P, QT, 16], io["scos"])
        load(L, w, sem, "sin", [P, QT, 16], io["ssin"])
        a = (L, w, sem, len(loads) + len(late_loads) - n0)
        L, w, sem = "L2f", {}, core.sem("L2f_loaded")
        n0 = len(loads) + len(late_loads)
        load(L, w, sem, "gate", [P, 8], io["L2_ffn_Wgate"])
        load(L, w, sem, "gate_b", [1, 8], row(io["L2_ffn_expert_bias"]))
        load(L, w, sem, "ln2", [P, D], io["L2_ffn_w_ln2"].partition_broadcast(P))
        load(L, w, sem, "wg", [P, 9, 64], io["L2_ffn_Wg"].rearrange("e c i -> c e i"), dst=lambda x: x[:, 0:8, :])
        load(L, w, sem, "wg", [P, 9, 64], io["L2_ffn_sWg"].rearrange("e c i -> c e i"), dst=lambda x: x[:, 8:9, :])
        load(L, w, sem, "wu", [P, 9, 64], io["L2_ffn_Wu"].rearrange("e c i -> c e i"), dst=lambda x: x[:, 0:8, :])
        load(L, w, sem, "wu", [P, 9, 64], io["L2_ffn_sWu"].rearrange("e c i -> c e i"), dst=lambda x: x[:, 8:9, :])
        load(L, w, sem, "wd", [P, 5, D], io["L2_ffn_Wd"].rearrange("(a e) i d -> (e i) a d", e=2), dst=lambda x: x[:, 0:4, :])
        load(L, w, sem, "wd", [P, 5, D], io["L2_ffn_sWd"][0], dst=lambda x: x[0:64, 4, :])
        lo, hi = slice(0, 64), slice(64, 128)

        def pair(wg, wu, wd, i):
            return ([(wg[:, 2 * i:2 * i + 2, :].rearrange("p e i -> p (e i)"), wu[:, 2 * i:2 * i + 2, :].rearrange("p e i -> p (e i)"), P, None)],
                    [(2 * i, [(0, lo, wd[lo, i, :])]), (2 * i + 1, [(0, hi, wd[hi, i, :])])])

        items = [pair(w["wg"], w["wu"], w["wd"], i) for i in range(4)]
        items.append(([(w["wg"][:, 8, :], w["wu"][:, 8, :], 64, None)], [(8, [(0, lo, w["wd"][lo, 4, :])])]))
        a2 = (L, w, sem, len(loads) + len(late_loads) - n0, items)

        def level2(a=a, a2=a2):
            with nc.cleanup_on_exit():
                causal_attention(core, a[0], a[1], x1, a[2], a[3])
            experts(core, a2[0], a2[1], 6, 8, a2[4], a2[2], a2[3], glu=True, extra="one", x1=x1)

        layers.append(level2)

        L, w, sem = "L3x", {}, core.sem("L3x_loaded")
        n0 = len(loads) + len(late_loads)
        for n in ("q", "k", "v"):
            load(L, w, sem, "w" + n, [P, 8], io[f"L3_xattn_w{n}"])
        load(L, w, sem, "wo", [D, D], io["L3_xattn_wo"])
        for n in ("q", "k"):
            load(L, w, sem, "b" + n, [P, D], io[f"L3_xattn_b{n}"].partition_broadcast(P))
        load(L, w, sem, "bv", [1, D], row(io["L3_xattn_bv"]))
        load(L, w, sem, "bo", [1, D], row(io["L3_xattn_bo"]))
        w["pad"] = pad
        a = (L, w, sem, len(loads) + len(late_loads) - n0)
        layers.append(lambda a=a: narrow_attention(core, a[0], a[1], 3, "plain", a[2], a[3]))

        L, w, sem = "L3f", {}, core.sem("L3f_loaded")
        n0 = len(loads) + len(late_loads)
        load(L, w, sem, "gate", [P, 17], io["L3_ffn_gate_w"], dst=lambda x: x[:, 0:16])
        load(L, w, sem, "gate", [P, 17], io["L3_ffn_shared_gate_w"], dst=lambda x: x[:, 16:17])
        gu = io["L3_ffn_w_gate_up"].rearrange("e c i -> c e i")
        load(L, w, sem, "wg", [P, 16, 64], gu[:, :, 0:64])
        load(L, w, sem, "wu", [P, 16, 64], gu[:, :, 64:128])
        load(L, w, sem, "wd", [P, 8, D], io["L3_ffn_w_down"].rearrange("(a e) i d -> (e i) a d", e=2))
        load(L, w, sem, "swg", [P, 352], io["L3_ffn_shared_w_gate"])
        load(L, w, sem, "swu", [P, 352], io["L3_ffn_shared_w_up"])
        swd = io["L3_ffn_shared_w_down"]
        load(L, w, sem, "swd", [P, 3, D], swd[0:256, :].rearrange("(c p) d -> p c d", p=P), dst=lambda x: x[:, 0:2, :])
        load(L, w, sem, "swd", [P, 3, D], swd[256:352, :], dst=lambda x: x[0:96, 2, :])
        items = [pair(w["wg"], w["wu"], w["wd"], i) for i in range(8)]
        widths = [P, P, 96]
        items.append(([(w["swg"][:, k * P:k * P + m], w["swu"][:, k * P:k * P + m], m, None) for k, m in enumerate(widths)],
                      [(16, [(k, slice(0, m), w["swd"][0:m, k, :]) for k, m in enumerate(widths)])]))
        a = (L, w, sem, len(loads) + len(late_loads) - n0, items)
        layers.append(lambda a=a: experts(core, a[0], a[1], 7, 16, a[4], a[2], a[3], glu=True, extra="sigmoid"))

        setup(core, io, [x for x in loads if x[3] < LAYERS])
        for layer in layers[:LAYERS]:
            with nc.cleanup_on_exit():
                layer()
        store(core, io)



def kernel(**inputs):
    import concourse.bacc as _bacc
    from concourse.bass_utils import run_bass_kernel_spmd as _run

    c = {k: np.asarray(v) for k, v in inputs.items()}
    t = np.ascontiguousarray
    arrays = {
        "x": c["x"], "ctx": c["ctx_1024"], "g_xattn": c["g_xattn"], "g_ffn": c["g_ffn"],
    }
    for n in "qkvo":
        arrays[f"L0_xattn_W{n}"] = t(c[f"L0_xattn_W{n}"].T)
    arrays["L0_xattn_q_norm_w"] = c["L0_xattn_q_norm_w"]
    arrays["L0_xattn_k_norm_w"] = c["L0_xattn_k_norm_w"]

    for n in ("gate_w", "gate_b", "w1", "w2", "b2"):
        arrays[f"L0_ffn_{n}"] = c[f"L0_ffn_{n}"]
    arrays["L0_ffn_b1"] = c["L0_ffn_b1"].reshape(8, 4, P).transpose(2, 0, 1)
    for n in ("Wq", "Wk", "Wv", "Wo", "bv", "bo", "ln_gamma", "ln_beta"):
        arrays[f"L1_xattn_{n}"] = c[f"L1_xattn_{n}"]
    for n in ("bq", "bk"):
        arrays[f"L1_xattn_{n}"] = c[f"L1_xattn_{n}"].reshape(8, P).T
    for n in ("gate_w", "gate_up_w", "down_w"):
        arrays[f"L1_ffn_{n}"] = c[f"L1_ffn_{n}"]

    for n in "qkvo":
        arrays[f"L2_xattn_W{n}"] = c[f"L2_xattn_W{n}"].T
    for n in ("bq", "bk", "bv", "bo"):
        arrays[f"L2_xattn_{n}"] = c[f"L2_xattn_{n}"]
    arrays["mask"] = c["mask_BxS2_bf1"].reshape(B, CTX).T.view(np.uint8)
    pad = np.zeros((2, KH), np.float32)
    pad[1, CTX - KH:] = PAD_PENALTY
    arrays["pad"] = pad.T
    for n in ("Wq", "Wkva", "Wkvb", "w_ln1", "w_ln2", "Wgate", "expert_bias", "Wg", "Wu", "Wd", "sWg", "sWu", "sWd"):
        arrays[f"L2_ffn_{n}"] = c[f"L2_ffn_{n}"]
    arrays["L2_ffn_Wo"] = c["L2_ffn_Wo"].reshape(4, 4, 64, D)[:, :, 0:32].transpose(1, 2, 0, 3).reshape(P, 4, D)
    for n in "qkv":
        a = c[f"L3_xattn_w{n}"].T
        arrays[f"L3_xattn_w{n}"] = np.broadcast_to(a[None], (H, 8, 8)).reshape(P, 8)
    arrays["L3_xattn_wo"] = c["L3_xattn_wo"].T
    for n in ("bq", "bk", "bv"):
        arrays[f"L3_xattn_{n}"] = np.broadcast_to(c[f"L3_xattn_{n}"][None], (H, 8)).reshape(-1)
    arrays["L3_xattn_bo"] = c["L3_xattn_bo"]
    for n in ("gate_w", "shared_w_gate", "shared_w_up", "shared_w_down", "shared_gate_w"):
        arrays[f"L3_ffn_{n}"] = c[f"L3_ffn_{n}"].T
    for n in ("w_gate_up", "w_down"):
        arrays[f"L3_ffn_{n}"] = c[f"L3_ffn_{n}"]

    def table(n, theta, dim, rows):
        f = np.float32(theta) ** (-np.arange(0, dim, 2, dtype=np.float32) / np.float32(dim))
        ang = np.arange(n, dtype=np.float32)[:, None] * f[None, :].astype(np.float32)
        ang = ang.reshape(n // rows, rows, dim // 2).transpose(1, 0, 2)
        return t(np.cos(ang).astype(np.float32)), t(np.sin(ang).astype(np.float32))

    arrays["qcos"], arrays["qsin"] = table(SEQ, 32.0, 8, P)
    arrays["kcos"], arrays["ksin"] = table(KP, 1000.0, 8, KH)
    arrays["scos"], arrays["ssin"] = table(SEQ, 100000.0, 32, P)

    nc = _bacc.Bacc("TRN2", target_bir_lowering=False, num_devices=1)
    feed, io = {}, {}
    for name, a in arrays.items():
        a = t(a)
        feed[f"in_{name}"] = a
        io[name] = nc.dram_tensor(f"in_{name}", a.shape, mybir.dt.from_np(a.dtype), kind="ExternalInput").ap()
    io["out"] = nc.dram_tensor("out_x", (B, SEQ, D), F32, kind="ExternalOutput").ap()
    build(nc, io)
    r = _run(nc, [feed], core_ids=[0])
    return r.results[0]["out_x"]
```

```python
from contextlib import ExitStack

import concourse.bass as bass
from concourse import mybir
import numpy as np

F32 = mybir.dt.float32
BF16 = mybir.dt.bfloat16
U8 = mybir.dt.uint8
ALU = mybir.AluOpType
ACT = mybir.ActivationFunctionType
X_AXIS = mybir.AxisListType.X

LAYERS = 8
P = 128
D = 128
B = 4
SEQ = 512
QT = SEQ // P
NT = B * QT
CTX = 154
KC = CTX // 2
H = 16
LN_EPS = 1e-5


def at(trip, per_trip, n):
    return trip * per_trip + n


class Core:

    def __init__(self, nc, ctx):
        self.nc, self.ctx = nc, ctx
        self.resid = self.sb("resid", [P, NT, D])
        self.stat = self.sb("stat", [P, NT, 2])
        self.std = self.sb("std", [P, NT])
        self.rstd = self.sb("rstd", [P, NT])
        self.ident = self.sb("ident", [P, P])
        self.identb = self.sb("identb", [P, P], BF16)
        self.ones = self.sb("ones", [1, P])
        self.oneb = self.sb("oneb", [P, P], BF16)
        self.hmask = self.sb("hmask", [P, H])
        self.ctxT = self.sb("ctxT", [P, B * CTX])
        self.gate = self.sb("gate", [P, 8])
        self.padded = []
        self.squares = self.sem("squares")
        self.psum = ctx.enter_context(nc.psum_tensor("psum", [P, 8, 512], F32))

    def sb(self, name, shape, dt=F32):
        return self.ctx.enter_context(self.nc.sbuf_tensor(name, shape, dt))

    def sem(self, name):
        return self.ctx.enter_context(self.nc.semaphore(name))


def setup(core, io, loads):
    nc = core.nc
    with ExitStack() as scope:
        ctx_rows = scope.enter_context(nc.sbuf_tensor("ctx_rows", [KC, 2 * B, D], F32))
        parts = scope.enter_context(nc.sbuf_tensor("setup_parts", [P, NT, 6], F32))
        x_in = [core.sem(f"x_in{b}") for b in range(B)]
        ctx_in, gate_in = core.sem("ctx_in"), core.sem("gate_in")
        consts, ident_made = core.sem("consts"), core.sem("ident_made")
        ctx_ps, ctx_made = core.sem("ctx_ps"), core.sem("ctx_made")
        parts_made = core.sem("parts_made")
        zeroed = core.sem("zeroed")
        with nc.Block() as block:

            @block.sync
            def _(sp):
                sp.dma_start(ctx_rows[:], io["ctx"].rearrange("b (c p) d -> p (b c) d", p=KC)).then_inc(ctx_in, 16)
                xv = io["x"].rearrange("b (t p) d -> p (b t) d", p=P)
                for b in range(B):
                    sp.dma_start(core.resid[:, 4 * b:4 * b + 4, :], xv[:, 4 * b:4 * b + 4, :]).then_inc(x_in[b], 16)
                sp.dma_start(core.gate[:, 0:4], io["g_xattn"].partition_broadcast(P)).then_inc(gate_in, 16)
                sp.dma_start(core.gate[:, 4:8], io["g_ffn"].partition_broadcast(P)).then_inc(gate_in, 16)

            @block.gpsimd
            def _(pool):
                for small in core.padded:
                    nc.gpsimd.memset(small[:], 0.0).then_inc(zeroed, 1)
                nc.gpsimd.memset(core.ident[:], 0.0).then_inc(consts, 1)
                nc.gpsimd.memset(core.ones[:], 1.0).then_inc(consts, 1)
                nc.gpsimd.memset(core.oneb[:], 1.0).then_inc(consts, 1)
                nc.gpsimd.memset(core.hmask[:], 1.0).then_inc(consts, 1)
                pool.wait_ge(consts, 4)
                nc.gpsimd.affine_select(out=core.ident[:], in_=core.ident[:], compare_op=ALU.not_equal,
                                        fill=1.0, base=0, pattern=[[-1, P]], channel_multiplier=1).then_inc(consts, 1)
                nc.gpsimd.affine_select(out=core.hmask[:], in_=core.hmask[:], compare_op=ALU.is_ge,
                                        fill=0.0, base=0, pattern=[[-8, H]], channel_multiplier=1).then_inc(consts, 1)
                pool.wait_ge(consts, 6)
                nc.gpsimd.affine_select(out=core.hmask[:], in_=core.hmask[:], compare_op=ALU.is_ge,
                                        fill=0.0, base=7, pattern=[[8, H]], channel_multiplier=-1).then_inc(consts, 1)
                nc.gpsimd.tensor_copy(core.identb[:], core.ident[:]).then_inc(ident_made, 1)

            @block.tensor
            def _(pe):
                pe.wait_ge(ctx_in, 16)
                pe.wait_ge(ident_made, 1)
                for k in range(2 * B):
                    last = nc.tensor.transpose(core.psum[:, k // 4, (k % 4) * KC:(k % 4 + 1) * KC],
                                               ctx_rows[:, k, :], core.ident[0:KC, 0:KC])
                last.then_inc(ctx_ps, 1)

            @block.scalar
            def _(act):
                for dst, src, sem, _ in loads:
                    act.dma_start(dst, src).then_inc(sem, 16)
                act.wait_ge(zeroed, len(core.padded))
                act.wait_ge(gate_in, 32)
                nc.scalar.activation(core.gate[:], core.gate[:], ACT.Tanh)
                act.wait_ge(ctx_ps, 1)
                for k in range(2):
                    nc.scalar.activation(core.ctxT[:, k * 4 * KC:(k + 1) * 4 * KC],
                                         core.psum[:, k, 0:4 * KC], ACT.Copy).then_inc(ctx_made, 1)

            @block.vector
            def _(dve):
                for n in range(NT):
                    if n % 4 == 0:
                        dve.wait_ge(x_in[n // 4], 16)
                    nc.vector.bn_stats(parts[:, n, :], core.resid[:, n, :]).then_inc(parts_made, 1)
                for n in range(NT):
                    dve.wait_ge(parts_made, n + 1)
                    last = nc.vector.bn_aggr(core.stat[:, n, :], parts[:, n, :])
                last.then_inc(parts_made, 1)


class View:

    def __init__(self, ap):
        self.ap = ap

    def __getitem__(self, key):
        return self.ap[key] if key != slice(None) else self.ap


class Steps:

    def __init__(self, eng, sem, per_trip, trip):
        self.eng, self.sem, self.per, self.trip, self.n = eng, sem, per_trip, trip, 0

    def step(self, ins):
        self.n += 1
        ins.then_inc(self.sem, 1)
        return self.n

    def done(self, n=None):
        self.eng.wait_ge(self.sem, at(self.trip, self.per, self.n if n is None else n))

    def close(self):
        assert self.n == self.per, f"{self.n} steps a trip, not {self.per}"


def rows_rstd(core, name, dve_sem, act_sem, rms=False):
    nc = core.nc

    def vector(dve):
        if rms:
            nc.vector.tensor_tensor(core.rstd[:], core.stat[:, :, 0], core.stat[:, :, 0], ALU.mult).then_inc(core.squares, 1)
            dve.wait_ge(core.squares, 1)
            nc.vector.scalar_tensor_tensor(out=core.std[:], in0=core.rstd[:], scalar=LN_EPS, in1=core.stat[:, :, 1],
                                           op0=ALU.add, op1=ALU.add).then_inc(dve_sem, 1)
        else:
            nc.vector.tensor_scalar(core.std[:], core.stat[:, :, 1], LN_EPS, None, ALU.add).then_inc(dve_sem, 1)
        dve.wait_ge(act_sem, 1)
        nc.vector.reciprocal(core.rstd[:], core.std[:]).then_inc(dve_sem, 1)
        dve.wait_ge(dve_sem, 2)

    def scalar(act):
        act.wait_ge(dve_sem, 1)
        nc.scalar.activation(core.std[:], core.std[:], ACT.Sqrt).then_inc(act_sem, 1)

    return vector, scalar


def wide_attention(core, L, w, gate, loaded, n_loads, late_loads):
    nc, psum = core.nc, core.psum
    DK, G = 64, 2
    NG = H // G
    UPU = 2
    LAG = 2
    RING = (LAG + 1) * UPU
    PV_BANKS = 4
    scale = float(DK) ** -0.5
    NR = 2 * NG
    half = NG // 2
    s = {n: nc.alloc_semaphore(f"{L}_{n}") for n in (
        "prep", "var", "sd", "vec", "xn", "ctxb", "proj", "freed", "vb", "sc", "mx", "mp", "mt_ps", "mt", "s2", "pt",
        "pv", "o", "rs", "on", "out", "y", "yvar", "ysd")}

    with ExitStack() as scope:
        def sb(name, shape, dt=F32):
            return scope.enter_context(nc.sbuf_tensor(f"{L}_{name}", shape, dt))

        xn = sb("xn", [P, QT, D])
        xnT = sb("xnT", [P, SEQ])
        ctxb = sb("ctxb", [P, CTX])
        qT = sb("qT", [P, NG, SEQ])
        kT = sb("kT", [P, NG, G, CTX])
        pick = sb("pick", [P, G, KC], BF16)
        va = sb("va", [KC, 2, H, 2, DK])
        negmax = sb("negmax", [P, QT, H])
        rest = sb("rest", [P, QT, H])
        mparts = sb("mparts", [P, QT, H, DK], BF16)
        mT = sb("mT", [P, NG, SEQ], BF16)
        pT = sb("pT", [KC, RING, SEQ])
        rsum = sb("rsum", [P, 2, SEQ])
        oT = sb("oT", [P, NG, SEQ])
        parts = sb("parts", [P, QT, 6])
        mv = sb("mv", [P, QT, 2])
        y = sb("y", [P, QT, D])
        sdv = sb("sdv", [P, QT])
        stats_v, stats_s = rows_rstd(core, L, s["var"], s["sd"])

        units = [("x", 0)]
        units += [("k", g) for g in range(NG)] + [("q", g) for g in range(NG)]
        units += [("v", (c, h)) for c in range(2) for h in range(2)]
        NUNIT = len(units)
        NFREED = NUNIT - 4
        V_UNITS = range(1 + 2 * NG, 5 + 2 * NG)
        DVE_STEPS = 41

        with nc.Block() as block:

            @block.sync
            def _(sp):
                for dst, src, sem, _ in late_loads:
                    sp.dma_start(dst, src).then_inc(sem, 16)

            @block.gpsimd
            def _(pool):
                nc.gpsimd.memset(mparts[:], 0.0).then_inc(s["prep"], 1)
                nc.gpsimd.memset(va[:], 1.0).then_inc(s["prep"], 1)
                nc.gpsimd.memset(kT[:], 0.0).then_inc(s["prep"], 1)
                nc.gpsimd.memset(pick[:], 0.0).then_inc(s["prep"], 1)
                for j in range(G):
                    pool.wait_ge(s["prep"], 4 + j)
                    nc.gpsimd.memset(pick[DK * j:DK * j + DK, j, :], 1.0).then_inc(s["prep"], 1)

            @block.tensor
            def _(pe):
                pe.wait_ge(loaded, 16 * n_loads)
                pe.wait_ge(s["prep"], 4 + G)
                with pe.Fori(0, B) as b:
                    pe.wait_ge(s["xn"], at(b, 1, 1))
                    for t in range(QT):
                        last = nc.tensor.transpose(psum[:, 0, t * P:(t + 1) * P], xn[:, t, :], core.ident[:])
                    last.then_inc(s["proj"], 1)
                    pe.wait_ge(s["ctxb"], at(b, 1, 1))
                    for n, (what, a) in enumerate(units):
                        if n == 0:
                            continue
                        if n >= 4:
                            pe.wait_ge(s["freed"], at(b, NFREED, n - 3))
                        out = psum[:, n % 4, :]
                        if what == "q":
                            last = nc.tensor.matmul(out, w["wq"][:, a * P:(a + 1) * P], xnT[:], start=True, stop=True)
                        elif what == "k":
                            last = nc.tensor.matmul(out[:, 0:CTX], w["wk"][:, a * P:(a + 1) * P], ctxb[:], start=True, stop=True)
                        else:
                            c, hh = a
                            last = nc.tensor.matmul(out[0:KC, :], ctxb[:, c * KC:(c + 1) * KC], w["wv"][:, hh * 512:(hh + 1) * 512],
                                                    start=True, stop=True)
                        last.then_inc(s["proj"], 1)
                    pe.wait_ge(s["freed"], at(b, NFREED, NFREED))
                    pe.wait_ge(s["vb"], at(b, 4, 4))

                    def score_round(g, pair):
                        r = 2 * g + pair
                        if r >= 3:
                            pe.wait_ge(s["mx"], at(b, NR, r - 2))
                        for q in range(2):
                            t = 2 * pair + q
                            last = nc.tensor.matmul(psum[:, 2 * (r % 3) + q, 0:G * CTX], qT[:, g, t * P:(t + 1) * P],
                                                    kT[:, g].rearrange("p j k -> p (j k)"), start=True, stop=True)
                        last.then_inc(s["sc"], 1)

                    def max_rows(hf):
                        pe.wait_ge(s["mp"], at(b, 2, hf + 1))
                        for k in range(half // 2):
                            if hf or k:
                                pe.wait_ge(s["mt"], at(b, NG // 2, hf * (half // 2) + k))
                            bb = psum[:, 7, :].bitcast(BF16)
                            for gg in range(2):
                                g = hf * half + 2 * k + gg
                                for t in range(QT):
                                    last = nc.tensor.transpose(bb[:, (gg * QT + t) * P:(gg * QT + t + 1) * P],
                                                               mparts[:, t, g * G:(g + 1) * G, :].rearrange("p h s -> p (h s)"),
                                                               core.identb[:])
                            last.then_inc(s["mt_ps"], 1)

                    def scoresT(h):
                        g, j = h // G, h % G
                        if h % 4 == 0:
                            pe.wait_ge(s["mt"], at(b, NG // 2, h // 4 + 1))
                        for c in range(2):
                            n = h * UPU + c
                            if n >= 3:
                                pe.wait_ge(s["pt"], at(b, 2 * H, n - 2))
                            out = psum[0:KC, 4 + n % 3, :]
                            nc.tensor.matmul(out, kT[:, g, j, c * KC:(c + 1) * KC], qT[:, g, :], start=True, stop=False)
                            nc.tensor.matmul(out, pick[:, j, :], mT[:, g, :], start=False, stop=True).then_inc(s["s2"], 1)

                    def values(h):
                        pe.wait_ge(s["pt"], at(b, 2 * H, (h + 1) * UPU))
                        if h >= PV_BANKS:
                            pe.wait_ge(s["o"], at(b, H, h - PV_BANKS + 1))
                            pe.wait_ge(s["rs"], at(b, H, h - PV_BANKS + 1))
                        for c in range(2):
                            last = nc.tensor.matmul(psum[:, h % PV_BANKS, :], va[:, c, h].rearrange("p a e -> p (a e)"),
                                                    pT[:, (h * UPU + c) % RING, :], start=(c == 0), stop=(c == 1))
                        last.then_inc(s["pv"], 1)

                    for g in range(NG):
                        score_round(g, 0)
                        score_round(g, 1)
                        if g == half:
                            max_rows(0)
                    max_rows(1)
                    for h in range(H + LAG):
                        if h < H:
                            scoresT(h)
                        if h >= LAG:
                            values(h - LAG)
                    for k in range(NG):
                        pe.wait_ge(s["on"], at(b, NG, k + 1))
                        for t in range(QT):
                            last = nc.tensor.matmul(psum[:, 7, t * P:(t + 1) * P], oT[:, k, t * P:(t + 1) * P],
                                                    w["wo"][:, k * P:(k + 1) * P], start=(k == 0 and t == 0), stop=False, skip_group_check=True)
                    for t in range(QT):
                        last = nc.tensor.matmul(psum[:, 7, t * P:(t + 1) * P], core.ones[0:1, :], w["bo"][0:1, :],
                                                start=False, stop=True, skip_group_check=True)
                    last.then_inc(s["out"], 1)

            @block.scalar
            def _(act):
                stats_s(act)
                act.wait_ge(s["prep"], 4 + G)
                act.wait_ge(loaded, 16 * n_loads)
                with act.Fori(0, B) as b:
                    for n, (what, a) in enumerate(units):
                        src = psum[:, n % 4, :]
                        if n in V_UNITS:
                            continue
                        act.wait_ge(s["proj"], at(b, NUNIT, n + 1))
                        if what == "x":
                            ins = nc.scalar.activation(xnT[:], src, ACT.Copy)
                        elif what == "q":
                            ins = nc.scalar.activation(qT[:, a, :], src, ACT.Identity, bias=w["bq"][:, a:a + 1])
                        else:
                            for j in range(G):
                                rows = slice(DK * j, DK * j + DK)
                                ins = nc.scalar.activation(kT[rows, a, j, :], src[rows, 0:CTX], ACT.Identity, bias=w["bk"][rows, a:a + 1])
                        ins.then_inc(s["freed"], 1)

                    def sums(h):
                        act.wait_ge(s["pv"], at(b, H, h + 1))
                        if h >= 4 and h % 2 == 0:
                            act.wait_ge(s["on"], at(b, NG, h // 2 - 1))
                        r0 = DK * (h % 2)
                        nc.scalar.activation(rsum[r0:r0 + DK, (h // 2) % 2, :], psum[DK:P, h % PV_BANKS, :], ACT.Copy).then_inc(s["rs"], 1)

                    for h in range(H):
                        for c in range(UPU):
                            n = h * UPU + c
                            act.wait_ge(s["s2"], at(b, 2 * H, n + 1))
                            if c == 0 and h > LAG:
                                act.wait_ge(s["pv"], at(b, H, h - LAG))
                            nc.scalar.activation(pT[:, n % RING, :], psum[0:KC, 4 + n % 3, :], ACT.Exp, scale=scale).then_inc(s["pt"], 1)
                        if h >= LAG + 1:
                            sums(h - LAG - 1)
                    for h in range(H - LAG - 1, H):
                        sums(h)
                    act.wait_ge(s["yvar"], at(b, 1, 1))
                    nc.scalar.activation(sdv[:], sdv[:], ACT.Sqrt).then_inc(s["ysd"], 1)

            @block.vector
            def _(dve):
                stats_v(dve)
                dve.wait_ge(loaded, 16 * n_loads)
                dve.wait_ge(s["prep"], 4 + G)
                def front(f):
                    for t in range(QT):
                        n = f * QT + t
                        ins = nc.vector.tensor_scalar(xn[:, t, :], core.resid[:, bass.ds(n, 1), :].rearrange("p a d -> p (a d)"),
                                                      core.stat[:, bass.ds(n, 1), 0:1].rearrange("p a d -> p (a d)"),
                                                      core.rstd[:, bass.ds(n, 1)], ALU.subtract, ALU.mult)
                    ins.then_inc(s["xn"], 1)
                    nc.vector.tensor_copy(ctxb[:], core.ctxT[:, bass.ds(f * CTX, CTX)]).then_inc(s["ctxb"], 1)

                def attention(b, f):
                    v = Steps(dve, s["vec"], DVE_STEPS, b)
                    for n in V_UNITS:
                        c, hh = units[n][1]
                        dve.wait_ge(s["proj"], at(b, NUNIT, n + 1))
                        nc.vector.tensor_tensor(va[:, c, hh * 8:(hh + 1) * 8, 0, :], psum[0:KC, n % 4, :].rearrange("p (h d) -> p h d", d=DK),
                                                w["bv"][:, hh * 512:(hh + 1) * 512].rearrange("p (h d) -> p h d", d=DK),
                                                ALU.add).then_inc(s["vb"], 1)

                    for g in range(NG):
                        for pair in range(2):
                            r = 2 * g + pair
                            dve.wait_ge(s["sc"], at(b, NR, r + 1))
                            nc.vector.tensor_reduce(
                                negmax[:, 2 * pair:2 * pair + 2, g * G:(g + 1) * G],
                                psum[:, 2 * (r % 3):2 * (r % 3) + 2, 0:2 * CTX].rearrange("p t (j c) -> p t j c", c=CTX),
                                X_AXIS, ALU.max, negate=True).then_inc(s["mx"], 1)
                        if g % half == half - 1:
                            hf = g // half
                            hs = slice(hf * half * G, (hf + 1) * half * G)
                            dve.wait_ge(s["mx"], at(b, NR, 2 * g + 2))
                            mpv = mparts[:, :, hs, :]
                            v.step(nc.vector.tensor_copy(mpv[:, :, :, 0], negmax[:, :, hs]))
                            v.done()
                            v.step(nc.vector.tensor_tensor(rest[:, :, hs], negmax[:, :, hs], mpv[:, :, :, 0], ALU.subtract))
                            v.done()
                            v.step(nc.vector.tensor_copy(mpv[:, :, :, 1], rest[:, :, hs]))
                            v.done()
                            nc.vector.tensor_tensor(mpv[:, :, :, 2], rest[:, :, hs], mpv[:, :, :, 1], ALU.subtract).then_inc(s["mp"], 1)
                        if g == half or g == NG - 1:
                            for k in range(half // 2) if g == half else range(half // 2, NG // 2):
                                dve.wait_ge(s["mt_ps"], at(b, NG // 2, k + 1))
                                nc.vector.tensor_copy(mT[:, 2 * k:2 * k + 2, :].rearrange("p g q -> p (g q)"),
                                                      psum[:, 7, :].bitcast(BF16)).then_inc(s["mt"], 1)

                    def products(h):
                        dve.wait_ge(s["pv"], at(b, H, h + 1))
                        r0 = DK * (h % 2)
                        nc.vector.tensor_copy(oT[r0:r0 + DK, h // 2, :], psum[0:DK, h % PV_BANKS, :]).then_inc(s["o"], 1)

                    for g in range(NG):
                        products(2 * g)
                        products(2 * g + 1)
                        dve.wait_ge(s["rs"], at(b, H, 2 * g + 2))
                        v.step(nc.vector.reciprocal(rsum[:, g % 2, :], rsum[:, g % 2, :]))
                        v.done()
                        dve.wait_ge(s["o"], at(b, H, 2 * g + 2))
                        nc.vector.tensor_tensor(oT[:, g, :], oT[:, g, :], rsum[:, g % 2, :], ALU.mult).then_inc(s["on"], 1)
                    dve.wait_ge(s["out"], at(b, 1, 1))
                    v.step(nc.vector.tensor_tensor(y[:], psum[:, 7, :].rearrange("p (t d) -> p t d", d=D), xn[:], ALU.add))
                    v.done()
                    if f is not None:
                        front(f)
                    for t in range(QT):
                        v.step(nc.vector.bn_stats(parts[:, t, :], y[:, t, :]))
                    v.done()
                    nc.vector.memset(rest[:, 0, 0:1], 0.0)
                    for t in range(QT):
                        v.step(nc.vector.bn_aggr(mv[:, t, :], parts[:, t, :]))
                    v.done()
                    nc.vector.tensor_scalar(sdv[:], mv[:, :, 1], LN_EPS, None, ALU.add).then_inc(s["yvar"], 1)
                    dve.wait_ge(s["ysd"], at(b, 1, 1))
                    v.step(nc.vector.reciprocal(sdv[:], sdv[:]))
                    v.done()
                    for t in range(QT):
                        v.step(nc.vector.tensor_scalar(y[:, t, :], y[:, t, :], mv[:, t, 0:1], sdv[:, t:t + 1], ALU.subtract, ALU.mult))
                    v.done()
                    v.step(nc.vector.tensor_tensor(y[:], y[:], w["gamma"][:].unsqueeze(1).to_broadcast([P, QT, D]), ALU.mult))
                    v.done()
                    v.step(nc.vector.tensor_tensor(y[:], y[:], w["beta"][:].unsqueeze(1).to_broadcast([P, QT, D]), ALU.add))
                    v.done()
                    update_rows(core, v, b, y[:].rearrange("p t d -> p (t d)"), gate, y, parts, mv)
                    v.close()

                front(0)
                with dve.Fori(0, B - 1) as b:
                    attention(b, b + 1)
                attention(B - 1, None)


def add_rows(core, v, b, src, gate, new, base=None):
    rb = core.resid[:, bass.ds(b * QT, QT), :].rearrange("p t d -> p (t d)") if base is None else base
    v.step(core.nc.vector.scalar_tensor_tensor(out=new[:].rearrange("p t d -> p (t d)"), in0=src,
                                               scalar=1.0 if gate is None else core.gate[:, gate:gate + 1],
                                               in1=rb, op0=ALU.mult, op1=ALU.add))
    v.done()


def keep_rows(core, v, b, new, parts, mv, dest=None):
    nc = core.nc
    rb = (dest or core.resid)[:, bass.ds(b * QT, QT), :].rearrange("p t d -> p (t d)")
    for t in range(QT):
        v.step(nc.vector.bn_stats(parts[:, t, :], new[:, t, :]))
    v.done()
    v.step(nc.vector.tensor_scalar(rb, new[:].rearrange("p t d -> p (t d)"), 1.0, None, ALU.mult))
    for t in range(QT):
        v.step(nc.vector.bn_aggr(mv[:, t, :], parts[:, t, :]))
    v.done()
    v.step(nc.vector.tensor_scalar(core.stat[:, bass.ds(b * QT, QT), :], mv[:], 1.0, None, ALU.mult))
    v.done()


def update_rows(core, v, b, src, gate, new, parts, mv):
    add_rows(core, v, b, src, gate, new)
    keep_rows(core, v, b, new, parts, mv)


NK = 5
KP = NK * 32
KH = KP // 2
PART = 32
PAD_PENALTY = -1e30


def narrow_attention(core, L, w, gate, kind, loaded, n_loads, late_loads=()):
    nc, psum = core.nc, core.psum
    rope, masked = kind == "rope", kind == "mask"
    DK, G, NG = 8, 4, 4
    scale = 128.0 ** -0.5 if kind == "plain" else float(DK) ** -0.5
    RING = 2 * NK
    NX = NG * NK
    s = {n: nc.alloc_semaphore(f"{L}_{n}") for n in (
        "prep", "prepd", "var", "sd", "vec", "fvec", "updated", "xn", "ctxr", "xt_ps", "xt", "q_ps", "k_ps", "v_ps", "q_raw", "k_raw", "rms_v", "rms_s",
        "q_f", "k_f", "q_hi", "k_hi", "q_rest", "k_rest", "q_mid", "k_mid", "q_lo", "k_lo", "q_dup", "k_dup", 
        "kt_ps", "kt", "bd_a", "bd_b", "vbd", "qt_ps", "qa", "qb", "sc", "mx", "mp", "rt_ps", "rt", "s2", "pt", "pv", "rs", "o", "on", "out")}

    with ExitStack() as scope:
        def sb(name, shape, dt=F32):
            return scope.enter_context(nc.sbuf_tensor(f"{L}_{name}", shape, dt))

        xn = sb("xn", [P, QT, D])
        xnT = sb("xnT", [P, SEQ])
        ctxr = sb("ctxr", [P, NK, G, 32])
        ctxp = sb("ctxp", [P, KP])
        qf = sb("qf", [P, QT * H, DK])
        kf = sb("kf", [KH, 2 * H, DK])
        qr = sb("qr", [P, QT * H, DK])
        kr = sb("kr", [KH, 2 * H, DK])
        qst = sb("qst", [P, 2, QT * H, PART], BF16)
        kst = sb("kst", [KH, 2, 2 * H, PART], BF16)
        qT = sb("qT", [P, 2, NG, SEQ], BF16)
        qmT = sb("qmT", [P, NG, SEQ], BF16)
        kT = sb("kT", [P, 2, NG, KP], BF16)
        bd = sb("bd", [P, 2, NG, NK, G, 32], BF16)
        vbd = sb("vbd", [P, NK * NG, 2, G, DK])
        quad = sb("quad", [P, G])
        quadb = sb("quadb", [P, G], BF16)
        one = sb("one", [P, 1])
        negmax = sb("negmax", [P, QT, H])
        neglast = sb("neglast", [P, QT, G])
        rest = sb("rest", [P, QT, G])
        pT = sb("pT", [P, RING, SEQ])
        rsum = sb("rsum", [P, SEQ])
        oT = sb("oT", [P, SEQ])
        parts = sb("parts", [P, QT, 6])
        mv = sb("mv", [P, QT, 2])
        new = sb("new", [P, QT, D])
        if rope:
            ss = sb("ss", [P, 2, QT * H])
            ra = sb("ra", [P, QT * H, DK])
            rb = sb("rb", [P, QT * H, DK])
        pen = sb("pen", [KH, B, 2])
        if kind == "plain":
            wq, wk, wv = (sb(f"blk{n}", [P, H, DK]) for n in "qkv")
            wq, wk, wv = (x[:].rearrange("p h d -> p (h d)") for x in (wq, wk, wv))
        else:
            wq, wk, wv = w["wq"][:], w["wk"][:], w["wv"][:]
        if masked:
            m_f = sb("m_f", [KH, B, 2])
            m_b = sb("m_b", [KH, 2])
        pen_r = sb("pen_r", [KH, B, 2])
        pen3 = sb("pen3", [KH, B, 2, 3], BF16)
        def value_bank(g):
            return 6 if g < NG - 1 else 1

        stats_v, stats_s = rows_rstd(core, L, s["var"], s["sd"])
        N_PREP = 8 + (3 if kind == "plain" else 0) + 1
        DVE_STEPS = 31
        FRONT_STEPS = {"rope": 24, "mask": 6, "plain": 4}[kind]

        with nc.Block() as block:

            @block.sync
            def _(sp):
                for dst, src, sem, _ in late_loads:
                    sp.dma_start(dst, src).then_inc(sem, 16)

            @block.gpsimd
            def _(pool):
                for x, value in ((qst, 0.0), (kst, 0.0), (vbd, 0.0), (quad, 1.0), (one, 1.0), (ctxr, 0.0), (ctxp, 0.0)):
                    nc.gpsimd.memset(x[:], value).then_inc(s["prep"], 1)
                n = 7
                pool.wait_ge(s["prep"], n)
                nc.gpsimd.memset(qst[:, 0, :, 27:30], 1.0).then_inc(s["prep"], 1)
                nc.gpsimd.memset(kst[:, 0, :, 24:27], 1.0).then_inc(s["prepd"], 1)
                nc.gpsimd.affine_select(out=quad[:], in_=quad[:], compare_op=ALU.is_ge, fill=0.0, base=0,
                                        pattern=[[-32, G]], channel_multiplier=1).then_inc(s["prepd"], 1)
                pool.wait_ge(s["prepd"], 2)
                nc.gpsimd.affine_select(out=quad[:], in_=quad[:], compare_op=ALU.is_ge, fill=0.0, base=31,
                                        pattern=[[32, G]], channel_multiplier=-1).then_inc(s["prepd"], 1)
                if kind == "plain":
                    pool.wait_ge(loaded, 16 * n_loads)
                    hm = core.hmask[:].unsqueeze(2).to_broadcast([P, H, DK])
                    for dst, src in ((wq, w["wq"]), (wk, w["wk"]), (wv, w["wv"])):
                        nc.gpsimd.tensor_tensor(dst.rearrange("p (h d) -> p h d", d=DK), src[:].unsqueeze(1).to_broadcast([P, H, DK]),
                                                hm, ALU.mult).then_inc(s["prep"], 1)
                pool.wait_ge(s["prepd"], 3)
                nc.gpsimd.tensor_copy(quadb[:], quad[:]).then_inc(s["prep"], 1)
                pool.wait_ge(s["prep"], N_PREP)
                with pool.Fori(0, B) as b:
                    def copied(dst, src, sem):
                        rows, n = dst.shape[0], dst.shape[1]
                        nc.gpsimd.tensor_tensor(dst, src, core.oneb[0:rows, 0:1].unsqueeze(2).to_broadcast([rows, n, DK]),
                                                ALU.mult).then_inc(sem, 1)

                    pool.wait_ge(s["k_hi"], at(b, 1, 1))
                    copied(kst[:, 0, :, 16:24], kst[:, 0, :, 0:8], s["k_dup"])
                    copied(kst[:, 1, :, 16:24], kst[:, 0, :, 0:8], s["k_dup"])
                    pool.wait_ge(s["k_mid"], at(b, 1, 1))
                    copied(kst[:, 1, :, 0:8], kst[:, 0, :, 8:16], s["k_dup"])
                    pool.wait_ge(s["q_hi"], at(b, 1, 1))
                    copied(qst[:, 0, :, 8:16], qst[:, 0, :, 0:8], s["q_dup"])
                    copied(qst[:, 1, :, 8:16], qst[:, 0, :, 0:8], s["q_dup"])
                    pool.wait_ge(s["q_mid"], at(b, 1, 1))
                    copied(qst[:, 1, :, 0:8], qst[:, 0, :, 16:24], s["q_dup"])
                    pool.wait_ge(s["kt"], at(b, 2, 2))
                    for g in range(NG):
                        ins = nc.gpsimd.tensor_tensor(bd[:, 1, g], kT[:, 1, g, :].rearrange("p (c k) -> p c k", k=32).unsqueeze(2).to_broadcast([P, NK, G, 32]),
                                                      quadb[:].unsqueeze(1).unsqueeze(3).to_broadcast([P, NK, G, 32]), ALU.mult)
                        ins.then_inc(s["bd_b"], 1)

            @block.tensor
            def _(pe):
                pe.wait_ge(loaded, 16 * n_loads)
                pe.wait_ge(s["prep"], N_PREP)

                def front_x(f):
                    pe.wait_ge(s["xn"], at(f, 1, 1))
                    for t in range(QT):
                        last = nc.tensor.transpose(psum[:, 7, t * P:(t + 1) * P], xn[:, t, :], core.ident[:])
                    last.then_inc(s["xt_ps"], 1)

                def front_q(f):
                    pe.wait_ge(s["xt"], at(f, 1, 1))
                    for t in range(QT):
                        last = nc.tensor.matmul(psum[:, 7, t * P:(t + 1) * P], xnT[:, t * P:(t + 1) * P], wq, start=True, stop=True)
                    last.then_inc(s["q_ps"], 1)

                def front_k(f):
                    pe.wait_ge(s["ctxr"], at(f, 1, 1))
                    pe.wait_ge(s["q_raw"], at(f, 1, 1))
                    for c in range(2):
                        last = nc.tensor.matmul(psum[0:KH, 7, c * D:(c + 1) * D], ctxp[:, c * KH:(c + 1) * KH], wk, start=True, stop=True)
                    last.then_inc(s["k_ps"], 1)

                def front_v(f):
                    for c in range(NK):
                        out = psum[:, 3, c * P:(c + 1) * P] if c < 4 else psum[:, 2, 0:P]
                        last = nc.tensor.matmul(out, ctxr[:, c].rearrange("p j k -> p (j k)"), wv, start=True, stop=rope)
                        if not rope:
                            last = nc.tensor.matmul(out, core.ones[0:1, :], w["bv"][:], start=False, stop=True)
                    last.then_inc(s["v_ps"], 1)

                def front_stacks(f, b=None):
                    pe.wait_ge(s["k_dup"], at(f, 3, 3))
                    pe.wait_ge(s["k_lo"], at(f, 1, 1))
                    for x in range(2):
                        bb = psum[:, 4 + x, :].bitcast(BF16)
                        for g in range(NG):
                            for c in range(2):
                                last = nc.tensor.transpose(bb[:, g * KP + c * KH:g * KP + (c + 1) * KH],
                                                           kst[:, x, c * H + g * G:c * H + (g + 1) * G, :].rearrange("p h r -> p (h r)"),
                                                           core.identb[0:KH, 0:KH])
                        last.then_inc(s["kt_ps"], 1)
                    pe.wait_ge(s["q_dup"], at(f, 3, 3))
                    pe.wait_ge(s["q_lo"], at(f, 1, 1))
                    for x in range(2):
                        if x == 1:
                            pe.wait_ge(s["vbd"], at(f, 1, 1))
                        for gg in range(2):
                            if (x, gg) == (0, 1) and b is not None:
                                pe.wait_ge(s["o"], at(b, NG, NG))
                                pe.wait_ge(s["rs"], at(b, NG, NG))
                            bb = psum[:, 2 * x + gg, :].bitcast(BF16)
                            for g in (2 * gg, 2 * gg + 1):
                                for t in range(QT):
                                    last = nc.tensor.transpose(bb[:, ((g % 2) * QT + t) * P:((g % 2) * QT + t + 1) * P],
                                                               qst[:, x, t * H + g * G:t * H + (g + 1) * G, :].rearrange("p h r -> p (h r)"),
                                                               core.identb[:])
                            last.then_inc(s["qt_ps"], 1)

                def attention(b, f):
                    pe.wait_ge(s["bd_a"], at(b, 1, 1))
                    pe.wait_ge(s["bd_b"], at(b, NG, NG))
                    pe.wait_ge(s["qb"], at(b, 2, 1))

                    def keys_of(x, g, c0, c1):
                        return bd[:, x, g, c0:c1].rearrange("p c j k -> p (c j k)")

                    def score_rounds(g):
                        for t in range(QT):
                            r = g * QT + t
                            if g == 0 and t < 2:
                                pe.wait_ge(s["qa"], at(b, 2, t + 1))
                            if r >= 3:
                                pe.wait_ge(s["mx"], at(b, NG * (QT + 1), g * (QT + 1) + t - 2 if t >= 3 else (g - 1) * (QT + 1) + t + 2))
                            rows = slice(t * P, (t + 1) * P)
                            for x in range(2):
                                last = nc.tensor.matmul(psum[:, r % 3, :], qT[:, x, g, rows], keys_of(x, g, 0, 4), start=(x == 0), stop=(x == 1))
                            if t < QT - 1:
                                last.then_inc(s["sc"], 1)
                                continue
                            last.then_inc(s["sc"], 1)
                            if g:
                                pe.wait_ge(s["mx"], at(b, NG * (QT + 1), g * (QT + 1)))
                            else:
                                pe.wait_ge(s["qb"], at(b, 2, 2))
                            for u in range(QT):
                                rows = slice(u * P, (u + 1) * P)
                                for x in range(2):
                                    last = nc.tensor.matmul(psum[:, 3, rows], qT[:, x, g, rows], keys_of(x, g, 4, 5), start=(x == 0), stop=(x == 1))
                            last.then_inc(s["sc"], 1)

                    def max_rows(g):
                        pe.wait_ge(s["mp"], at(b, NG, g + 1))
                        if g:
                            pe.wait_ge(s["rt"], at(b, NG, g))
                        if g and f is not None:
                            pe.wait_ge(s[(None, "xt", "q_raw", "k_raw")[g]], at(f, 1, 1))
                        bb = psum[:, 7, :].bitcast(BF16)
                        for t in range(QT):
                            last = nc.tensor.transpose(bb[:, t * P:(t + 1) * P],
                                                       qst[:, 0, t * H + g * G:t * H + (g + 1) * G, :].rearrange("p h r -> p (h r)"), core.identb[:])
                        last.then_inc(s["rt_ps"], 1)

                    def scoresT(g, c):
                        n = g * NK + c
                        if c == 0:
                            pe.wait_ge(s["rt"], at(b, NG, g + 1))
                        if n >= 2:
                            pe.wait_ge(s["pt"], at(b, NX, n - 1))
                        for x in range(2):
                            last = nc.tensor.matmul(psum[:, 4 + n % 2, :], keys_of(x, g, c, c + 1), qmT[:, g, :] if x == 0 else qT[:, 1, g, :],
                                                    start=(x == 0), stop=(x == 1))
                        last.then_inc(s["s2"], 1)

                    def values(g, c):
                        n = g * NK + c
                        pe.wait_ge(s["pt"], at(b, NX, n + 1))
                        if c == 0 and g == 0:
                            pe.wait_ge(s["updated"], at(b, 1, 1))
                        if c == 0 and 0 < g < NG - 1:
                            pe.wait_ge(s["o"], at(b, NG, g))
                            pe.wait_ge(s["rs"], at(b, NG, g))
                        last = nc.tensor.matmul(psum[0:2 * G * DK, value_bank(g), :], vbd[:, c * NG + g].rearrange("p a j e -> p (a j e)"), pT[:, n % RING, :],
                                                start=(c == 0), stop=(c == NK - 1))
                        if c == NK - 1:
                            last.then_inc(s["pv"], 1)

                    for i in range(NG + 2):
                        if i < NG:
                            score_rounds(i)
                        if 1 <= i <= NG:
                            max_rows(i - 1)
                        for c in range(NK):
                            if 2 <= i <= NG + 1:
                                values(i - 2, c)
                            if 1 <= i <= NG:
                                scoresT(i - 1, c)
                            if c == 0 and f is not None and 1 <= i <= NG:
                                (front_x, front_q, front_k, front_v)[i - 1](f)
                    if f is not None:
                        pe.wait_ge(s["pt"], at(b, NX, NX))
                        front_stacks(f, b)
                    for t in range(QT):
                        pe.wait_ge(s["on"], at(b, QT, t + 1))
                        last = nc.tensor.matmul(psum[:, 6, t * P:(t + 1) * P], oT[:, t * P:(t + 1) * P], w["wo"][:], start=True, stop=rope)
                        if not rope:
                            last = nc.tensor.matmul(psum[:, 6, t * P:(t + 1) * P], core.ones[0:1, :], w["bo"][:], start=False, stop=True)
                    last.then_inc(s["out"], 1)

                for front in (front_x, front_q, front_k, front_v, front_stacks):
                    front(0)
                with pe.Fori(0, B - 1) as b:
                    attention(b, b + 1)
                attention(B - 1, None)

            @block.scalar
            def _(act):
                stats_s(act)
                act.wait_ge(s["prep"], N_PREP)

                def front_x(f):
                    act.wait_ge(s["xt_ps"], at(f, 1, 1))
                    nc.scalar.activation(xnT[:], psum[:, 7, :], ACT.Copy).then_inc(s["xt"], 1)

                def front_q(f):
                    act.wait_ge(s["q_ps"], at(f, 1, 1))
                    nc.scalar.activation(qf[:].rearrange("p h d -> p (h d)"), psum[:, 7, :], ACT.Copy).then_inc(s["q_raw"], 1)

                def front_k(f):
                    act.wait_ge(s["k_ps"], at(f, 1, 1))
                    nc.scalar.activation(kf[:].rearrange("p h d -> p (h d)"), psum[0:KH, 7, 0:2 * D], ACT.Copy).then_inc(s["k_raw"], 1)

                def front_parts(f, k):
                    x, r, st, hi, mid, fs, hs, rs, ms = ((kf, kr, kst, 0, 8, "k_f", "k_hi", "k_rest", "k_mid"),
                                                         (qf, qr, qst, 0, 16, "q_f", "q_hi", "q_rest", "q_mid"))[k]
                    if rope:
                        rows, cols = ((KH, 2 * H), (P, QT * H))[k]
                        act.wait_ge(s["rms_s"], at(f, 2, k + 1))
                        nc.scalar.activation(ss[0:rows, k, 0:cols], ss[0:rows, k, 0:cols], ACT.Sqrt).then_inc(s["rms_v"], 1)
                    act.wait_ge(s[fs], at(f, 1, 1))
                    nc.scalar.activation(st[:, 0, :, hi:hi + 8], x[:], ACT.Copy).then_inc(s[hs], 1)
                    act.wait_ge(s[rs], at(f, 1, 1))
                    nc.scalar.activation(st[:, 0, :, mid:mid + 8], r[:], ACT.Copy).then_inc(s[ms], 1)

                def front_stacks(f):
                    for x in range(2):
                        act.wait_ge(s["kt_ps"], at(f, 2, x + 1))
                        nc.scalar.activation(kT[:, x].rearrange("p g k -> p (g k)"), psum[:, 4 + x, :].bitcast(BF16)[:, 0:NG * KP],
                                             ACT.Copy).then_inc(s["kt"], 1)
                    for gg in range(2):
                        act.wait_ge(s["qt_ps"], at(f, 4, gg + 1))
                        nc.scalar.activation(qT[:, 0, 2 * gg:2 * gg + 2, :].rearrange("p g q -> p (g q)"),
                                             psum[:, gg, :].bitcast(BF16), ACT.Copy).then_inc(s["qa"], 1)

                def attention(b, f):
                    def products(g):
                        act.wait_ge(s["pv"], at(b, NG, g + 1))
                        nc.scalar.activation(oT[g * G * DK:(g + 1) * G * DK, :], psum[0:G * DK, value_bank(g), :], ACT.Copy).then_inc(s["o"], 1)
                        nc.scalar.activation(rsum[g * G * DK:(g + 1) * G * DK, :], psum[G * DK:2 * G * DK, value_bank(g), :], ACT.Copy).then_inc(s["rs"], 1)

                    for g in range(NG):
                        act.wait_ge(s["rt_ps"], at(b, NG, g + 1))
                        nc.scalar.activation(qmT[:, g, :], psum[:, 7, :].bitcast(BF16)[:, 0:SEQ], ACT.Copy).then_inc(s["rt"], 1)
                        for c in range(NK):
                            n = g * NK + c
                            act.wait_ge(s["s2"], at(b, NX, n + 1))
                            if c == 0 and g >= 2:
                                act.wait_ge(s["pv"], at(b, NG, g - 1))
                            nc.scalar.activation(pT[:, n % RING, :], psum[:, 4 + n % 2, :], ACT.Exp, scale=scale).then_inc(s["pt"], 1)
                            if c == 1 and f is not None and g < 3:
                                (front_x, front_q, front_k)[g](f)
                        if g:
                            products(g - 1)
                    if f is not None:
                        front_parts(f, 0)
                    products(NG - 1)
                    if f is not None:
                        front_parts(f, 1)
                        front_stacks(f)

                for front in (front_x, front_q, front_k):
                    front(0)
                front_parts(0, 0)
                front_parts(0, 1)
                front_stacks(0)
                with act.Fori(0, B - 1) as b:
                    attention(b, b + 1)
                attention(B - 1, None)

            @block.vector
            def _(dve):
                stats_v(dve)
                dve.wait_ge(loaded, 16 * n_loads)
                dve.wait_ge(s["prep"], N_PREP)
                c = Steps(dve, s["prepd"], 0, 0)
                c.n = 3
                if masked:
                    c.step(nc.vector.tensor_copy(m_f[:], w["mask"][:].rearrange("k c b -> k b c")))
                    c.done()
                    c.step(nc.vector.tensor_scalar(pen[:], m_f[:], 1.0, 1e8 / scale, ALU.subtract, ALU.mult))
                    c.done()
                    c.step(nc.vector.tensor_tensor(pen[:], pen[:], w["pad"][:].unsqueeze(1).to_broadcast([KH, B, 2]), ALU.add))
                else:
                    c.step(nc.vector.tensor_copy(pen[:], w["pad"][:].unsqueeze(1).to_broadcast([KH, B, 2])))
                c.done()
                c.step(nc.vector.tensor_copy(pen3[:, :, :, 0], pen[:]))
                c.done()
                c.step(nc.vector.tensor_tensor(pen_r[:], pen[:], pen3[:, :, :, 0], ALU.subtract))
                c.done()
                c.step(nc.vector.tensor_copy(pen3[:, :, :, 1], pen_r[:]))
                c.done()
                c.step(nc.vector.tensor_tensor(pen3[:, :, :, 2], pen_r[:], pen3[:, :, :, 1], ALU.subtract))
                c.step(nc.vector.tensor_copy(vbd[:, :, 1], quad[:].unsqueeze(1).unsqueeze(3).to_broadcast([P, NK * NG, G, DK])))
                c.done()
                nc.vector.memset(neglast[:], 0.0).then_inc(s["updated"], 1)

                def front_x(f):
                    for t in range(QT):
                        n = f * QT + t
                        ins = nc.vector.tensor_scalar(xn[:, t, :], core.resid[:, bass.ds(n, 1), :].rearrange("p a d -> p (a d)"),
                                                      core.stat[:, bass.ds(n, 1), 0:1].rearrange("p a d -> p (a d)"),
                                                      core.rstd[:, bass.ds(n, 1)], ALU.subtract, ALU.mult)
                    ins.then_inc(s["xn"], 1)

                def front_context(f, v):
                    v.step(nc.vector.tensor_scalar(ctxp[:, 0:CTX], core.ctxT[:, bass.ds(f * CTX, CTX)], 1.0, None, ALU.mult))
                    v.done()
                    nc.vector.tensor_copy(ctxr[:], ctxp[:].rearrange("p (c k) -> p c k", k=32).unsqueeze(2).to_broadcast([P, NK, G, 32])).then_inc(s["ctxr"], 1)

                def front_parts(f, v):
                    def rotated(k):
                        x, rows, nt, cs, sn, wn, raw = ((kf, KH, 2, w["kcos"], w["ksin"], w["kn"], "k_raw"),
                                                        (qf, P, QT, w["qcos"], w["qsin"], w["qn"], "q_raw"))[k]
                        nh = nt * H
                        full = [rows, nh, DK]
                        dve.wait_ge(s[raw], at(f, 1, 1))
                        tmp, tmpb = ra[0:rows, 0:nh, :], rb[0:rows, 0:nh, :]
                        v.step(nc.vector.tensor_tensor(tmp, x[:], x[:], ALU.mult))
                        v.done()
                        v.step(nc.vector.tensor_reduce(ss[0:rows, k, 0:nh], tmp, X_AXIS, ALU.add))
                        v.done()
                        nc.vector.tensor_scalar(ss[0:rows, k, 0:nh], ss[0:rows, k, 0:nh], 1.0 / DK, 1e-6, ALU.mult, ALU.add).then_inc(s["rms_s"], 1)
                        dve.wait_ge(s["rms_v"], at(f, 2, k + 1))
                        v.step(nc.vector.reciprocal(ss[0:rows, k, 0:nh], ss[0:rows, k, 0:nh]))
                        v.done()
                        v.step(nc.vector.tensor_tensor(tmp, x[:], ss[0:rows, k, 0:nh].unsqueeze(2).to_broadcast(full), ALU.mult))
                        v.done()
                        v.step(nc.vector.tensor_tensor(x[:], tmp, wn[0:rows, :].unsqueeze(1).to_broadcast(full), ALU.mult))
                        v.done()
                        xv = x[:].rearrange("p (t h) d -> p t h d", h=H)
                        av = tmp.rearrange("p (t h) d -> p t h d", h=H)
                        bv = tmpb.rearrange("p (t h) d -> p t h d", h=H)
                        shape = [rows, nt, H, DK // 2]
                        cb = cs[0:rows, :, :].unsqueeze(2).to_broadcast(shape)
                        sbn = sn[0:rows, :, :].unsqueeze(2).to_broadcast(shape)
                        lo, hi = slice(0, DK // 2), slice(DK // 2, DK)
                        v.step(nc.vector.tensor_tensor(av[:, :, :, lo], xv[:, :, :, lo], cb, ALU.mult))
                        v.step(nc.vector.tensor_tensor(av[:, :, :, hi], xv[:, :, :, hi], cb, ALU.mult))
                        v.step(nc.vector.tensor_tensor(bv[:, :, :, lo], xv[:, :, :, hi], sbn, ALU.mult))
                        v.step(nc.vector.tensor_tensor(bv[:, :, :, hi], xv[:, :, :, lo], sbn, ALU.mult))
                        v.done()
                        v.step(nc.vector.tensor_tensor(xv[:, :, :, lo], av[:, :, :, lo], bv[:, :, :, lo], ALU.subtract))
                        v.done()
                        nc.vector.tensor_tensor(xv[:, :, :, hi], av[:, :, :, hi], bv[:, :, :, hi], ALU.add).then_inc(s["k_f" if k == 0 else "q_f"], 1)
                        dve.wait_ge(s["k_f" if k == 0 else "q_f"], at(f, 1, 1))

                    def split(x, r, st, mid, lo_x, lo, hs, rs, ms, ls):
                        dve.wait_ge(s[hs], at(f, 1, 1))
                        nc.vector.tensor_tensor(r[:], x[:], st[:, 0, :, 0:8], ALU.subtract).then_inc(s[rs], 1)
                        dve.wait_ge(s[ms], at(f, 1, 1))
                        nc.vector.tensor_tensor(st[:, lo_x, :, lo:lo + 8], r[:], st[:, 0, :, mid:mid + 8], ALU.subtract).then_inc(s[ls], 1)

                    v.step(nc.vector.tensor_scalar(kst[:, 0, :, 27:30].rearrange("p (c h) r -> p c h r", h=H),
                                                   pen3[:, bass.ds(f, 1)].rearrange("p o c r -> p (o c) r").unsqueeze(2).to_broadcast([KH, 2, H, 3]),
                                                   1.0, None, ALU.mult))
                    if masked:
                        v.step(nc.vector.tensor_scalar(m_b[:], m_f[:, bass.ds(f, 1)].rearrange("p o c -> p (o c)"), 1.0, None, ALU.mult))
                    if rope:
                        rotated(0)
                    else:
                        dve.wait_ge(s["k_raw"], at(f, 1, 1))
                        kv = kf[:].rearrange("p (c h) d -> p c (h d)", c=2)
                        kb = w["bk"][0:KH, :].unsqueeze(1).to_broadcast([KH, 2, D])
                        if masked:
                            v.step(nc.vector.tensor_tensor(kv, kv, kb, ALU.add))
                            v.done()
                            nc.vector.tensor_tensor(kv, kv, m_b[:].unsqueeze(2).to_broadcast([KH, 2, D]), ALU.mult).then_inc(s["k_f"], 1)
                        else:
                            nc.vector.tensor_tensor(kv, kv, kb, ALU.add).then_inc(s["k_f"], 1)
                        dve.wait_ge(s["k_f"], at(f, 1, 1))
                    split(kf, kr, kst, 8, 1, 8, "k_hi", "k_rest", "k_mid", "k_lo")
                    if rope:
                        rotated(1)
                    else:
                        dve.wait_ge(s["q_raw"], at(f, 1, 1))
                        qv = qf[:].rearrange("p (t h) d -> p t (h d)", h=H)
                        nc.vector.tensor_tensor(qv, qv, w["bq"][:].unsqueeze(1).to_broadcast([P, QT, D]), ALU.add).then_inc(s["q_f"], 1)
                        dve.wait_ge(s["q_f"], at(f, 1, 1))
                    v.step(nc.vector.memset(qst[:, 0, :, 24:27], 0.0))
                    split(qf, qr, qst, 16, 1, 16, "q_hi", "q_rest", "q_mid", "q_lo")

                def front_values(f, v):
                    dve.wait_ge(s["v_ps"], at(f, 1, 1))
                    v.step(nc.vector.tensor_tensor(vbd[:, 0:4 * NG, 0], psum[:, 3, :].rearrange("p (n j d) -> p n j d", j=G, d=DK),
                                                   quad[:].unsqueeze(1).unsqueeze(3).to_broadcast([P, 4 * NG, G, DK]), ALU.mult))
                    v.done()
                    nc.vector.tensor_tensor(vbd[:, 4 * NG:, 0], psum[:, 2, 0:P].rearrange("p (n j d) -> p n j d", j=G, d=DK),
                                            quad[:].unsqueeze(1).unsqueeze(3).to_broadcast([P, NG, G, DK]), ALU.mult).then_inc(s["vbd"], 1)

                def front_stacks(f):
                    dve.wait_ge(s["kt"], at(f, 2, 1))
                    for g in range(NG):
                        ins = nc.vector.tensor_tensor(bd[:, 0, g], kT[:, 0, g, :].rearrange("p (c k) -> p c k", k=32).unsqueeze(2).to_broadcast([P, NK, G, 32]),
                                                      quadb[:].unsqueeze(1).unsqueeze(3).to_broadcast([P, NK, G, 32]), ALU.mult)
                    ins.then_inc(s["bd_a"], 1)
                    for gg in range(2):
                        dve.wait_ge(s["qt_ps"], at(f, 4, 3 + gg))
                        nc.vector.tensor_copy(qT[:, 1, 2 * gg:2 * gg + 2, :].rearrange("p g q -> p (g q)"),
                                              psum[:, 2 + gg, :].bitcast(BF16)).then_inc(s["qb"], 1)

                def attention(b, f):
                    v = Steps(dve, s["vec"], DVE_STEPS, b)
                    fv = None if f is None else Steps(dve, s["fvec"], FRONT_STEPS, f)
                    def maxima(g):
                        for t in range(QT):
                            dve.wait_ge(s["sc"], at(b, NG * (QT + 1), g * (QT + 1) + t + 1))
                            nc.vector.tensor_reduce(negmax[:, t, g * G:(g + 1) * G], psum[:, (g * QT + t) % 3, :].rearrange("p (c j k) -> p j c k", j=G, k=32),
                                                    mybir.AxisListType.XY, ALU.max, negate=True).then_inc(s["mx"], 1)
                        dve.wait_ge(s["sc"], at(b, NG * (QT + 1), (g + 1) * (QT + 1)))
                        nc.vector.tensor_reduce(neglast[:], psum[:, 3, :].rearrange("p (t j k) -> p t j k", j=G, k=32),
                                                X_AXIS, ALU.max, negate=True).then_inc(s["mx"], 1)
                        dve.wait_ge(s["mx"], at(b, NG * (QT + 1), (g + 1) * (QT + 1)))
                        nm = negmax[:, :, g * G:(g + 1) * G]
                        v.step(nc.vector.tensor_tensor(nm, nm, neglast[:], ALU.min))
                        v.done()
                        st = qst[:, 0].rearrange("p (t h) r -> p t h r", h=H)[:, :, g * G:(g + 1) * G, :]
                        v.step(nc.vector.tensor_copy(st[:, :, :, 24], nm))
                        v.done()
                        v.step(nc.vector.tensor_tensor(rest[:], nm, st[:, :, :, 24], ALU.subtract))
                        v.done()
                        v.step(nc.vector.tensor_copy(st[:, :, :, 25], rest[:]))
                        v.done()
                        nc.vector.tensor_tensor(st[:, :, :, 26], rest[:], st[:, :, :, 25], ALU.subtract).then_inc(s["mp"], 1)

                    for g in range(NG):
                        maxima(g)
                        if f is not None and g == 0:
                            front_x(f)
                        if f is not None and g == 1:
                            front_context(f, fv)
                    if f is not None:
                        front_parts(f, fv)
                        dve.wait_ge(s["pv"], at(b, NG, NG))
                        front_values(f, fv)
                    dve.wait_ge(s["rs"], at(b, NG, NG))
                    dve.wait_ge(s["o"], at(b, NG, NG))
                    r0 = v.n
                    for t in range(QT):
                        rows = slice(t * P, (t + 1) * P)
                        v.step(nc.vector.reciprocal(rsum[:, rows], rsum[:, rows]))
                    for t in range(QT):
                        rows = slice(t * P, (t + 1) * P)
                        v.done(r0 + t + 1)
                        nc.vector.tensor_tensor(oT[:, rows], oT[:, rows], rsum[:, rows], ALU.mult).then_inc(s["on"], 1)
                    if f is not None:
                        front_stacks(f)
                        fv.close()
                    dve.wait_ge(s["out"], at(b, 1, 1))
                    update_rows(core, v, b, psum[:, 6, :], gate, new, parts, mv)
                    nc.vector.memset(neglast[:], 0.0).then_inc(s["updated"], 1)
                    v.close()

                fv = Steps(dve, s["fvec"], FRONT_STEPS, 0)
                front_x(0)
                front_context(0, fv)
                front_parts(0, fv)
                front_values(0, fv)
                front_stacks(0)
                fv.close()
                with dve.Fori(0, B - 1) as b:
                    attention(b, b + 1)
                attention(B - 1, None)



def experts(core, L, w, gate, E, items, loaded, n_loads, glu, capacity=0, biased=False, extra=None, x1=None):
    nc, psum = core.nc, core.psum
    NC = E + (extra is not None)
    NL = E + (extra == "sigmoid")
    NI = len(items)
    NUN = sum(len(u) for u, _ in items)
    ND = sum(len(d) for _, d in items) + biased
    MU = max(len(u) for u, _ in items)
    RING = 2 * MU
    SETS = 2 if glu else 4
    first_unit = [sum(len(u) for u, _ in items[:i]) for i in range(NI + 1)]
    first_down = [biased + sum(len(d) for _, d in items[:i]) for i in range(NI + 1)]
    STEPS = 28 + (2 if extra == "sigmoid" else 0) + (2 if capacity else 0)
    s = {n: nc.alloc_semaphore(f"{L}_{n}") for n in (
        "var", "sd", "vec", "xn", "xt_ps", "xt", "lg_ps", "gap", "th", "mask", "rank_ps", "comb", "ct_ps", "ct",
        "up", "silu", "hid", "down", "acc", "const")}

    with ExitStack() as scope:
        def sb(name, shape, dt=F32):
            return scope.enter_context(nc.sbuf_tensor(f"{L}_{name}", shape, dt))

        xn = sb("xn", [P, QT, D])
        xnT = sb("xnT", [P, SEQ])
        lg = sb("lg", [P, QT, NL])
        lg2 = sb("lg2", [P, QT, E])
        eq = sb("eq", [P, QT, E])
        score = sb("score", [P, QT, E])
        rev = sb("rev", [P, E])
        oh = sb("oh", [P, 2, QT, E])
        top = sb("top", [P, 2, QT])
        pick = sb("pick", [P, QT])
        gap = sb("gap", [P, 2, QT])
        wt = sb("wt", [P, 2, QT])
        comb = sb("comb", [P, QT, NC])
        acc = sb("acc", [P, QT, D])
        new = sb("new", [P, QT, D])
        parts = sb("parts", [P, QT, 6])
        mv = sb("mv", [P, QT, 2])
        hid = sb("hid", [P, RING, SEQ])
        if glu:
            sg = sb("sg", [P, 2, SEQ])
        if capacity:
            mask = sb("mask", [P, QT, E], BF16)
            before = sb("before", [P, E], BF16)
            tri = sb("tri", [P, P], BF16)
            picks = sb("picks", [P, E])
        if biased:
            cT = sb("cT", [E, SEQ])
        stats_v, stats_s = rows_rstd(core, L, s["var"], s["sd"], rms=x1 is not None)

        with nc.Block() as block:

            @block.gpsimd
            def _(pool):
                for e in range(E):
                    nc.gpsimd.memset(rev[:, e:e + 1], float(E - e)).then_inc(s["const"], 1)
                n = E
                if extra == "one":
                    nc.gpsimd.memset(comb[:], 1.0).then_inc(s["const"], 1)
                    n += 1
                if capacity:
                    nc.gpsimd.memset(tri[:], 1.0).then_inc(s["const"], 1)
                    nc.gpsimd.memset(before[:], 0.0).then_inc(s["const"], 1)
                    n += 2
                    pool.wait_ge(s["const"], n)
                    nc.gpsimd.affine_select(out=tri[:], in_=tri[:], compare_op=ALU.is_ge, fill=0.0, base=0,
                                            pattern=[[1, P]], channel_multiplier=-1).then_inc(s["const"], 1)

            n_const = E + (extra == "one") + (3 if capacity else 0)

            @block.tensor
            def _(pe):
                pe.wait_ge(loaded, 16 * n_loads)
                pe.wait_ge(s["const"], n_const)
                with pe.Fori(0, B) as b:
                    def router():
                        pe.wait_ge(s["xn"], at(b, 1, 1))
                        for t in range(QT):
                            last = nc.tensor.transpose(psum[:, 7, t * P:(t + 1) * P], xn[:, t, :], core.ident[:])
                        last.then_inc(s["xt_ps"], 1)
                        pe.wait_ge(s["xt"], at(b, 1, 1))
                        for t in range(QT):
                            out = psum[:, 7, t * NL:(t + 1) * NL]
                            last = nc.tensor.matmul(out, xnT[:, t * P:(t + 1) * P], w["gate"][:], start=True, stop="gate_b" not in w)
                            if "gate_b" in w:
                                last = nc.tensor.matmul(out, core.ones[0:1, :], w["gate_b"][:], start=False, stop=True)
                        last.then_inc(s["lg_ps"], 1)

                    def ranks():
                        pe.wait_ge(s["mask"], at(b, 1, 1))
                        for t in range(QT):
                            out = psum[:, 7, t * E:(t + 1) * E]
                            nc.tensor.matmul(out, tri[:], mask[:, t, :], start=True, stop=False)
                            for k in range(t):
                                nc.tensor.matmul(out, core.oneb[:], mask[:, k, :], start=False, stop=False)
                            last = nc.tensor.matmul(out, core.oneb[:], before[:], start=False, stop=True)
                        last.then_inc(s["rank_ps"], 1)

                    def second_biases():
                        pe.wait_ge(s["comb"], at(b, 1, 1))
                        for t in range(QT):
                            last = nc.tensor.transpose(psum[0:E, 7, t * P:(t + 1) * P], comb[:, t, 0:E], core.ident[:])
                        last.then_inc(s["ct_ps"], 1)
                        pe.wait_ge(s["ct"], at(b, 1, 1))
                        for t in range(QT):
                            last = nc.tensor.matmul(psum[:, 4, t * P:(t + 1) * P], cT[:, t * P:(t + 1) * P], w["b2"][:],
                                                    start=True, stop=True)
                        last.then_inc(s["down"], 1)

                    def up(i):
                        for k, (wg, wu, rows, _) in enumerate(items[i][0]):
                            n = first_unit[i] + k
                            if n >= SETS:
                                pe.wait_ge(s["hid"], at(b, NUN, n - SETS + 1))
                            if glu:
                                nc.tensor.matmul(psum[0:rows, 2 * (n % 2), :], wg, xnT[:], start=True, stop=True)
                                last = nc.tensor.matmul(psum[0:rows, 2 * (n % 2) + 1, :], wu, xnT[:], start=True, stop=True)
                            else:
                                last = nc.tensor.matmul(psum[0:rows, n % 4, :], wg, xnT[:], start=True, stop=True)
                            last.then_inc(s["up"], 1)

                    def down(i):
                        for k, (_, terms) in enumerate(items[i][1]):
                            n = first_down[i] + k
                            if k == 0:
                                pe.wait_ge(s["hid"], at(b, NUN, first_unit[i + 1]))
                            if n >= 3:
                                pe.wait_ge(s["acc"], at(b, ND, n - 2))
                            for t in range(QT):
                                for m, (u, rows, w2) in enumerate(terms):
                                    slot = (first_unit[i] + u) % RING
                                    last = nc.tensor.matmul(psum[:, 4 + n % 3, t * P:(t + 1) * P],
                                                            hid[rows, slot, t * P:(t + 1) * P], w2,
                                                            start=(m == 0), stop=(m == len(terms) - 1))
                            last.then_inc(s["down"], 1)

                    router()
                    up(0)
                    if capacity:
                        ranks()
                    for i in range(NI):
                        if i + 1 < NI:
                            up(i + 1)
                        if i == 0 and biased:
                            second_biases()
                        down(i)

            @block.scalar
            def _(act):
                stats_s(act)
                act.wait_ge(loaded, 16 * n_loads)
                with act.Fori(0, B) as b:
                    act.wait_ge(s["xt_ps"], at(b, 1, 1))
                    nc.scalar.activation(xnT[:], psum[:, 7, :], ACT.Copy).then_inc(s["xt"], 1)

                    def unit(i, k):
                        _, _, rows, bias = items[i][0][k]
                        n = first_unit[i] + k
                        act.wait_ge(s["up"], at(b, NUN, n + 1))
                        if glu:
                            if n >= 2:
                                act.wait_ge(s["hid"], at(b, NUN, n - 1))
                            nc.scalar.activation(sg[0:rows, n % 2, :], psum[0:rows, 2 * (n % 2), :], ACT.Silu).then_inc(s["silu"], 1)
                        else:
                            if k == 0 and i >= 2:
                                act.wait_ge(s["down"], at(b, ND, first_down[i - 1]))
                            nc.scalar.activation(hid[0:rows, n % RING, :], psum[0:rows, n % 4, :], ACT.Relu,
                                                 bias=bias).then_inc(s["hid"], 1)

                    for k in range(len(items[0][0])):
                        unit(0, k)
                    act.wait_ge(s["gap"], at(b, 1, 1))
                    nc.scalar.activation(gap[:], gap[:], ACT.Tanh, scale=0.5).then_inc(s["th"], 1)
                    for i in range(1, NI):
                        for k in range(len(items[i][0])):
                            unit(i, k)

            @block.vector
            def _(dve):
                stats_v(dve)
                dve.wait_ge(loaded, 16 * n_loads)
                dve.wait_ge(s["const"], n_const)
                if extra != "sigmoid":
                    nc.vector.memset(gap[:], 0.0).then_inc(s["var"], 1)
                    dve.wait_ge(s["var"], 3)

                def front(f):
                    for t in range(QT):
                        n = f * QT + t
                        if x1 is None:
                            ins = nc.vector.tensor_scalar(xn[:, t, :], core.resid[:, bass.ds(n, 1), :].rearrange("p a d -> p (a d)"),
                                                          core.stat[:, bass.ds(n, 1), 0:1].rearrange("p a d -> p (a d)"),
                                                          core.rstd[:, bass.ds(n, 1)], ALU.subtract, ALU.mult)
                        else:
                            ins = nc.vector.scalar_tensor_tensor(out=xn[:, t, :], in0=x1[:, bass.ds(n, 1), :].rearrange("p a d -> p (a d)"),
                                                                 scalar=core.rstd[:, bass.ds(n, 1)], in1=w["ln2"][:],
                                                                 op0=ALU.mult, op1=ALU.mult)
                    ins.then_inc(s["xn"], 1)

                def mixture(b, f):
                    v = Steps(dve, s["vec"], STEPS, b)
                    dve.wait_ge(s["lg_ps"], at(b, 1, 1))
                    v.step(nc.vector.tensor_copy(lg[:], psum[:, 7, 0:QT * NL].rearrange("p (t e) -> p t e", e=NL)))
                    v.done()
                    le = lg[:, :, 0:E]
                    revb = rev[:].unsqueeze(1).to_broadcast([P, QT, E])

                    def across(x):
                        return x.unsqueeze(2).to_broadcast([P, QT, E])

                    src = le
                    for r in range(2):
                        v.step(nc.vector.tensor_reduce(top[:, r, :], src, X_AXIS, ALU.max))
                        v.done()
                        v.step(nc.vector.tensor_tensor(eq[:], src, across(top[:, r, :]), ALU.is_equal))
                        v.done()
                        v.step(nc.vector.tensor_tensor(score[:], eq[:], revb, ALU.mult))
                        v.done()
                        v.step(nc.vector.tensor_reduce(pick[:], score[:], X_AXIS, ALU.max))
                        v.done()
                        v.step(nc.vector.tensor_tensor(oh[:, r, :, :], revb, across(pick[:]), ALU.is_equal))
                        v.done()
                        if r == 0:
                            v.step(nc.vector.scalar_tensor_tensor(out=lg2[:], in0=oh[:, 0, :, :], scalar=-3e38, in1=le,
                                                                  op0=ALU.mult, op1=ALU.add))
                            v.done()
                            src = lg2[:]
                    if capacity:
                        v.step(nc.vector.tensor_tensor(mask[:], oh[:, 0, :, :], oh[:, 1, :, :], ALU.add))
                        v.done()
                        nc.vector.tensor_reduce(picks[:], mask[:].rearrange("p t e -> p e t"), X_AXIS, ALU.add).then_inc(s["mask"], 1)
                    if extra == "sigmoid":
                        v.step(nc.vector.tensor_copy(gap[:, 1, :], lg[:, :, E]))
                    nc.vector.tensor_tensor(gap[:, 0, :], top[:, 0, :], top[:, 1, :], ALU.subtract).then_inc(s["gap"], 1)
                    dve.wait_ge(s["th"], at(b, 1, 1))
                    v.step(nc.vector.tensor_scalar(wt[:, 0, :], gap[:, 0, :], 0.5, 0.5, ALU.mult, ALU.add))
                    v.step(nc.vector.tensor_scalar(wt[:, 1, :], gap[:, 0, :], -0.5, 0.5, ALU.mult, ALU.add))
                    v.done()
                    v.step(nc.vector.tensor_tensor(eq[:], oh[:, 0, :, :], across(wt[:, 0, :]), ALU.mult))
                    v.step(nc.vector.tensor_tensor(score[:], oh[:, 1, :, :], across(wt[:, 1, :]), ALU.mult))
                    v.done()
                    if extra == "sigmoid":
                        v.step(nc.vector.tensor_scalar(comb[:, :, E], gap[:, 1, :], 0.5, 0.5, ALU.mult, ALU.add))
                    v.step(nc.vector.tensor_tensor(comb[:, :, 0:E], eq[:], score[:], ALU.add))
                    v.done()
                    if capacity:
                        dve.wait_ge(s["rank_ps"], at(b, 1, 1))
                        v.step(nc.vector.tensor_scalar(eq[:], psum[:, 7, 0:QT * E].rearrange("p (t e) -> p t e", e=E),
                                                       float(capacity), None, ALU.is_le))
                        v.done()
                        nc.vector.tensor_tensor(before[:], before[:], picks[:], ALU.add)
                        nc.vector.tensor_tensor(comb[:], comb[:], eq[:], ALU.mult).then_inc(s["comb"], 1)
                        dve.wait_ge(s["comb"], at(b, 1, 1))
                    if biased:
                        dve.wait_ge(s["ct_ps"], at(b, 1, 1))
                        nc.vector.tensor_copy(cT[:], psum[0:E, 7, :]).then_inc(s["ct"], 1)

                    def product(i):
                        for k, (_, _, rows, _) in enumerate(items[i][0]):
                            n = first_unit[i] + k
                            dve.wait_ge(s["silu"], at(b, NUN, n + 1))
                            if k == 0 and i >= 2:
                                dve.wait_ge(s["down"], at(b, ND, first_down[i - 1]))
                            nc.vector.tensor_tensor(hid[0:rows, n % RING, :], sg[0:rows, n % 2, :],
                                                    psum[0:rows, 2 * (n % 2) + 1, :], ALU.mult).then_inc(s["hid"], 1)

                    def accumulate(n, col):
                        dve.wait_ge(s["down"], at(b, ND, n + 1))
                        if n:
                            dve.wait_ge(s["acc"], at(b, ND, n))
                        for t in range(QT):
                            ps = psum[:, 4 + n % 3, t * P:(t + 1) * P]
                            if col is None:
                                ins = nc.vector.tensor_copy(acc[:, t, :], ps)
                            elif n or x1 is not None:
                                base = acc[:, t, :] if n else x1[:, bass.ds(b * QT + t, 1), :].rearrange("p a d -> p (a d)")
                                ins = nc.vector.scalar_tensor_tensor(out=acc[:, t, :], in0=ps, scalar=comb[:, t, col:col + 1],
                                                                     in1=base, op0=ALU.mult, op1=ALU.add)
                            else:
                                ins = nc.vector.tensor_scalar(acc[:, t, :], ps, comb[:, t, col:col + 1], None, ALU.mult)
                        ins.then_inc(s["acc"], 1)

                    if glu:
                        product(0)
                    if biased:
                        accumulate(0, None)
                    for i in range(NI):
                        if glu and i + 1 < NI:
                            product(i + 1)
                        if f is not None and i == NI - 1:
                            front(f)
                        for k, (col, _) in enumerate(items[i][1]):
                            accumulate(first_down[i] + k, col)
                    dve.wait_ge(s["acc"], at(b, ND, ND))
                    update_rows(core, v, b, acc[:].rearrange("p t d -> p (t d)"), gate, new, parts, mv)
                    v.close()

                front(0)
                with dve.Fori(0, B - 1) as b:
                    mixture(b, b + 1)
                mixture(B - 1, None)


def causal_attention(core, L, w, x1, loaded, n_loads):
    nc, psum = core.nc, core.psum
    DK, NOPE, ROPE, R = 64, 32, 32, 16
    G, NG = 2, 8
    HB = P // NOPE
    PV_BANKS = 4
    LAG, RING = 1, 8
    scale = float(DK) ** -0.5
    NR = NG * QT
    s = {n: nc.alloc_semaphore(f"{L}_{n}") for n in (
        "var", "sd", "vec", "fvec", "ms", "rms", "xr", "proj", "freed", "freed_v", "qrot", "krot", "kfull", "sc", "mx", "mp", "mt_ps", "mt",
        "s2", "pt", "pv", "o", "rs", "on", "out", "const")}
    units = [("x", 0), ("lat", 0), ("kr", 0)] + [("kv", t) for t in range(QT)]
    units += [("q", (t, h)) for t in range(QT) for h in range(2)]
    units += [("kt", g) for g in range(NG)] + [("qt", g) for g in range(NG)]
    NUNIT = len(units)
    NFREED = NUNIT - NG // 2

    def freed_by(n):
        return n + 1 - max(0, n - units.index(("qt", 0)) + 1) // 2

    NS2 = H * QT
    STEPS = 64
    FRONT_STEPS = 14

    with ExitStack() as scope:
        def sb(name, shape, dt=F32):
            return scope.enter_context(nc.sbuf_tensor(f"{L}_{name}", shape, dt))

        y = sb("y", [P, QT, D])
        xr = sb("xr", [P, QT, D])
        xrT = sb("xrT", [P, SEQ])
        lat = sb("lat", [R, SEQ])
        krow = sb("krow", [P, QT, ROPE])
        krr = sb("krr", [P, QT, ROPE])
        qwork = sb("qwork", [P, RING * SEQ])
        qp = qwork[:].rearrange("p (t h e) -> p t h e", t=QT, e=DK)
        pT = qwork[:].rearrange("p (r q) -> p r q", q=SEQ)
        kwork = View(core.projections[:].rearrange("p a e -> p (a e)"))
        kp = kwork[:].rearrange("p (t h e) -> p t h e", t=QT, e=DK)
        oT = kwork[:, 0:H * NOPE // P * SEQ].rearrange("p (c q) -> p c q", q=SEQ)
        qT = sb("qT", [P, NG, SEQ])
        kT = sb("kT", [P, NG, G, SEQ])
        va = core.spare[0][:].rearrange("p e f -> p (e f)").rearrange("p (t h a e) -> p t h a e", t=QT, h=H, a=2)
        pick = sb("pick", [P, G, P], BF16)
        ra = sb("ra", [P, 2, H, ROPE // 2])
        rb = sb("rb", [P, 2, H, ROPE // 2])
        negmax = sb("negmax", [P, QT, H])
        rest = sb("rest", [P, QT, H])
        mparts = sb("mparts", [P, QT, H, DK], BF16)
        mT = core.spare[1][:].rearrange("p e c d -> p (e c d)").bitcast(BF16).rearrange("p (g q) -> p g q", q=SEQ)
        rsum = sb("rsum", [P, 2, SEQ])
        parts = sb("parts", [P, QT, 6])
        mv = sb("mv", [P, QT, 2])
        ms = sb("ms", [P, QT])
        new = sb("new", [P, QT, D])
        future = sb("future", [P, P], BF16)
        futureT = sb("futureT", [P, P], BF16)
        unit = sb("unit", [P, ROPE])
        stats_v, stats_s = rows_rstd(core, L, s["var"], s["sd"])

        with nc.Block() as block:

            @block.gpsimd
            def _(pool):
                nc.gpsimd.memset(mparts[:], 0.0).then_inc(s["const"], 1)
                nc.gpsimd.memset(va[:], 1.0).then_inc(s["const"], 1)
                nc.gpsimd.memset(future[:], 0.0).then_inc(s["const"], 1)
                nc.gpsimd.memset(futureT[:], 0.0).then_inc(s["const"], 1)
                nc.gpsimd.memset(unit[:], 1.0).then_inc(s["const"], 1)
                nc.gpsimd.memset(kT[:], 0.0).then_inc(s["const"], 1)
                nc.gpsimd.memset(pick[:], 0.0).then_inc(s["const"], 1)
                for j in range(G):
                    pool.wait_ge(s["const"], 7 + j)
                    nc.gpsimd.memset(pick[DK * j:DK * j + DK, j, :], 1.0).then_inc(s["const"], 1)
                pool.wait_ge(s["const"], 7 + G)
                nc.gpsimd.affine_select(out=future[:], in_=future[:], compare_op=ALU.is_ge, fill=-1e30, base=0,
                                        pattern=[[-1, P]], channel_multiplier=1).then_inc(s["const"], 1)
                nc.gpsimd.affine_select(out=futureT[:], in_=futureT[:], compare_op=ALU.is_ge, fill=-1e30, base=0,
                                        pattern=[[1, P]], channel_multiplier=-1).then_inc(s["const"], 1)
                with pool.Fori(0, B) as b:
                    pool.wait_ge(s["krot"], at(b, 1, 1))
                    nc.gpsimd.tensor_tensor(kp[:, :, :, NOPE:DK], krr[:].unsqueeze(2).to_broadcast([P, QT, H, ROPE]),
                                            unit[:].unsqueeze(1).unsqueeze(1).to_broadcast([P, QT, H, ROPE]), ALU.mult).then_inc(s["kfull"], 1)

            @block.tensor
            def _(pe):
                pe.wait_ge(loaded, 16 * n_loads)
                pe.wait_ge(s["const"], 9 + G)
                with pe.Fori(0, B) as b:
                    pe.wait_ge(s["xr"], at(b, 1, 1))

                    def bank_read(n):
                        what, a = units[n]
                        if what != "qt" or a % 2 == 0:
                            pe.wait_ge(s["freed"], at(b, NFREED, freed_by(n)))
                        if what in ("kt", "qt"):
                            pe.wait_ge(s["freed_v"], at(b, NG + NG // 2, a + 1 if what == "kt" else NG + (a + 1) // 2))

                    for n, (what, a) in enumerate(units):
                        out = psum[:, n % 4, :]
                        if what == "lat":
                            pe.wait_ge(s["freed"], at(b, NFREED, 1))
                        if n >= 4:
                            bank_read(n - 4)
                        if what == "x":
                            for t in range(QT):
                                last = nc.tensor.transpose(out[:, t * P:(t + 1) * P], xr[:, t, :], core.ident[:])
                        elif what == "lat":
                            last = nc.tensor.matmul(out[0:R, :], w["wkva"][:, 0:R], xrT[:], start=True, stop=True)
                        elif what == "kr":
                            for t in range(QT):
                                last = nc.tensor.matmul(out[:, t * ROPE:(t + 1) * ROPE], xrT[:, t * P:(t + 1) * P],
                                                        w["wkva"][:, R:R + ROPE], start=True, stop=True)
                        elif what == "kv":
                            if a == 0:
                                pe.wait_ge(s["freed"], at(b, NFREED, 2))
                            last = nc.tensor.matmul(out, lat[:, a * P:(a + 1) * P], w["wkvb"][:], start=True, stop=True)
                        elif what == "q":
                            t, h = a
                            last = nc.tensor.matmul(out, xrT[:, t * P:(t + 1) * P], w["wq"][:, h * 512:(h + 1) * 512],
                                                    start=True, stop=True)
                        else:
                            if a == 0:
                                pe.wait_ge(s["kfull" if what == "kt" else "qrot"], at(b, 1, 1) if what == "kt" else at(b, QT, QT))
                                if what == "kt":
                                    pe.wait_ge(s["freed"], at(b, NFREED, 7))
                            src = kp if what == "kt" else qp
                            for t in range(QT):
                                last = nc.tensor.transpose(out[:, t * P:(t + 1) * P],
                                                           src[:, t, a * G:(a + 1) * G, :].rearrange("p h e -> p (h e)"), core.ident[:])
                        last.then_inc(s["proj"], 1)
                    pe.wait_ge(s["freed"], at(b, NFREED, NFREED))
                    pe.wait_ge(s["freed_v"], at(b, NG + NG // 2, NG + NG // 2))

                    for g in range(NG):
                        for t in range(QT):
                            r = g * QT + t
                            n = (t + 1) * P
                            if r >= 3:
                                pe.wait_ge(s["mx"], at(b, NR, r - 2))
                            for j in range(G):
                                bk = 2 * (r % 3) + j
                                nc.tensor.matmul(psum[:, bk, 0:n], qT[:, g, t * P:n], kT[:, g, j, 0:n],
                                                 start=True, stop=True)
                            for j in range(G):
                                bk = 2 * (r % 3) + j
                                last = nc.tensor.matmul(psum[:, bk, t * P:n], core.identb[:], future[:], start=False, stop=True,
                                                        skip_group_check=True)
                            last.then_inc(s["sc"], 1)
                    for k in range(NG // 2):
                        if k % 2 == 0:
                            pe.wait_ge(s["mp"], at(b, 2, k // 2 + 1))
                        if k:
                            pe.wait_ge(s["mt"], at(b, NG // 2, k))
                        bb = psum[:, 7, :].bitcast(BF16)
                        for gg in range(2):
                            g = 2 * k + gg
                            for t in range(QT):
                                last = nc.tensor.transpose(bb[:, (gg * QT + t) * P:(gg * QT + t + 1) * P],
                                                           mparts[:, t, g * G:(g + 1) * G, :].rearrange("p h s -> p (h s)"), core.identb[:])
                        last.then_inc(s["mt_ps"], 1)
                    pe.wait_ge(s["mt"], at(b, NG // 2, NG // 2))

                    def scoresT(h):
                        g, j = h // G, h % G
                        for k in range(QT):
                            n = h * QT + k
                            q0 = k * P
                            if n >= 3:
                                pe.wait_ge(s["pt"], at(b, NS2, n - 2))
                            out = psum[:, 4 + n % 3, q0:SEQ]
                            nc.tensor.matmul(out, kT[:, g, j, q0:q0 + P], qT[:, g, q0:SEQ], start=True, stop=False)
                            nc.tensor.matmul(out, pick[:, j, :], mT[:, g, q0:SEQ], start=False, stop=True)
                            nc.tensor.matmul(psum[:, 4 + n % 3, q0:q0 + P], core.identb[:], futureT[:], start=False, stop=True,
                                             skip_group_check=True).then_inc(s["s2"], 1)

                    def values(h):
                        pe.wait_ge(s["pt"], at(b, NS2, (h + 1) * QT))
                        if h >= PV_BANKS:
                            pe.wait_ge(s["o"], at(b, H, h - PV_BANKS + 1))
                            pe.wait_ge(s["rs"], at(b, H, h - PV_BANKS + 1))
                        for k in range(QT):
                            last = nc.tensor.matmul(psum[0:2 * NOPE, h % PV_BANKS, k * P:SEQ], va[:, k, h].rearrange("p a e -> p (a e)"),
                                                    pT[:, (h * QT + k) % RING, k * P:SEQ], start=(k == 0), stop=(k == QT - 1),
                                                    skip_group_check=True)
                        last.then_inc(s["pv"], 1)

                    for h in range(H + LAG):
                        if h < H:
                            scoresT(h)
                        if h >= LAG:
                            values(h - LAG)
                    for c in range(H // HB):
                        pe.wait_ge(s["on"], at(b, H // HB, c + 1))
                        for t in range(QT):
                            last = nc.tensor.matmul(psum[:, 7, t * P:(t + 1) * P], oT[:, c, t * P:(t + 1) * P],
                                                    w["wo"][:, c, :], start=(c == 0 and t == 0), stop=(c == 3), skip_group_check=True)
                    last.then_inc(s["out"], 1)

            @block.scalar
            def _(act):
                stats_s(act)
                act.wait_ge(s["const"], 9 + G)
                with act.Fori(0, B) as b:
                    act.wait_ge(s["ms"], at(b, 1, 1))
                    nc.scalar.activation(ms[:], ms[:], ACT.Sqrt).then_inc(s["rms"], 1)
                    for n, (what, a) in enumerate(units):
                        src = psum[:, n % 4, :]
                        if what == "qt" and a % 2:
                            continue
                        act.wait_ge(s["proj"], at(b, NUNIT, n + 1))
                        if what == "x":
                            ins = nc.scalar.activation(xrT[:], src, ACT.Copy)
                        elif what == "lat":
                            ins = nc.scalar.activation(lat[:], src[0:R, :], ACT.Copy)
                        elif what == "kr":
                            ins = nc.scalar.activation(krow[:].rearrange("p t e -> p (t e)"), src[:, 0:QT * ROPE], ACT.Copy)
                        elif what == "kv":
                            kv = src.rearrange("p (h e) -> p h e", e=NOPE)
                            nc.scalar.activation(kp[:, a, :, 0:NOPE], kv, ACT.Copy)
                            ins = nc.scalar.activation(va[:, a, :, 0, :], kv, ACT.Copy)
                        elif what == "q":
                            t, h = a
                            ins = nc.scalar.activation(qp[:, t, 8 * h:8 * h + 8, :], src.rearrange("p (h e) -> p h e", e=DK), ACT.Copy)
                        elif what == "kt":
                            ins = nc.scalar.activation(kT[0:DK, a, 0, :], src[0:DK, :], ACT.Copy)
                        else:
                            ins = nc.scalar.activation(qT[:, a, :], src, ACT.Copy)
                        ins.then_inc(s["freed"], 1)

                    def sums(h):
                        act.wait_ge(s["pv"], at(b, H, h + 1))
                        if h >= 2 * HB and h % HB == 0:
                            act.wait_ge(s["on"], at(b, H // HB, h // HB - 1))
                        r0 = NOPE * (h % HB)
                        nc.scalar.activation(rsum[r0:r0 + NOPE, (h // HB) % 2, :], psum[NOPE:2 * NOPE, h % PV_BANKS, :],
                                             ACT.Copy).then_inc(s["rs"], 1)

                    for h in range(H):
                        for k in range(QT):
                            n = h * QT + k
                            act.wait_ge(s["s2"], at(b, NS2, n + 1))
                            if k == 0 and h > LAG:
                                act.wait_ge(s["pv"], at(b, H, h - LAG))
                            nc.scalar.activation(pT[:, n % RING, k * P:SEQ], psum[:, 4 + n % 3, k * P:SEQ], ACT.Exp, scale=scale).then_inc(s["pt"], 1)
                        if h > LAG:
                            sums(h - LAG - 1)
                    for h in range(H - LAG - 1, H):
                        sums(h)

            @block.vector
            def _(dve):
                stats_v(dve)
                dve.wait_ge(loaded, 16 * n_loads)
                def front(f, v):
                    for t in range(QT):
                        n = f * QT + t
                        v.step(nc.vector.tensor_scalar(y[:, t, :], core.resid[:, bass.ds(n, 1), :].rearrange("p a d -> p (a d)"),
                                                       core.stat[:, bass.ds(n, 1), 0:1].rearrange("p a d -> p (a d)"),
                                                       core.rstd[:, bass.ds(n, 1)], ALU.subtract, ALU.mult))
                    v.done()
                    for t in range(QT):
                        v.step(nc.vector.bn_stats(parts[:, t, :], y[:, t, :]))
                    v.done()
                    nc.vector.memset(rest[:, 0, 0:1], 0.0)
                    for t in range(QT):
                        v.step(nc.vector.bn_aggr(mv[:, t, :], parts[:, t, :]))
                    v.done()
                    v.step(nc.vector.tensor_tensor(ms[:], mv[:, :, 0], mv[:, :, 0], ALU.mult))
                    v.done()
                    nc.vector.scalar_tensor_tensor(out=ms[:], in0=ms[:], scalar=LN_EPS, in1=mv[:, :, 1],
                                                   op0=ALU.add, op1=ALU.add).then_inc(s["ms"], 1)
                    dve.wait_ge(s["rms"], at(f, 1, 1))
                    v.step(nc.vector.reciprocal(ms[:], ms[:]))
                    v.done()
                    for t in range(QT):
                        ins = nc.vector.scalar_tensor_tensor(out=xr[:, t, :], in0=y[:, t, :], scalar=ms[:, t:t + 1],
                                                             in1=w["ln1"][:], op0=ALU.mult, op1=ALU.mult)
                    ins.then_inc(s["xr"], 1)

                def attention(b, f):
                    v = Steps(dve, s["vec"], STEPS, b)

                    def rotate(dst, src, cos, sin, shape, sem):
                        n, hh, half = shape[1:]
                        a, c = ra[:, 0, 0:hh, :], ra[:, 1, 0:hh, :]
                        d, e = rb[:, 0, 0:hh, :], rb[:, 1, 0:hh, :]
                        x0, x1_ = src[:, :, 0::2], src[:, :, 1::2]
                        cb = cos.unsqueeze(1).to_broadcast([P, hh, half])
                        sb_ = sin.unsqueeze(1).to_broadcast([P, hh, half])
                        v.step(nc.vector.tensor_tensor(a, x0, cb, ALU.mult))
                        v.step(nc.vector.tensor_tensor(d, x1_, sb_, ALU.mult))
                        v.step(nc.vector.tensor_tensor(c, x0, sb_, ALU.mult))
                        v.step(nc.vector.tensor_tensor(e, x1_, cb, ALU.mult))
                        v.done()
                        v.step(nc.vector.tensor_tensor(dst[:, :, 0::2], a, d, ALU.subtract))
                        ins = nc.vector.tensor_tensor(dst[:, :, 1::2], c, e, ALU.add)
                        if sem is None:
                            v.step(ins)
                            v.done()
                        else:
                            return ins

                    dve.wait_ge(s["freed"], at(b, NFREED, 3))
                    for t in range(QT):
                        ins = rotate(krr[:, t, :].unsqueeze(1), krow[:, t, :].unsqueeze(1), w["cos"][:, t, :], w["sin"][:, t, :],
                                     (P, 1, 1, ROPE // 2), None if t < QT - 1 else True)
                    ins.then_inc(s["krot"], 1)
                    dve.wait_ge(s["krot"], at(b, 1, 1))
                    for t in range(QT):
                        dve.wait_ge(s["freed"], at(b, NFREED, 7 + 2 * (t + 1)))
                        rotate(qp[:, t, :, NOPE:DK], qp[:, t, :, NOPE:DK], w["cos"][:, t, :], w["sin"][:, t, :],
                               (P, 1, H, ROPE // 2), True).then_inc(s["qrot"], 1)
                        dve.wait_ge(s["qrot"], at(b, QT, t + 1))

                    for n, (what, a) in enumerate(units):
                        if what == "kt" or (what == "qt" and a % 2):
                            dve.wait_ge(s["proj"], at(b, NUNIT, n + 1))
                            if what == "kt":
                                ins = nc.vector.tensor_copy(kT[DK:P, a, 1, :], psum[DK:P, n % 4, :])
                            else:
                                ins = nc.vector.tensor_copy(qT[:, a, :], psum[:, n % 4, :])
                            ins.then_inc(s["freed_v"], 1)

                    for g in range(NG):
                        for t in range(QT):
                            r = g * QT + t
                            n = (t + 1) * P
                            dve.wait_ge(s["sc"], at(b, NR, r + 1))
                            bk = 2 * (r % 3)
                            nc.vector.tensor_reduce(negmax[:, t, g * G:(g + 1) * G], psum[:, bk:bk + 2, 0:n],
                                                    X_AXIS, ALU.max, negate=True).then_inc(s["mx"], 1)
                        if g % 4 == 3:
                            hs = slice((g - 3) * G, (g + 1) * G)
                            dve.wait_ge(s["mx"], at(b, NR, (g + 1) * QT))
                            v.step(nc.vector.tensor_copy(mparts[:, :, hs, 0], negmax[:, :, hs]))
                            v.done()
                            v.step(nc.vector.tensor_tensor(rest[:, :, hs], negmax[:, :, hs], mparts[:, :, hs, 0], ALU.subtract))
                            v.done()
                            v.step(nc.vector.tensor_copy(mparts[:, :, hs, 1], rest[:, :, hs]))
                            v.done()
                            nc.vector.tensor_tensor(mparts[:, :, hs, 2], rest[:, :, hs], mparts[:, :, hs, 1], ALU.subtract).then_inc(s["mp"], 1)
                    for k in range(NG // 2):
                        dve.wait_ge(s["mt_ps"], at(b, NG // 2, k + 1))
                        nc.vector.tensor_copy(mT[:, 2 * k:2 * k + 2, :].rearrange("p g q -> p (g q)"),
                                              psum[:, 7, :].bitcast(BF16)).then_inc(s["mt"], 1)
                    for c in range(H // HB):
                        for h in range(c * HB, (c + 1) * HB):
                            dve.wait_ge(s["pv"], at(b, H, h + 1))
                            r0 = NOPE * (h % HB)
                            nc.vector.tensor_copy(oT[r0:r0 + NOPE, c, :], psum[0:NOPE, h % PV_BANKS, :]).then_inc(s["o"], 1)
                        dve.wait_ge(s["rs"], at(b, H, (c + 1) * HB))
                        v.step(nc.vector.reciprocal(rsum[:, c % 2, :], rsum[:, c % 2, :]))
                        v.done()
                        dve.wait_ge(s["o"], at(b, H, (c + 1) * HB))
                        nc.vector.tensor_tensor(oT[:, c, :], oT[:, c, :], rsum[:, c % 2, :], ALU.mult).then_inc(s["on"], 1)
                    dve.wait_ge(s["out"], at(b, 1, 1))
                    add_rows(core, v, b, psum[:, 7, :], None, new, base=y[:].rearrange("p t d -> p (t d)"))
                    if f is not None:
                        fv = Steps(dve, s["fvec"], FRONT_STEPS, f)
                        front(f, fv)
                        fv.close()
                    keep_rows(core, v, b, new, parts, mv, dest=x1)
                    v.close()

                fv = Steps(dve, s["fvec"], FRONT_STEPS, 0)
                front(0, fv)
                fv.close()
                with dve.Fori(0, B - 1) as b:
                    attention(b, b + 1)
                attention(B - 1, None)


def store(core, io):
    stored = core.sem("stored")
    with core.nc.Block() as block:

        @block.sync
        def _(sp):
            sp.dma_start(io["out"].rearrange("b (t p) d -> p (b t) d", p=P), core.resid[:]).then_inc(stored, 16)
            sp.wait_ge(stored, 16)


def row(ap):
    return ap.rearrange("(a n) -> a n", a=1)


def build(nc, io):
    with ExitStack() as ctx:
        core = Core(nc, ctx)
        loads, late_loads, layers = [], [], []

        def load(L, w, sem, name, shape, src, dt=F32, dst=None):
            late = L in ("L2a", "L2f", "L3f") and name != "swd"
            if name not in w and late:
                n = int(np.prod(shape[1:]))
                view = core.arena[0:shape[0], core.arena_used:core.arena_used + n]
                core.arena_used += n
                assert core.arena_used <= core.arena.shape[1]
                if len(shape) == 3:
                    view = view.rearrange("p (a b) -> p a b", b=shape[2])
                w[name] = View(view)
            if name not in w:
                w[name] = core.sb(f"{L}_{name}", shape, dt)
            (late_loads if late else loads).append((w[name][:] if dst is None else dst(w[name]), src, sem, len(layers)))

        L, w, sem = "L0x", {}, core.sem("L0x_loaded")
        n0 = len(loads) + len(late_loads)
        for n in ("q", "k", "v", "o"):
            load(L, w, sem, "w" + n, [D, D], io[f"L0_xattn_W{n}"])
        load(L, w, sem, "qn", [P, 8], io["L0_xattn_q_norm_w"].partition_broadcast(P))
        load(L, w, sem, "kn", [P, 8], io["L0_xattn_k_norm_w"].partition_broadcast(P))
        for n in ("qcos", "qsin"):
            load(L, w, sem, n, [P, QT, 4], io[n])
        for n in ("kcos", "ksin"):
            load(L, w, sem, n, [KH, 2, 4], io[n])
        load(L, w, sem, "pad", [KH, 2], io["pad"])
        pad = w["pad"]
        a = (L, w, sem, len(loads) + len(late_loads) - n0)
        layers.append(lambda a=a: narrow_attention(core, a[0], a[1], 0, "rope", a[2], a[3],
                                                   [x for x in loads if 0 < x[3] < LAYERS]))

        L, w, sem = "L0f", {}, core.sem("L0f_loaded")
        n0 = len(loads) + len(late_loads)
        load(L, w, sem, "gate", [P, 8], io["L0_ffn_gate_w"])
        load(L, w, sem, "gate_b", [1, 8], row(io["L0_ffn_gate_b"]))
        load(L, w, sem, "b1", [P, 8, 4], io["L0_ffn_b1"])
        load(L, w, sem, "b2", [8, D], io["L0_ffn_b2"])
        core.arena = core.sb("expert_arena", [P, 2 * 8 * 512])
        core.arena_used = 0
        w["w1"] = View(core.arena[:, 0:4096].rearrange("p (e f) -> p e f", e=8))
        w["w2"] = View(core.arena[:, 4096:8192].rearrange("p (e c d) -> p e c d", e=8, c=4))
        for e in range(8):
            load(L, w, sem, "w1", [P, 8, 512], io["L0_ffn_w1"][e], dst=lambda x, e=e: x[:, e, :])
            load(L, w, sem, "w2", [P, 8, 4, D], io["L0_ffn_w2"][e].rearrange("(c p) d -> p c d", p=P), dst=lambda x, e=e: x[:, e, :, :])
        items = [([(w["w1"][:, e, c * P:(c + 1) * P], None, P, w["b1"][:, e, c:c + 1]) for c in range(4)],
                  [(e, [(c, slice(0, P), w["w2"][:, e, c, :]) for c in range(4)])]) for e in range(8)]
        a = (L, w, sem, len(loads) + len(late_loads) - n0, items)
        layers.append(lambda a=a: experts(core, a[0], a[1], 4, 8, a[4], a[2], a[3], glu=False,
                                          capacity=int(1.25 * B * SEQ / 8), biased=True))

        L, w, sem = "L1x", {}, core.sem("L1x_loaded")
        n0 = len(loads) + len(late_loads)
        core.projections = core.sb("projections", [P, 4, H * 64])
        for k, n in enumerate(("q", "k", "v")):
            w["w" + n] = View(core.projections[:, k, :])
            load(L, w, sem, "w" + n, [D, H * 64], io[f"L1_xattn_W{n}"])
        w["wo"] = View(core.projections[:, 3, :].rearrange("p (c d) -> p c d", d=D))
        load(L, w, sem, "wo", [P, 8, D], io["L1_xattn_Wo"].rearrange("(c p) d -> p c d", p=P))
        w["wo"] = w["wo"][:].rearrange("p c d -> p (c d)")
        for n in ("q", "k"):
            load(L, w, sem, "b" + n, [P, 8], io[f"L1_xattn_b{n}"])
        load(L, w, sem, "bv", [KC, H * 64], io["L1_xattn_bv"].partition_broadcast(KC))
        load(L, w, sem, "bo", [1, D], row(io["L1_xattn_bo"]))
        load(L, w, sem, "gamma", [P, D], io["L1_xattn_ln_gamma"].partition_broadcast(P))
        load(L, w, sem, "beta", [P, D], io["L1_xattn_ln_beta"].partition_broadcast(P))
        a = (L, w, sem, len(loads) + len(late_loads) - n0)
        layers.append(lambda a=a: wide_attention(core, a[0], a[1], 1, a[2], a[3],
                                                 [x for x in late_loads if x[3] < LAYERS]))

        L, w, sem = "L1f", {}, core.sem("L1f_loaded")
        n0 = len(loads) + len(late_loads)
        load(L, w, sem, "gate", [P, 8], io["L1_ffn_gate_w"])
        for e in range(8):
            load(L, w, sem, "gu", [P, 8, 512], io["L1_ffn_gate_up_w"][e], dst=lambda x, e=e: x[:, e, :])
            load(L, w, sem, "dn", [P, 8, 2, D], io["L1_ffn_down_w"][e].rearrange("(c p) d -> p c d", p=P), dst=lambda x, e=e: x[:, e, :, :])
        core.spare = w["gu"], w["dn"]
        items = [([(w["gu"][:, e, c * P:(c + 1) * P], w["gu"][:, e, 256 + c * P:256 + (c + 1) * P], P, None) for c in range(2)],
                  [(e, [(c, slice(0, P), w["dn"][:, e, c, :]) for c in range(2)])]) for e in range(8)]
        a = (L, w, sem, len(loads) + len(late_loads) - n0, items)
        layers.append(lambda a=a: experts(core, a[0], a[1], 5, 8, a[4], a[2], a[3], glu=True))

        L, w, sem = "L2x", {}, core.sem("L2x_loaded")
        n0 = len(loads) + len(late_loads)
        for n in ("q", "k", "v", "o"):
            load(L, w, sem, "w" + n, [D, D], io[f"L2_xattn_W{n}"])
        for n in ("q", "k"):
            load(L, w, sem, "b" + n, [P, D], io[f"L2_xattn_b{n}"].partition_broadcast(P))
        load(L, w, sem, "bv", [1, D], row(io["L2_xattn_bv"]))
        load(L, w, sem, "bo", [1, D], row(io["L2_xattn_bo"]))
        load(L, w, sem, "mask", [KH, 2, B], io["mask"][0:KH, :], dt=U8, dst=lambda x: x[:, 0, :])
        load(L, w, sem, "mask", [KH, 2, B], io["mask"][KH:CTX, :], dst=lambda x: x[0:CTX - KH, 1, :])
        core.padded.append(w["mask"])
        w["pad"] = pad
        a = (L, w, sem, len(loads) + len(late_loads) - n0)
        layers.append(lambda a=a: narrow_attention(core, a[0], a[1], 2, "mask", a[2], a[3]))

        x1 = core.sb("x1", [P, NT, D])
        L, w, sem = "L2a", {}, core.sem("L2a_loaded")
        n0 = len(loads) + len(late_loads)
        load(L, w, sem, "wq", [P, H * 64], io["L2_ffn_Wq"])
        load(L, w, sem, "wkva", [P, 48], io["L2_ffn_Wkva"])
        load(L, w, sem, "wkvb", [16, 512], io["L2_ffn_Wkvb"])
        load(L, w, sem, "wo", [P, 4, D], io["L2_ffn_Wo"])
        load(L, w, sem, "ln1", [P, D], io["L2_ffn_w_ln1"].partition_broadcast(P))
        load(L, w, sem, "cos", [P, QT, 16], io["scos"])
        load(L, w, sem, "sin", [P, QT, 16], io["ssin"])
        a = (L, w, sem, len(loads) + len(late_loads) - n0)
        L, w, sem = "L2f", {}, core.sem("L2f_loaded")
        n0 = len(loads) + len(late_loads)
        load(L, w, sem, "gate", [P, 8], io["L2_ffn_Wgate"])
        load(L, w, sem, "gate_b", [1, 8], row(io["L2_ffn_expert_bias"]))
        load(L, w, sem, "ln2", [P, D], io["L2_ffn_w_ln2"].partition_broadcast(P))
        load(L, w, sem, "wg", [P, 9, 64], io["L2_ffn_Wg"].rearrange("e c i -> c e i"), dst=lambda x: x[:, 0:8, :])
        load(L, w, sem, "wg", [P, 9, 64], io["L2_ffn_sWg"].rearrange("e c i -> c e i"), dst=lambda x: x[:, 8:9, :])
        load(L, w, sem, "wu", [P, 9, 64], io["L2_ffn_Wu"].rearrange("e c i -> c e i"), dst=lambda x: x[:, 0:8, :])
        load(L, w, sem, "wu", [P, 9, 64], io["L2_ffn_sWu"].rearrange("e c i -> c e i"), dst=lambda x: x[:, 8:9, :])
        load(L, w, sem, "wd", [P, 5, D], io["L2_ffn_Wd"].rearrange("(a e) i d -> (e i) a d", e=2), dst=lambda x: x[:, 0:4, :])
        load(L, w, sem, "wd", [P, 5, D], io["L2_ffn_sWd"][0], dst=lambda x: x[0:64, 4, :])
        lo, hi = slice(0, 64), slice(64, 128)

        def pair(wg, wu, wd, i):
            return ([(wg[:, 2 * i:2 * i + 2, :].rearrange("p e i -> p (e i)"), wu[:, 2 * i:2 * i + 2, :].rearrange("p e i -> p (e i)"), P, None)],
                    [(2 * i, [(0, lo, wd[lo, i, :])]), (2 * i + 1, [(0, hi, wd[hi, i, :])])])

        items = [pair(w["wg"], w["wu"], w["wd"], i) for i in range(4)]
        items.append(([(w["wg"][:, 8, :], w["wu"][:, 8, :], 64, None)], [(8, [(0, lo, w["wd"][lo, 4, :])])]))
        a2 = (L, w, sem, len(loads) + len(late_loads) - n0, items)

        def level2(a=a, a2=a2):
            with nc.cleanup_on_exit():
                causal_attention(core, a[0], a[1], x1, a[2], a[3])
            experts(core, a2[0], a2[1], 6, 8, a2[4], a2[2], a2[3], glu=True, extra="one", x1=x1)

        layers.append(level2)

        L, w, sem = "L3x", {}, core.sem("L3x_loaded")
        n0 = len(loads) + len(late_loads)
        for n in ("q", "k", "v"):
            load(L, w, sem, "w" + n, [P, 8], io[f"L3_xattn_w{n}"])
        load(L, w, sem, "wo", [D, D], io["L3_xattn_wo"])
        for n in ("q", "k"):
            load(L, w, sem, "b" + n, [P, D], io[f"L3_xattn_b{n}"].partition_broadcast(P))
        load(L, w, sem, "bv", [1, D], row(io["L3_xattn_bv"]))
        load(L, w, sem, "bo", [1, D], row(io["L3_xattn_bo"]))
        w["pad"] = pad
        a = (L, w, sem, len(loads) + len(late_loads) - n0)
        layers.append(lambda a=a: narrow_attention(core, a[0], a[1], 3, "plain", a[2], a[3]))

        L, w, sem = "L3f", {}, core.sem("L3f_loaded")
        n0 = len(loads) + len(late_loads)
        load(L, w, sem, "gate", [P, 17], io["L3_ffn_gate_w"], dst=lambda x: x[:, 0:16])
        load(L, w, sem, "gate", [P, 17], io["L3_ffn_shared_gate_w"], dst=lambda x: x[:, 16:17])
        gu = io["L3_ffn_w_gate_up"].rearrange("e c i -> c e i")
        load(L, w, sem, "wg", [P, 16, 64], gu[:, :, 0:64])
        load(L, w, sem, "wu", [P, 16, 64], gu[:, :, 64:128])
        load(L, w, sem, "wd", [P, 8, D], io["L3_ffn_w_down"].rearrange("(a e) i d -> (e i) a d", e=2))
        load(L, w, sem, "swg", [P, 352], io["L3_ffn_shared_w_gate"])
        load(L, w, sem, "swu", [P, 352], io["L3_ffn_shared_w_up"])
        swd = io["L3_ffn_shared_w_down"]
        load(L, w, sem, "swd", [P, 3, D], swd[0:256, :].rearrange("(c p) d -> p c d", p=P), dst=lambda x: x[:, 0:2, :])
        load(L, w, sem, "swd", [P, 3, D], swd[256:352, :], dst=lambda x: x[0:96, 2, :])
        items = [pair(w["wg"], w["wu"], w["wd"], i) for i in range(8)]
        widths = [P, P, 96]
        items.append(([(w["swg"][:, k * P:k * P + m], w["swu"][:, k * P:k * P + m], m, None) for k, m in enumerate(widths)],
                      [(16, [(k, slice(0, m), w["swd"][0:m, k, :]) for k, m in enumerate(widths)])]))
        a = (L, w, sem, len(loads) + len(late_loads) - n0, items)
        layers.append(lambda a=a: experts(core, a[0], a[1], 7, 16, a[4], a[2], a[3], glu=True, extra="sigmoid"))

        setup(core, io, [x for x in loads if x[3] == 0])
        for layer in layers[:LAYERS]:
            with nc.cleanup_on_exit():
                layer()
        store(core, io)



def kernel(**inputs):
    import concourse.bacc as _bacc
    from concourse.bass_utils import run_bass_kernel_spmd as _run

    c = {k: np.asarray(v) for k, v in inputs.items()}
    t = np.ascontiguousarray
    arrays = {
        "x": c["x"], "ctx": c["ctx_1024"], "g_xattn": c["g_xattn"], "g_ffn": c["g_ffn"],
    }
    for n in "qkvo":
        arrays[f"L0_xattn_W{n}"] = t(c[f"L0_xattn_W{n}"].T)
    arrays["L0_xattn_q_norm_w"] = c["L0_xattn_q_norm_w"]
    arrays["L0_xattn_k_norm_w"] = c["L0_xattn_k_norm_w"]

    for n in ("gate_w", "gate_b", "w1", "w2", "b2"):
        arrays[f"L0_ffn_{n}"] = c[f"L0_ffn_{n}"]
    arrays["L0_ffn_b1"] = c["L0_ffn_b1"].reshape(8, 4, P).transpose(2, 0, 1)
    for n in ("Wq", "Wk", "Wv", "Wo", "bv", "bo", "ln_gamma", "ln_beta"):
        arrays[f"L1_xattn_{n}"] = c[f"L1_xattn_{n}"]
    for n in ("bq", "bk"):
        arrays[f"L1_xattn_{n}"] = c[f"L1_xattn_{n}"].reshape(8, P).T
    for n in ("gate_w", "gate_up_w", "down_w"):
        arrays[f"L1_ffn_{n}"] = c[f"L1_ffn_{n}"]

    for n in "qkvo":
        arrays[f"L2_xattn_W{n}"] = c[f"L2_xattn_W{n}"].T
    for n in ("bq", "bk", "bv", "bo"):
        arrays[f"L2_xattn_{n}"] = c[f"L2_xattn_{n}"]
    arrays["mask"] = c["mask_BxS2_bf1"].reshape(B, CTX).T.view(np.uint8)
    pad = np.zeros((2, KH), np.float32)
    pad[1, CTX - KH:] = PAD_PENALTY
    arrays["pad"] = pad.T
    for n in ("Wq", "Wkva", "Wkvb", "w_ln1", "w_ln2", "Wgate", "expert_bias", "Wg", "Wu", "Wd", "sWg", "sWu", "sWd"):
        arrays[f"L2_ffn_{n}"] = c[f"L2_ffn_{n}"]
    arrays["L2_ffn_Wo"] = c["L2_ffn_Wo"].reshape(4, 4, 64, D)[:, :, 0:32].transpose(1, 2, 0, 3).reshape(P, 4, D)
    for n in "qkv":
        a = c[f"L3_xattn_w{n}"].T
        arrays[f"L3_xattn_w{n}"] = np.broadcast_to(a[None], (H, 8, 8)).reshape(P, 8)
    arrays["L3_xattn_wo"] = c["L3_xattn_wo"].T
    for n in ("bq", "bk", "bv"):
        arrays[f"L3_xattn_{n}"] = np.broadcast_to(c[f"L3_xattn_{n}"][None], (H, 8)).reshape(-1)
    arrays["L3_xattn_bo"] = c["L3_xattn_bo"]
    for n in ("gate_w", "shared_w_gate", "shared_w_up", "shared_w_down", "shared_gate_w"):
        arrays[f"L3_ffn_{n}"] = c[f"L3_ffn_{n}"].T
    for n in ("w_gate_up", "w_down"):
        arrays[f"L3_ffn_{n}"] = c[f"L3_ffn_{n}"]

    def table(n, theta, dim, rows):
        f = np.float32(theta) ** (-np.arange(0, dim, 2, dtype=np.float32) / np.float32(dim))
        ang = np.arange(n, dtype=np.float32)[:, None] * f[None, :].astype(np.float32)
        ang = ang.reshape(n // rows, rows, dim // 2).transpose(1, 0, 2)
        return t(np.cos(ang).astype(np.float32)), t(np.sin(ang).astype(np.float32))

    arrays["qcos"], arrays["qsin"] = table(SEQ, 32.0, 8, P)
    arrays["kcos"], arrays["ksin"] = table(KP, 1000.0, 8, KH)
    arrays["scos"], arrays["ssin"] = table(SEQ, 100000.0, 32, P)

    nc = _bacc.Bacc("TRN2", target_bir_lowering=False, num_devices=1)
    feed, io = {}, {}
    for name, a in arrays.items():
        a = t(a)
        feed[f"in_{name}"] = a
        io[name] = nc.dram_tensor(f"in_{name}", a.shape, mybir.dt.from_np(a.dtype), kind="ExternalInput").ap()
    io["out"] = nc.dram_tensor("out_x", (B, SEQ, D), F32, kind="ExternalOutput").ap()
    build(nc, io)
    r = _run(nc, [feed], core_ids=[0])
    return r.results[0]["out_x"]
```
